# Optimizing a Trainium2 kernel written in Bass

```python
import numpy as np
import jax
import jax.numpy as jnp

def _softmax(x, axis=-1):
    return jax.nn.softmax(x, axis=axis)

def _gelu(x):
    return jax.nn.gelu(x, approximate=True)

def _silu(x):
    return jax.nn.silu(x)

def _sigmoid(x):
    return jax.nn.sigmoid(x)

def _layernorm(x, axis=-1, eps=1e-05):
    m = jnp.mean(x, axis=axis, keepdims=True)
    v = jnp.var(x, axis=axis, keepdims=True)
    return (x - m) / jnp.sqrt(v + eps)

def _scatter_add(tgt, idx, src, axis=0):
    return tgt.at[idx].add(src)

def _segment_sum(src, seg, n):
    return jax.ops.segment_sum(src, seg, n)
kernel_name = 'mk_decoder_postln_d2_seqx_r8_5b4f8f'

def setup_inputs(seed: int=0):
    np.random.seed(seed)
    _w = jnp.asarray

    def _rec_inputs():
        import jax
        import jax.numpy as jnp
        _rk = jax.random.key(seed)
        x = -0.000125 + 0.9999 * jax.random.normal(jax.random.fold_in(_rk, 1), (2, 256, 512), jnp.float32)
        _lenS = 256 - jax.random.randint(jax.random.fold_in(_rk, 7), (2,), 0, max(1, 256 // 4) + 1, jnp.int32)
        _lenS2 = 512 - jax.random.randint(jax.random.fold_in(_rk, 8), (2,), 0, max(1, 512 // 4) + 1, jnp.int32)
        _ctx_4096P = jax.random.normal(jax.random.fold_in(_rk, 11), (2, 16, 512), jnp.float32)
        _ctx_4096c = jax.random.dirichlet(jax.random.fold_in(_rk, 511), 0.3 * jnp.ones((16,), jnp.float32), (2, 512))
        _ctx_4096t = jnp.einsum('bsk,bkd->bsd', _ctx_4096c, _ctx_4096P)
        _ctx_4096t = _ctx_4096t * jax.lax.rsqrt(jnp.mean(jnp.square(_ctx_4096t)) + 1e-12) * 0.953939
        ctx_4096 = -5.72187e-05 + 0.999849 * (_ctx_4096t + 0.3 * jax.random.normal(jax.random.fold_in(_rk, 611), (2, 512, 512), jnp.float32))
        _validS = jnp.arange(256)[None, :] < _lenS[:, None]
        _validS2 = jnp.arange(512)[None, :] < _lenS2[:, None]
        _causal = jnp.tril(jnp.ones((256, 256), dtype=bool))
        mask_1x1xSxS2_ff0 = jnp.where(jnp.ones((1, 1, 256, 512), dtype=bool), 0.0, -1000000000.0).astype(jnp.float32)
        return (x, ctx_4096, mask_1x1xSxS2_ff0)
    x, ctx_4096, mask_1x1xSxS2_ff0 = _rec_inputs()

    def _L0_attn_setup():
        import jax, jax.numpy as jnp
        import numpy as np
        BLOCK_H = 32
        BLOCK_W = 32
        N_FEAT = 512
        K_FEAT = 512
        key = jax.random.key(seed)
        k1, k2, k3 = jax.random.split(key, 3)
        data = jax.random.normal(k1, (4, 128, K_FEAT), dtype=jnp.float32)
        weight = jax.random.normal(k2, (N_FEAT, K_FEAT), dtype=jnp.float32) * 0.02
        nb, kb = (N_FEAT // BLOCK_H, K_FEAT // BLOCK_W)
        block_pattern = jax.random.randint(k3, (nb, kb), 0, 2, dtype=jnp.int32)
        mask = jnp.repeat(jnp.repeat(block_pattern, BLOCK_H, axis=0), BLOCK_W, axis=1)
        return {'data': data, 'weight': weight, 'mask': mask}
    _L0_attn_all = _L0_attn_setup()
    _L0_attn_in = {k: v for k, v in _L0_attn_all.items() if k in ('weight', 'mask')}
    del _L0_attn_all

    def _L0_xattn_setup():
        import jax, jax.numpy as jnp
        import numpy as np
        QMIN = 0.0
        QMAX = 255.0

        def fake_quant(x, scale, zp):
            s = scale.reshape(())
            z = zp.reshape(())
            q = jnp.clip(jnp.round(x / s + z), QMIN, QMAX)
            return (q - z) * s
        key = jax.random.key(seed)
        k1, k2 = jax.random.split(key)
        B, M, K, N = (4, 256, 512, 512)
        x1 = jax.random.normal(k1, (B, M, K), dtype=jnp.float32)
        x2 = jax.random.normal(k2, (B, K, N), dtype=jnp.float32)
        x1_scale = jnp.full((1,), 8.0 / 255.0, dtype=jnp.float32)
        x1_zp = jnp.full((1,), 128.0, dtype=jnp.float32)
        x2_scale = jnp.full((1,), 8.0 / 255.0, dtype=jnp.float32)
        x2_zp = jnp.full((1,), 128.0, dtype=jnp.float32)
        return {'x1': x1, 'x2': x2, 'x1_scale': x1_scale, 'x1_zp': x1_zp, 'x2_scale': x2_scale, 'x2_zp': x2_zp}
    _L0_xattn_all = _L0_xattn_setup()
    _L0_xattn_in = {k: v for k, v in _L0_xattn_all.items() if k in ('x1_scale', 'x1_zp', 'x2_scale', 'x2_zp')}
    del _L0_xattn_all

    def _L0_ffn_setup():
        import jax, jax.numpy as jnp
        import numpy as np
        IN_F = 512
        OUT_F = 512
        N_CLUSTERS = 64
        THRESHOLD = 0.01
        TEMPERATURE = 0.1
        BATCH, SEQ = (4, 256)
        key = jax.random.key(seed)
        k1, k2, k3, k4, k5 = jax.random.split(key, 5)
        s = 1.0 / np.sqrt(IN_F)
        return {'input': jax.random.normal(k1, (BATCH, SEQ, IN_F), dtype=jnp.float32), 'weight': jax.random.normal(k2, (OUT_F, IN_F), dtype=jnp.float32) * s, 'bias': jax.random.uniform(k3, (OUT_F,), dtype=jnp.float32, minval=-s, maxval=s), 'centroids': jax.random.normal(k4, (N_CLUSTERS, IN_F), dtype=jnp.float32) * s, 'assignments': jax.random.randint(k5, (OUT_F,), 0, N_CLUSTERS, dtype=jnp.int32)}
    _L0_ffn_all = _L0_ffn_setup()
    _L0_ffn_in = {k: v for k, v in _L0_ffn_all.items() if k in ('weight', 'bias', 'centroids', 'assignments')}
    del _L0_ffn_all

    def _L1_attn_setup():
        import jax, jax.numpy as jnp
        import numpy as np
        import math
        HIDDEN = 512
        NUM_HEADS = 32
        HEAD_DIM = HIDDEN // NUM_HEADS
        SCALE = 1.0 / HEAD_DIM

        def _alibi_slopes(n_heads: int) -> np.ndarray:
            cp2 = 2 ** math.floor(math.log2(n_heads))
            base = 2 ** (-2 ** (-(math.log2(cp2) - 3)))
            slopes = base ** np.arange(1, cp2 + 1, dtype=np.float32)
            if cp2 != n_heads:
                extra_base = 2 ** (-2 ** (-(math.log2(2 * cp2) - 3)))
                n_rem = min(cp2, n_heads - cp2)
                extra = extra_base ** np.arange(1, 1 + 2 * n_rem, 2, dtype=np.float32)
                slopes = np.concatenate([slopes, extra])
            return slopes.astype(np.float32)
        key = jax.random.key(seed)
        k1, k2, k3, k4, k5 = jax.random.split(key, 5)
        B, S = (2, 256)
        return {'hidden_states': jax.random.normal(k1, (B, S, HIDDEN), dtype=jnp.float32), 'w_attn': jax.random.normal(k2, (HIDDEN, 3 * HIDDEN), dtype=jnp.float32) * 0.02, 'b_attn': jnp.zeros((3 * HIDDEN,), dtype=jnp.float32), 'w_proj': jax.random.normal(k3, (HIDDEN, HIDDEN), dtype=jnp.float32) * 0.02, 'b_proj': jnp.zeros((HIDDEN,), dtype=jnp.float32)}
    _L1_attn_all = _L1_attn_setup()
    _L1_attn_in = {k: v for k, v in _L1_attn_all.items() if k in ('w_attn', 'b_attn', 'w_proj', 'b_proj')}
    del _L1_attn_all

    def _L1_xattn_setup():
        import jax, jax.numpy as jnp
        import numpy as np
        NUM_HEADS = 32
        NUM_KV_HEADS = 8
        HEAD_DIM = 128
        HIDDEN = 512
        EPS = 1e-05

        def rmsnorm(x, w, eps=EPS):
            xf = x.astype(jnp.float32)
            var = jnp.mean(xf * xf, axis=-1, keepdims=True)
            return w * (xf * jax.lax.rsqrt(var + eps)).astype(x.dtype)
        key = jax.random.key(seed)
        ks = jax.random.split(key, 10)
        B, Q, KV = (1, 128, 6404)
        s = 1.0 / np.sqrt(HIDDEN)
        return {'hidden_states': jax.random.normal(ks[0], (B, Q, HIDDEN), jnp.float32), 'cross_attention_states': jax.random.normal(ks[1], (B, KV, HIDDEN), jnp.float32), 'attention_mask': jnp.zeros((B, 1, Q, KV), jnp.float32), 'q_proj_w': jax.random.normal(ks[2], (NUM_HEADS * HEAD_DIM, HIDDEN), jnp.float32) * s, 'k_proj_w': jax.random.normal(ks[3], (NUM_KV_HEADS * HEAD_DIM, HIDDEN), jnp.float32) * s, 'v_proj_w': jax.random.normal(ks[4], (NUM_KV_HEADS * HEAD_DIM, HIDDEN), jnp.float32) * s, 'o_proj_w': jax.random.normal(ks[5], (HIDDEN, NUM_HEADS * HEAD_DIM), jnp.float32) * s, 'q_norm_w': jnp.ones((HEAD_DIM,), jnp.float32), 'k_norm_w': jnp.ones((HEAD_DIM,), jnp.float32)}
    _L1_xattn_all = _L1_xattn_setup()
    _L1_xattn_in = {k: v for k, v in _L1_xattn_all.items() if k in ('q_proj_w', 'k_proj_w', 'v_proj_w', 'o_proj_w', 'q_norm_w', 'k_norm_w')}
    del _L1_xattn_all

    def _L1_ffn_setup():
        import jax, jax.numpy as jnp
        import numpy as np

        def sparsemax(z):
            E = z.shape[-1]
            z_sorted = -jnp.sort(-z, axis=-1)
            z_cum = jnp.cumsum(z_sorted, axis=-1)
            k = jnp.arange(1, E + 1, dtype=z.dtype)
            support = 1.0 + k * z_sorted > z_cum
            k_z = jnp.sum(support, axis=-1, keepdims=True)
            tau_sum = jnp.take_along_axis(z_cum, k_z.astype(jnp.int32) - 1, axis=-1)
            tau = (tau_sum - 1.0) / k_z.astype(z.dtype)
            return jnp.maximum(z - tau, 0.0)
        key = jax.random.key(seed)
        ks = jax.random.split(key, 6)
        B, S, D_IN, D_OUT, E, R = (8, 256, 512, 512, 8, 16)
        x = jax.random.normal(ks[0], (B, S, D_IN), dtype=jnp.float32)
        W_base = jax.random.normal(ks[1], (D_OUT, D_IN), dtype=jnp.float32) * D_IN ** (-0.5)
        b_base = jax.random.normal(ks[2], (D_OUT,), dtype=jnp.float32) * 0.01
        W_router = jax.random.normal(ks[3], (E, D_IN), dtype=jnp.float32) * D_IN ** (-0.5)
        b_router = jnp.zeros((E,), dtype=jnp.float32)
        lora_A = jax.random.normal(ks[4], (E, D_IN, R), dtype=jnp.float32) * D_IN ** (-0.5)
        lora_B = jnp.zeros((E, R, D_OUT), dtype=jnp.float32)
        return {'x': x, 'W_base': W_base, 'b_base': b_base, 'W_router': W_router, 'b_router': b_router, 'lora_A': lora_A, 'lora_B': lora_B}
    _L1_ffn_all = _L1_ffn_setup()
    _L1_ffn_in = {k: v for k, v in _L1_ffn_all.items() if k in ('W_base', 'b_base', 'W_router', 'b_router', 'lora_A', 'lora_B')}
    del _L1_ffn_all
    return {'x': x, 'ctx_4096': ctx_4096, 'mask_1x1xSxS2_ff0': mask_1x1xSxS2_ff0, 'L0_attn_weight': _L0_attn_in['weight'], 'L0_attn_mask': _L0_attn_in['mask'], 'L0_xattn_x1_scale': _L0_xattn_in['x1_scale'], 'L0_xattn_x1_zp': _L0_xattn_in['x1_zp'], 'L0_xattn_x2_scale': _L0_xattn_in['x2_scale'], 'L0_xattn_x2_zp': _L0_xattn_in['x2_zp'], 'L0_ffn_weight': _L0_ffn_in['weight'], 'L0_ffn_bias': _L0_ffn_in['bias'], 'L0_ffn_centroids': _L0_ffn_in['centroids'], 'L0_ffn_assignments': _L0_ffn_in['assignments'], 'L1_attn_w_attn': _L1_attn_in['w_attn'], 'L1_attn_b_attn': _L1_attn_in['b_attn'], 'L1_attn_w_proj': _L1_attn_in['w_proj'], 'L1_attn_b_proj': _L1_attn_in['b_proj'], 'L1_xattn_q_proj_w': _L1_xattn_in['q_proj_w'], 'L1_xattn_k_proj_w': _L1_xattn_in['k_proj_w'], 'L1_xattn_v_proj_w': _L1_xattn_in['v_proj_w'], 'L1_xattn_o_proj_w': _L1_xattn_in['o_proj_w'], 'L1_xattn_q_norm_w': _L1_xattn_in['q_norm_w'], 'L1_xattn_k_norm_w': _L1_xattn_in['k_norm_w'], 'L1_ffn_W_base': _L1_ffn_in['W_base'], 'L1_ffn_b_base': _L1_ffn_in['b_base'], 'L1_ffn_W_router': _L1_ffn_in['W_router'], 'L1_ffn_b_router': _L1_ffn_in['b_router'], 'L1_ffn_lora_A': _L1_ffn_in['lora_A'], 'L1_ffn_lora_B': _L1_ffn_in['lora_B']}

def reference(x, ctx_4096, mask_1x1xSxS2_ff0, L0_attn_weight, L0_attn_mask, L0_xattn_x1_scale, L0_xattn_x1_zp, L0_xattn_x2_scale, L0_xattn_x2_zp, L0_ffn_weight, L0_ffn_bias, L0_ffn_centroids, L0_ffn_assignments, L1_attn_w_attn, L1_attn_b_attn, L1_attn_w_proj, L1_attn_b_proj, L1_xattn_q_proj_w, L1_xattn_k_proj_w, L1_xattn_v_proj_w, L1_xattn_o_proj_w, L1_xattn_q_norm_w, L1_xattn_k_norm_w, L1_ffn_W_base, L1_ffn_b_base, L1_ffn_W_router, L1_ffn_b_router, L1_ffn_lora_A, L1_ffn_lora_B):
    import jax
    import jax.numpy as jnp

    def _L0_attn_ref(data, weight, mask):
        import jax, jax.numpy as jnp
        import numpy as np
        BLOCK_H = 32
        BLOCK_W = 32
        N_FEAT = 512
        K_FEAT = 512
        N, K = weight.shape
        nb, kb = (N // BLOCK_H, K // BLOCK_W)
        block_mask = mask.reshape(nb, BLOCK_H, kb, BLOCK_W).astype(jnp.float32).sum(axis=(1, 3)) > 0
        elem_mask = jnp.repeat(jnp.repeat(block_mask, BLOCK_H, axis=0), BLOCK_W, axis=1)
        w_masked = weight * elem_mask.astype(weight.dtype)
        out = jnp.einsum('bsk,nk->bsn', data, w_masked)
        return out

    def _L0_xattn_ref(x1, x2, x1_scale, x1_zp, x2_scale, x2_zp):
        import jax, jax.numpy as jnp
        import numpy as np
        QMIN = 0.0
        QMAX = 255.0

        def fake_quant(x, scale, zp):
            s = scale.reshape(())
            z = zp.reshape(())
            q = jnp.clip(jnp.round(x / s + z), QMIN, QMAX)
            return (q - z) * s
        q1 = fake_quant(x1, x1_scale, x1_zp)
        q2 = fake_quant(x2, x2_scale, x2_zp)
        return jnp.matmul(q1, q2)

    def _L0_ffn_ref(input, weight, bias, centroids, assignments):
        import jax, jax.numpy as jnp
        import numpy as np
        IN_F = 512
        OUT_F = 512
        N_CLUSTERS = 64
        THRESHOLD = 0.01
        TEMPERATURE = 0.1
        BATCH, SEQ = (4, 256)
        shape = input.shape
        x = input.reshape(-1, shape[-1])
        dots = jax.nn.softmax(x @ centroids.T / TEMPERATURE, axis=-1)
        hits = dots > THRESHOLD
        query_sel = jnp.any(hits, axis=1)
        cluster_sel = jnp.any(hits, axis=0)
        row_sel = cluster_sel[assignments]
        dense = x @ weight.T + bias
        out = jnp.where(query_sel[:, None] & row_sel[None, :], dense, jnp.zeros((), dense.dtype))
        return out.reshape(*shape[:-1], -1)

    def _L1_attn_ref(hidden_states, w_attn, b_attn, w_proj, b_proj):
        import jax, jax.numpy as jnp
        import numpy as np
        import math
        HIDDEN = 512
        NUM_HEADS = 32
        HEAD_DIM = HIDDEN // NUM_HEADS
        SCALE = 1.0 / HEAD_DIM

        def _alibi_slopes(n_heads: int) -> np.ndarray:
            cp2 = 2 ** math.floor(math.log2(n_heads))
            base = 2 ** (-2 ** (-(math.log2(cp2) - 3)))
            slopes = base ** np.arange(1, cp2 + 1, dtype=np.float32)
            if cp2 != n_heads:
                extra_base = 2 ** (-2 ** (-(math.log2(2 * cp2) - 3)))
                n_rem = min(cp2, n_heads - cp2)
                extra = extra_base ** np.arange(1, 1 + 2 * n_rem, 2, dtype=np.float32)
                slopes = np.concatenate([slopes, extra])
            return slopes.astype(np.float32)
        B, S, _ = hidden_states.shape
        H, D = (NUM_HEADS, HEAD_DIM)
        qkv = hidden_states @ w_attn + b_attn
        q, k, v = jnp.split(qkv, 3, axis=-1)
        q = q.reshape(B, S, H, D)
        k = k.reshape(B, S, H, D)
        v = v.reshape(B, S, H, D)
        scores = jnp.einsum('bqhd,bkhd->bhqk', q, k) * SCALE
        slopes = jnp.asarray(_alibi_slopes(H))
        pos = jnp.arange(S)
        rel = pos[None, :] - pos[:, None]
        bias = slopes[:, None, None] * rel[None, :, :]
        causal = rel <= 0
        scores = jnp.where(causal[None, None], scores + bias[None], -jnp.inf)
        attn = jax.nn.softmax(scores, axis=-1)
        out = jnp.einsum('bhqk,bkhd->bqhd', attn, v).reshape(B, S, HIDDEN)
        return out @ w_proj + b_proj

    def _L1_xattn_ref(hidden_states, cross_attention_states, attention_mask, q_proj_w, k_proj_w, v_proj_w, o_proj_w, q_norm_w, k_norm_w):
        import jax, jax.numpy as jnp
        import numpy as np
        NUM_HEADS = 32
        NUM_KV_HEADS = 8
        HEAD_DIM = 128
        HIDDEN = 512
        EPS = 1e-05

        def rmsnorm(x, w, eps=EPS):
            xf = x.astype(jnp.float32)
            var = jnp.mean(xf * xf, axis=-1, keepdims=True)
            return w * (xf * jax.lax.rsqrt(var + eps)).astype(x.dtype)
        B, Q, _ = hidden_states.shape
        KV = cross_attention_states.shape[1]
        n_rep = NUM_HEADS // NUM_KV_HEADS
        q = (hidden_states @ q_proj_w.T).reshape(B, Q, NUM_HEADS, HEAD_DIM).transpose(0, 2, 1, 3)
        k = (cross_attention_states @ k_proj_w.T).reshape(B, KV, NUM_KV_HEADS, HEAD_DIM).transpose(0, 2, 1, 3)
        v = (cross_attention_states @ v_proj_w.T).reshape(B, KV, NUM_KV_HEADS, HEAD_DIM).transpose(0, 2, 1, 3)
        q = rmsnorm(q, q_norm_w)
        k = jnp.repeat(k, n_rep, axis=1)
        v = jnp.repeat(v, n_rep, axis=1)
        k = rmsnorm(k, k_norm_w)
        scale = 1.0 / np.sqrt(HEAD_DIM)
        scores = jnp.einsum('bhqd,bhkd->bhqk', q, k) * scale + attention_mask
        attn = jax.nn.softmax(scores.astype(jnp.float32), axis=-1).astype(q.dtype)
        out = jnp.einsum('bhqk,bhkd->bhqd', attn, v)
        out = out.transpose(0, 2, 1, 3).reshape(B, Q, NUM_HEADS * HEAD_DIM)
        return out @ o_proj_w.T

    def _L1_ffn_ref(x, W_base, b_base, W_router, b_router, lora_A, lora_B):
        import jax, jax.numpy as jnp
        import numpy as np

        def sparsemax(z):
            E = z.shape[-1]
            z_sorted = -jnp.sort(-z, axis=-1)
            z_cum = jnp.cumsum(z_sorted, axis=-1)
            k = jnp.arange(1, E + 1, dtype=z.dtype)
            support = 1.0 + k * z_sorted > z_cum
            k_z = jnp.sum(support, axis=-1, keepdims=True)
            tau_sum = jnp.take_along_axis(z_cum, k_z.astype(jnp.int32) - 1, axis=-1)
            tau = (tau_sum - 1.0) / k_z.astype(z.dtype)
            return jnp.maximum(z - tau, 0.0)
        base_out = jnp.einsum('bsd,od->bso', x, W_base) + b_base
        logits = jnp.einsum('bsd,ed->bse', x, W_router) + b_router
        weights = sparsemax(logits)
        h = jnp.einsum('bsd,edr->bser', x, lora_A)
        expert_out = jnp.einsum('bser,bse,ero->bso', h, weights, lora_B)
        return base_out + expert_out
    x = _layernorm(x + _L0_attn_ref(x, L0_attn_weight, L0_attn_mask), axis=-1)
    x = _layernorm(x + _L0_xattn_ref(x, ctx_4096, L0_xattn_x1_scale, L0_xattn_x1_zp, L0_xattn_x2_scale, L0_xattn_x2_zp), axis=-1)
    x = _layernorm(x + _L0_ffn_ref(x, L0_ffn_weight, L0_ffn_bias, L0_ffn_centroids, L0_ffn_assignments), axis=-1)
    x = _layernorm(x + _L1_attn_ref(x, L1_attn_w_attn, L1_attn_b_attn, L1_attn_w_proj, L1_attn_b_proj), axis=-1)
    x = _layernorm(x + _L1_xattn_ref(x, ctx_4096, mask_1x1xSxS2_ff0, L1_xattn_q_proj_w, L1_xattn_k_proj_w, L1_xattn_v_proj_w, L1_xattn_o_proj_w, L1_xattn_q_norm_w, L1_xattn_k_norm_w), axis=-1)
    x = _layernorm(x + _L1_ffn_ref(x, L1_ffn_W_base, L1_ffn_b_base, L1_ffn_W_router, L1_ffn_b_router, L1_ffn_lora_A, L1_ffn_lora_B), axis=-1)
    return x

_drawn_inputs = setup_inputs


def setup_inputs(seed=0):
    import zlib

    import numpy as np

    out = dict(_drawn_inputs(seed))
    spreads = {'L1_attn_b_attn': (0.0, 0.285),
     'L1_attn_b_proj': (0.0, 0.1),
     'L1_xattn_q_norm_w': (1.0, 0.2),
     'L1_xattn_k_norm_w': (1.0, 0.2),
     'L1_ffn_b_router': (0.0, 0.302),
     'L1_ffn_lora_B': (0.0, 0.1)}
    factors = {'L0_ffn_bias': 4.671, 'L1_ffn_b_base': 8.0}
    for name, (base, spread) in spreads.items():
        noise = np.random.default_rng([zlib.crc32(name.encode()), seed]).standard_normal(out[name].shape)
        drawn = base * np.exp(spread * noise) if base else spread * noise
        out[name] = jnp.asarray(drawn.astype(out[name].dtype))
    for name, factor in factors.items():
        out[name] = (out[name] * factor).astype(out[name].dtype)
    return out
```

```python
import math
from contextlib import ExitStack

import concourse.bass as bass
from concourse import mybir

F32 = mybir.dt.float32
F32R = mybir.dt.float32r
BF16 = mybir.dt.bfloat16
F16 = mybir.dt.float16
I32 = mybir.dt.int32
ALU = mybir.AluOpType
ACT = mybir.ActivationFunctionType
AX_X = mybir.AxisListType.X

P = 128
B, S, S2, D = 2, 256, 512, 512
T = B * S // P
C = D // P
CT = B * S2 // P
LN_EPS = 1e-5
QMAX = 255.0
MID = 128.0
ROUND = 12582912.0
BLK = 32
NCL = 64
HIT = 0.01
INV_TEMP = 10.0
H1, D1 = 32, 16
PAIRS = H1 // 2
KQ = 384
PSCALE = 32768.0
G, J, HD = 8, 4, 128
NE, R = 8, 16
RA = NE + NE * R

K_ID, K_BLK, K_REL, K_SLOPE, K_IDX, K_CNT = 0, 128, 256, 640, 672, 673
K_ALL = K_CNT + NE


def decoder_kernel(nc, x, ctx, ctxT, amask, w0T, m0T, qs, wfT, fbias, centT, asg,
                   waT, ba, wpT, bp, wqT, wkT, wvT, woT, nw, wbT, bb, raT, br, lb, const, out):
    with ExitStack() as st:
        cursor = [nc.sbuf_base + (-nc.sbuf_base) % 32]

        def at(name, shape, dt, offset):
            return nc.alloc_sbuf_tensor_at(name, shape, dt, offset=offset)

        def size(shape, dt):
            n = {F32: 4, F32R: 4, I32: 4, BF16: 2, F16: 2}[dt]
            for s in shape[1:]:
                n *= s
            return n + (-n) % 32

        class Region:

            def __init__(self, start, room):
                self.at, self.end = start, start + room

            def __call__(self, name, shape, dt):
                t = at(name, shape, dt, self.at)
                self.at += size(shape, dt)
                assert self.at <= self.end, (name, self.at, self.end)
                return t

        def sem(name):
            return st.enter_context(nc.semaphore(name))

        base, room = cursor[0], nc.sbuf_usable_end - cursor[0]
        KEEP, R1 = 28960, 65536
        keep = Region(base, KEEP)
        r1 = Region(base + KEEP, R1)
        R2AT = base + KEEP + R1
        XROOM = room - KEEP - R1
        R3AT = R2AT + 65536

        xr = keep("xr", [P, T, D], F32)
        xth = keep("xth", [P, C, T * P], F32R)
        XTL_AT = keep.at
        xtl = keep("xtl", [P, C, T * P], F32R)
        cst = keep("cst", [P, K_ALL], F32)
        idh = keep("idh", [P, P], F16)
        idb = keep("idb", [P, P], BF16)
        oneb = keep("oneb", [P, P], BF16)
        stat = keep("stat", [P, T, 16], F32)
        scal = keep("scal", [P, 16], F32)
        half = keep("half", [P, 8], F32)
        small = keep("small", [P, 64], F32)
        ident = cst[:, K_ID:K_ID + P]

        w0l = r1("w0l", [P, C, D], F32R)
        w0h = r1("w0h", [P, C, D], F32R)
        wal = r1("wal", [P, C, 3 * D], F32R)
        wah = r1("wah", [P, C, 3 * D], F32R)
        w0raw = at("w0raw", [P, C, D], F32, base + KEEP)
        waraw = at("waraw", [P, C, 3 * D], F32, base + KEEP + 2 * 8192)

        a2 = Region(R2AT, 65536)
        m0 = a2("m0", [P, C, D], I32)
        ctxn = a2("ctxn", [P, CT, D], F32)
        c2 = a2("c2", [P, CT, D], BF16)
        CENT_AT = a2.at
        cenl = a2("cenl", [P, C, NCL], F32R)
        cenh = a2("cenh", [P, C, NCL], F32R)
        cenraw = at("cenraw", [P, C, NCL], F32, CENT_AT)
        asgi = a2("asgi", [NCL, D], I32)
        onehot = a2("onehot", [NCL, D], BF16)
        fb = a2("fb", [P, D], F32)
        bbn = a2("bbn", [P, B, D], F32)
        xb = a2("xb", [P, 2, D], F32)
        c1f = a2("c1f", [P, D], F32)
        c1 = a2("c1", [P, T, D], BF16)
        c1t = a2("c1t", [P, 2, D], BF16)
        d1 = a2("d1", [P, T, D], F32)
        msum = a2("msum", [P, C * D // BLK], F32)
        mkeep = a2("mkeep", [P, C * D // BLK], F32)

        a3 = Region(R3AT, base + room - R3AT)
        yb = a3("yb", [P, 2, D], F32)
        WF_AT = a3.at
        wfl = a3("wfl", [P, C, D], F32R)
        wfh = a3("wfh", [P, C, D], F32R)
        wfraw = at("wfraw", [P, C, D], F32, WF_AT)
        rsel = a3("rsel", [P, D], F32)

        b2 = Region(R2AT, 65536)
        wkl = b2("wkl", [P, C, G * HD], F32R)
        wkh = b2("wkh", [P, C, G * HD], F32R)
        wvl = b2("wvl", [P, C, G * HD], F32R)
        wvh = b2("wvh", [P, C, G * HD], F32R)
        wkraw = at("wkraw", [P, C, G * HD], F32, R2AT)
        wvraw = at("wvraw", [P, C, G * HD], F32, R2AT + 32768)
        kf = at("kf", [P, G, B * S2], F32, base + KEEP)
        vf = at("vf", [P, CT, G * HD], F32, base + KEEP + 32768)
        b3 = Region(R3AT + size([P, 2, D], F32), base + room - R3AT - size([P, 2, D], F32))
        QR_AT = b3.at
        qr = b3("qr", [P, PAIRS, T, 2 * D1], F32)
        kr = b3("kr", [P, PAIRS, T, 2 * D1], F32)
        v3 = b3("v3", [P, T * H1 * 3 * D1], BF16)
        BA_AT = b3.at
        rowp = b3("rowp", [P, 2, KQ], F32)
        bias = b3("bias", [P, 2, KQ], F32)
        phl = b3("phl", [P, 2, 2, KQ], F16)
        ptb = b3("ptb", [P, 2, 2 * KQ], F16)
        CT_AT = b3.at
        ctl = [b3(f"ctl{n}", [P, C, P], F32R)[:] for n in range(2)]
        ctr = [at(f"ctr{n}", [P, C, P], F32, CT_AT + n * C * P * 4)[:] for n in range(2)]
        cth = [b3("cth0", [P, C, P], F32R)[:],
               at("cth1", [P, C, B * S2], F32R, base + KEEP + 16384)[:, :, (CT - 1) * P:]]
        nrm = b3("nrm", [P, 64], F32)
        bab = at("bab", [P, 3 * D], F32, BA_AT)
        ao = at("ao", [P, T, D], F32, XTL_AT)
        x1 = Region(XTL_AT - 8192, 8192)
        sq = x1("sq", [P, T, 2, 4, D1], F32R)
        sk = x1("sk", [P, T, 2, 4, D1], F32R)
        qt = [x1("qt0", [P, T * P], F32R), at("qt1", [P, T * P], F32R, base + KEEP + 65536 - 4096)]
        kt = [x1("kt0", [P, T * P], F32R), at("kt1", [P, T * P], F32R, base + KEEP + 65536 - 2048)]
        nmx, zsum, zinv = nrm[:, 0:2], nrm[:, 8:24], nrm[:, 24:32]
        kss, kpw, wqk = nrm[:, 32:40], nrm[:, 40:48], nrm[:, 48:49]
        nwt = nrm[:, 50:52]
        orow = b3("orow", [P, T * 2 * D1], F32)
        wpl = at("wpl", [P, C, D], F32R, QR_AT)
        wph = at("wph", [P, C, D], F32R, QR_AT + 8192)
        wpraw = at("wpraw", [P, C, D], F32, QR_AT)
        ath = at("ath", [P, C, T * P], F32R, R2AT)
        atl = at("atl", [P, C, T * P], F32R, R2AT + 8192)
        x2 = Region(R2AT, 65536)
        woh = x2("woh", [P, J, D], F32R)
        wol = x2("wol", [P, J, D], F32R)
        STG_AT = x2.at
        stg = x2("stg", [P, C, D], F32)
        WQ_AT = x2.at
        wqh = x2("wqh", [P, C, D], F32R)
        wql = x2("wql", [P, C, D], F32R)
        kh = x2("kh", [P, B, S2], F32R)
        kl = x2("kl", [P, B, S2], F32R)
        vh = x2("vh", [P, B, S2 // P, HD], F32R)
        vl = x2("vl", [P, B, S2 // P, HD], F32R)
        mk = x2("mk", [P, S // P, S2], F32)
        sqj = x2("sqj", [P, D], F32)
        px3 = x2("px3", [P, S2], F32)
        x3 = Region(QR_AT, base + room - QR_AT)
        QT_AT = x3.at
        qth = x3("qth", [P, B, J, S], F32R)
        qtl = x3("qtl", [P, B, J, S], F32R)
        bpb = at("bpb", [P, D], F32, x3.at)
        oth = x3("oth", [P, B, J, S], F32R)
        otl = x3("otl", [P, B, J, S], F32R)
        pth = x3("pth", [P, S2 // P, S], F32R)
        ptl = x3("ptl", [P, S2 // P, S], F32R)
        px = [x3(f"px{n}", [P, S2], F32) for n in range(3)] + [px3]
        xmx, xz, xzi = small[:, 0:4], small[:, 4:8], small[:, 8:12]
        qss, qpw = small[:, 16:24], small[:, 24:32]
        wbh = at("wbh", [P, C, D], F32R, WQ_AT)
        wbl = at("wbl", [P, C, D], F32R, WQ_AT + 8192)
        wbraw = at("wbraw", [P, C, D], F32, WQ_AT + 8192)
        f4 = Region(STG_AT, 8192)
        rah = f4("rah", [P, C, RA], F32R)
        RA_AT = f4.at
        ral = f4("ral", [P, C, RA], F32R)
        raraw = at("raraw", [P, C, RA], F32, RA_AT)
        LB_AT = f4.at
        lbl = f4("lbl", [P, D], F32R)
        lbraw = at("lbraw", [P, D], F32, LB_AT)
        lbh = at("lbh", [P, D], F32R, STG_AT - 16384)
        f5 = Region(QT_AT, 16384)
        bbb = f5("bbb", [P, D], F32)
        brb = f5("brb", [P, NE], F32)
        hw = f5("hw", [P, 2, NE * R], F32)
        hth = f5("hth", [P, 2, NE * R], F32R)
        htl = f5("htl", [P, 2, NE * R], F32R)
        zt = f5("zt", [P, 2, 64], F32)
        f2 = a3("f2", [P, T, 4], F32)
        csel = a3("csel", [NCL, P], BF16)
        hits = a3("hits", [P, T, NCL], BF16)
        prob = a3("prob", [P, T, NCL], F32)

        bank = [st.enter_context(nc.psum_tensor(f"bank{i}", [P, 512], F32)) for i in range(8)]
        bank16 = [b[:].bitcast(BF16) for b in bank]
        bank16f = [b[:].bitcast(F16) for b in bank]

        d_cst, d_x, d_m0, d_w0, d_sc, d_ctx, d_wf, d_cen, d_asg, d_fb = (
            sem("d_" + n) for n in "cst x m0 w0 sc ctx wf cen asg fb".split())
        d_out = sem("d_out")
        consts = sem("consts")
        mask_summed = sem("mask_summed")
        mask_counts = sem("mask_counts")
        w0_masked = sem("w0_masked")
        w0_high = sem("w0_high")
        w0_split = sem("w0_split")
        xt_psum = sem("xt_psum")
        xt_high = sem("xt_high")
        xt_ready = sem("xt_ready")
        gemm_done = sem("gemm_done")
        moments = sem("moments")
        rstd = sem("rstd")
        ln_done = sem("ln_done")
        vchain = sem("vchain")
        wt_high = sem("wt_high")
        wt_split = sem("wt_split")
        c2_ready = sem("c2_ready")
        c1_ready = sem("c1_ready")
        c1_psum = sem("c1_psum")
        c1t_ready = sem("c1t_ready")
        r2_psum = sem("r2_psum")
        bbn_ready = sem("bbn_ready")
        xb_ready = sem("xb_ready")
        xat_done = sem("xat_done")
        rowb_ready = sem("rowb_ready")
        u_ready = sem("u_ready")
        xb_used = sem("xb_used")
        lg_psum = sem("lg_psum")
        lg_max = sem("lg_max")
        lg_exp = sem("lg_exp")
        hits_ready = sem("hits_ready")
        cl_psum = sem("cl_psum")
        csel_ready = sem("csel_ready")
        onehot_ready = sem("onehot_ready")
        rsel_ready = sem("rsel_ready")
        wa_high, wa_split = sem("wa_high"), sem("wa_split")
        wk_high, wk_split = sem("wk_high"), sem("wk_split")
        wv_high, wv_split = sem("wv_high"), sem("wv_split")
        wp_high, wp_split = sem("wp_high"), sem("wp_split")
        d_wa, d_ba, d_wk, d_wv, d_nw, d_wp, d_bp = (
            sem("d_" + n) for n in "wa ba wk wv nw wp bp".split())
        d_ctl = [sem(f"d_ctl{n}") for n in range(2)]
        ba_ready = sem("ba_ready")
        qkv_done = sem("qkv_done")
        qkv_out = sem("qkv_out")
        v_high = sem("v_high")
        v_rest = sem("v_rest")
        v_mid = sem("v_mid")
        v_low = sem("v_low")
        dve_passed, pool_passed = sem("dve_passed"), sem("pool_passed")
        pstack = sem("pstack")
        stacked = sem("stacked")
        b0_full = sem("b0_full")
        b0_free = sem("b0_free")
        sc_done = sem("sc_done")
        mx_done = sem("mx_done")
        ex_done = sem("ex_done")
        bias_ready = sem("bias_ready")
        ph_high = sem("ph_high")
        o_sum = sem("o_sum")
        k_add = sem("k_add")
        phl_ready = sem("phl_ready")
        pt_psum = sem("pt_psum")
        pt_ready = sem("pt_ready")
        pv_done = sem("pv_done")
        o_out = sem("o_out")
        kv_done = sem("kv_done")
        k_square = sem("k_square")
        k_sum = sem("k_sum")
        k_power = sem("k_power")
        k_row = sem("k_row")
        v_out = sem("v_out")
        ctx_high = sem("ctx_high")
        ctx_split = sem("ctx_split")
        d_mk, d_stg, d_wb, d_ra, d_lb, d_bb, d_br = (sem("d_" + n) for n in "mk stg wb ra lb bb br".split())
        wq_high, wq_split = sem("wq_high"), sem("wq_split")
        wo_high, wo_split = sem("wo_high"), sem("wo_split")
        kx_high, kx_split = sem("kx_high"), sem("kx_split")
        vx_high, vx_split = sem("vx_high"), sem("vx_split")
        q_done = sem("q_done")
        q_raw = sem("q_raw")
        q_square = sem("q_square")
        q_add = sem("q_add")
        q_sum = sem("q_sum")
        q_power = sem("q_power")
        q_norm = sem("q_norm")
        q_psum = sem("q_psum")
        q_high = sem("q_high")
        q_low = sem("q_low")
        s_done = sem("s_done")
        s_max = sem("s_max")
        s_exp = sem("s_exp")
        z_inv = sem("z_inv")
        p_norm = sem("p_norm")
        p_psum = sem("p_psum")
        p_high = sem("p_high")
        p_low = sem("p_low")
        a_done = sem("a_done")
        a_high = sem("a_high")
        a_low = sem("a_low")
        o_done = sem("o_done")
        o_added = sem("o_added")
        f_high, f_split = sem("f_high"), sem("f_split")
        ra_done = sem("ra_done")
        hw_ready = sem("hw_ready")
        hw_psum = sem("hw_psum")
        hw_high = sem("hw_high")
        hw_split = sem("hw_split")
        ff_done = sem("ff_done")
        nw_ready = sem("nw_ready")

        block = st.enter_context(nc.Block())

        @block.sync
        def _(sp):
            sp.dma_start(cst[:], const).then_inc(d_cst, 16)
            sp.dma_start(m0[:], m0T.rearrange("(c p) n -> p c n", p=P)).then_inc(d_m0, 16)
            sp.dma_start(w0raw[:], w0T.rearrange("(c p) n -> p c n", p=P)).then_inc(d_w0, 16)
            sp.dma_start(xr[:], x.rearrange("(t p) n -> p t n", p=P)).then_inc(d_x, 16)
            sp.dma_start(scal[:, 0:4], qs.partition_broadcast(P)).then_inc(d_sc, 16)
            sp.dma_start(ctxn[:], ctx.rearrange("(t p) n -> p t n", p=P)).then_inc(d_ctx, 16)
            sp.dma_start(wfraw[:], wfT.rearrange("(c p) n -> p c n", p=P)).then_inc(d_wf, 16)
            sp.dma_start(cenraw[:], centT.rearrange("(c p) n -> p c n", p=P)).then_inc(d_cen, 16)
            sp.dma_start(asgi[:], asg.partition_broadcast(NCL)).then_inc(d_asg, 16)
            sp.dma_start(fb[:], fbias.partition_broadcast(P)).then_inc(d_fb, 16)
            sp.dma_start(waraw[:], waT.rearrange("(c p) n -> p c n", p=P)).then_inc(d_wa, 16)
            sp.wait_ge(xat_done, T)
            sp.wait_ge(bbn_ready, B)
            sp.dma_start(wkraw[:], wkT.rearrange("(c p) n -> p c n", p=P)).then_inc(d_wk, 16)
            sp.wait_ge(ln_done, 3 * T)
            sp.wait_ge(xt_ready, 2 * T)
            sp.dma_start(wvraw[:], wvT.rearrange("(c p) n -> p c n", p=P)).then_inc(d_wv, 16)
            sp.dma_start(bab[:], ba.partition_broadcast(P)).then_inc(d_ba, 16)
            sp.dma_start(nwt, nw).then_inc(d_nw, 16)
            ctile = ctxT.rearrange("(c p) n -> p c n", p=P)
            sp.dma_start(ctr[0], ctile[:, :, 0:P]).then_inc(d_ctl[0], 16)
            sp.dma_start(ctr[1], ctile[:, :, P:2 * P]).then_inc(d_ctl[1], 16)
            with sp.Fori(1, CT // 2) as j:
                for n in range(2):
                    sp.wait_ge(kv_done, j * 8 - 4 + 4 * n)
                    sp.dma_start(ctr[n], ctile[:, :, bass.ds(j * 2 * P + n * P, P)]).then_inc(d_ctl[n], 16)
            sp.wait_ge(stacked, 2 * PAIRS)
            sp.dma_start(wpraw[:], wpT.rearrange("(c p) n -> p c n", p=P)).then_inc(d_wp, 16)
            sp.wait_ge(kv_done, 4 * CT)
            sp.dma_start(bpb[:], bp.partition_broadcast(P)).then_inc(d_bp, 16)
            sp.dma_start(mk[:], amask.rearrange("(q p) n -> p q n", p=P)).then_inc(d_mk, 16)
            wq_g = wqT.rearrange("(c p) n -> p c n", p=P)
            wo_g = woT.rearrange("(h p) n -> p h n", p=P)
            sp.dma_start(stg[:], wq_g[:, :, 0:D]).then_inc(d_stg, 16)
            sp.wait_ge(wq_split, C)
            sp.dma_start(stg[:], wq_g[:, :, D:2 * D]).then_inc(d_stg, 16)

            def sp_body(g, more):
                sp.wait_ge(wq_split, g * C + 2 * C if more or isinstance(g, int) and g + 2 <= G else G * C)
                sp.dma_start(stg[:], wo_g[:, bass.ds(g * J, J), :]).then_inc(d_stg, 16)
                if more:
                    sp.wait_ge(wo_split, g * J + J)
                    sp.dma_start(stg[:], wq_g[:, :, bass.ds(g * D + 2 * D, D)]).then_inc(d_stg, 16)

            with sp.Fori(0, G - 2) as g:
                sp_body(g, True)
            sp_body(G - 2, False)
            sp.wait_ge(q_done, T * G)
            sp.dma_start(wbraw[:], wbT.rearrange("(c p) n -> p c n", p=P)).then_inc(d_wb, 16)
            sp.wait_ge(wo_split, (G - 1) * J)
            sp_body(G - 1, False)
            sp.wait_ge(wo_split, G * J)
            sp.dma_start(raraw[:], raT.rearrange("(c p) n -> p c n", p=P)).then_inc(d_ra, 16)
            sp.dma_start(lbraw[:], lb).then_inc(d_lb, 16)
            sp.wait_ge(s_done, 2 * 8 * G)
            sp.dma_start(bbb[:], bb.partition_broadcast(P)).then_inc(d_bb, 16)
            sp.dma_start(brb[:], br.partition_broadcast(P)).then_inc(d_br, 16)
            rows = out.rearrange("(t p) n -> p t n", p=P)
            for t in range(T):
                sp.wait_ge(ln_done, 5 * T + t + 1)
                sp.dma_start(rows[:, t, :], xr[:, t, :]).then_inc(d_out, 16)
            sp.wait_ge(d_out, 16 * T)

        @block.gpsimd
        def _(pool):
            pool.memset(half[:], -0.5).then_inc(consts, 1)
            pool.memset(oneb[:], 1.0).then_inc(consts, 1)
            pool.wait_ge(d_cst, 16)
            pool.tensor_copy(idh[:], ident).then_inc(consts, 1)
            pool.tensor_copy(idb[:], ident).then_inc(consts, 1)
            pool.wait_ge(consts, 4)

            def low(job, lo, raw, hi):
                pool.wait_ge(wt_high, job)
                pool.tensor_tensor(lo, raw, hi.bitcast(F32), ALU.subtract).then_inc(wt_split, 1)

            def ln_power(n):
                pool.wait_ge(moments, n + 1)
                s = stat[:, n % T, :]
                pool.tensor_tensor(s[:, 9:10], s[:, 8:9], half[:, 0:1], ALU.pow).then_inc(rstd, 1)

            low(1, wfl[:], wfraw[:], wfh[:])
            low(2, cenl[:], cenraw[:], cenh[:])
            def wa_low(n):
                c, q = n // 3, n % 3 * D
                pool.wait_ge(wa_high, c + 1)
                pool.tensor_tensor(wal[:, c, q:q + D], waraw[:, c, q:q + D], wah[:, c, q:q + D].bitcast(F32),
                                   ALU.subtract).then_inc(wa_split, 1)

            for t in range(T):
                ln_power(t)
                wa_low(t)
            for t in range(T):
                wa_low(T + t)
                pool.wait_ge(ln_done, t + 1)
                pool.wait_ge(bbn_ready, t // 2 + 1)
                if t >= 2:
                    pool.wait_ge(xb_used, t - 1)
                pool.tensor_tensor(xb[:, t % 2, :], xr[:, t, :], bbn[:, t // 2, :], ALU.add).then_inc(xb_ready, 1)
                if t >= 1:
                    ln_power(T + t - 1)
            ln_power(2 * T - 1)
            for t in range(T):
                wa_low(2 * T + t)
                ln_power(2 * T + t)
            for c in range(C):
                pool.wait_ge(wk_high, c + 1)
                pool.tensor_tensor(wkl[:, c, :], wkraw[:, c, :], wkh[:, c, :].bitcast(F32), ALU.subtract)\
                    .then_inc(wk_split, 1)
            for t in range(T):
                part = v3[:, t * H1 * 3 * D1:(t + 1) * H1 * 3 * D1].rearrange("p (h k d) -> p h k d", k=3, d=D1)
                pool.wait_ge(v_mid, t + 1)
                pool.tensor_tensor(part[:, :, 2, :], yb[:, 1, :].rearrange("p (h d) -> p h d", d=D1),
                                   part[:, :, 1, :], ALU.subtract).then_inc(v_low, 1)
            for c in range(C):
                pool.wait_ge(wv_high, c + 1)
                pool.tensor_tensor(wvl[:, c, :], wvraw[:, c, :], wvh[:, c, :].bitcast(F32), ALU.subtract)\
                    .then_inc(wv_split, 1)

            def stack(n):
                pair = [P, 2 * T, 2, D1]
                src_q = qr[:].rearrange("p a t k -> p (a t k)")[:, bass.ds(n * P, P)]\
                    .rearrange("p (a d) -> p a d", d=D1).unsqueeze(2).broadcast_to(pair)
                src_k = kr[:].rearrange("p a t k -> p (a t k)")[:, bass.ds(n * P, P)]\
                    .rearrange("p (a d) -> p a d", d=D1).unsqueeze(2).broadcast_to(pair)
                q4 = sq[:].rearrange("p t h k d -> p (t h) k d")
                k4 = sk[:].rearrange("p t h k d -> p (t h) k d")
                pool.tensor_copy(q4[:, :, 0:2, :], src_q).then_inc(pstack, 1)
                pool.tensor_copy(k4[:, :, 0:4:2, :], src_k).then_inc(pstack, 1)
                pool.wait_ge(pstack, n * 2 + 2)
                pool.sem_inc(pool_passed, 1)
                pool.tensor_tensor(q4[:, :, 2:4, :], src_q, q4[:, :, 0:2, :].bitcast(F32), ALU.subtract)\
                    .then_inc(stacked, 1)
                pool.tensor_tensor(k4[:, :, 1:4:2, :], src_k, k4[:, :, 0:4:2, :].bitcast(F32), ALU.subtract)\
                    .then_inc(stacked, 1)

            def context_low(i, n):
                pool.wait_ge(ctx_high, i + 1)
                pool.tensor_tensor(ctl[n], ctr[n], cth[n].bitcast(F32), ALU.subtract).then_inc(ctx_split, 1)

            def key_power(i, h):
                pool.wait_ge(k_sum, i * 2 + h + 1)
                pool.tensor_tensor(kpw[:, 4 * h:4 * h + 4], kss[:, 4 * h:4 * h + 4], half[:, 0:4], ALU.pow)\
                    .then_inc(k_power, 1)

            def pool_body(i, odd, last=False):
                if not last:
                    pool.wait_ge(b0_full, i * 6 + 4)
                    stack(i * 2 + 2)
                key_power(i, 0)
                if not last:
                    context_low(i + 1, 1 - odd)
                key_power(i, 1)
                if not last:
                    pool.wait_ge(b0_full, i * 6 + 7)
                    stack(i * 2 + 3)

            pool.wait_ge(qkv_out, 3 * T)
            stack(0)
            context_low(0, 0)
            pool.wait_ge(b0_full, 2)
            stack(1)
            pool_body(0, 0)
            with pool.Fori(0, CT // 2 - 1) as j:
                pool_body(j * 2 + 1, 1)
                pool_body(j * 2 + 2, 0)
            pool_body(CT - 1, 1, last=True)
            pool.wait_ge(wp_high, 1)
            pool.tensor_tensor(wpl[:], wpraw[:], wph[:].bitcast(F32), ALU.subtract).then_inc(wp_split, 1)
            for t in range(T):
                ln_power(3 * T + t)
            def wq_low(g):
                for c in range(C):
                    pool.wait_ge(wq_high, g * 2 + c // 2 + 1)
                    pool.tensor_tensor(wql[:, c, :], stg[:, c, :], wqh[:, c, :].bitcast(F32), ALU.subtract)\
                        .then_inc(wq_split, 1)

            def wo_low(g):
                for j in range(J):
                    pool.wait_ge(wo_high, g * 2 + j // 2 + 1)
                    pool.tensor_tensor(wol[:, j, :], stg[:, j, :], woh[:, j, :].bitcast(F32), ALU.subtract)\
                        .then_inc(wo_split, 1)

            def keys_low(g, b):
                pool.wait_ge(kx_high, g * 2 + b + 1)
                pool.tensor_tensor(kl[:, b:b + 1, :], kf[:, bass.ds(g, 1), b * S2:(b + 1) * S2],
                                   kh[:, b:b + 1, :].bitcast(F32), ALU.subtract).then_inc(kx_split, 1)

            def values_low(g, b):
                pool.wait_ge(vx_high, g * 2 + b + 1)
                pool.tensor_tensor(vl[:, b], vf[:, b * C:(b + 1) * C, bass.ds(g * HD, HD)],
                                   vh[:, b].bitcast(F32), ALU.subtract).then_inc(vx_split, 1)

            def query_power(n, slot):
                pool.wait_ge(q_sum, n + 1)
                pool.tensor_tensor(qpw[:, 4 * slot:4 * slot + 4], qss[:, 4 * slot:4 * slot + 4], half[:, 0:4], ALU.pow)\
                    .then_inc(q_power, 1)

            wq_low(0)
            keys_low(0, 0)
            keys_low(0, 1)
            values_low(0, 0)
            values_low(0, 1)
            for t in range(T):
                query_power(t, t % 2)
            wq_low(1)

            def pool_group(g, more, most):
                if not (isinstance(g, int) and g == 0):
                    values_low(g, 1)
                if more:
                    query_power(g * T + T, 0)
                wo_low(g)
                if more:
                    query_power(g * T + T + 1, 1)
                    keys_low(g + 1, 0)
                    values_low(g + 1, 0)
                    query_power(g * T + T + 2, 0)
                    query_power(g * T + T + 3, 1)
                if most:
                    wq_low(g + 2)
                if more:
                    keys_low(g + 1, 1)

            pool_group(0, True, True)
            with pool.Fori(1, G - 2) as g:
                pool_group(g, True, True)
            pool_group(G - 2, True, False)
            pool_group(G - 1, False, False)
            pool.wait_ge(f_high, 1)
            pool.tensor_tensor(wbl[:], wbraw[:], wbh[:].bitcast(F32), ALU.subtract).then_inc(f_split, 1)
            pool.wait_ge(f_high, 2)
            pool.tensor_tensor(ral[:], raraw[:], rah[:].bitcast(F32), ALU.subtract).then_inc(f_split, 1)
            for t in range(T):
                ln_power(4 * T + t)
            pool.wait_ge(f_high, 3)
            pool.tensor_tensor(lbl[:], lbraw[:], lbh[:].bitcast(F32), ALU.subtract).then_inc(f_split, 1)
            for t in range(T):
                ln_power(5 * T + t)

        @block.scalar
        def _(act):
            act.wait_ge(consts, 4)
            for c in range(C):
                act.wait_ge(w0_masked, c + 1)
                act.activation(w0h[:, c, :], w0raw[:, c, :], ACT.Copy).then_inc(w0_high, 1)

            def xt_high_parts(n):
                t = n % T
                act.wait_ge(xt_psum, n + 1)
                act.activation(xth[:, :, t * P:(t + 1) * P],
                               bank[t % 2][:].rearrange("p (c q) -> p c q", c=C), ACT.Copy).then_inc(xt_high, 1)

            def high(dma, hi, raw):
                act.wait_ge(dma, 16)
                act.activation(hi, raw, ACT.Copy).then_inc(wt_high, 1)

            for t in range(T):
                xt_high_parts(t)
            high(d_wf, wfh[:], wfraw[:])
            high(d_cen, cenh[:], cenraw[:])
            act.wait_ge(d_wa, 16)
            for c in range(C):
                act.activation(wah[:, c, :], waraw[:, c, :], ACT.Copy).then_inc(wa_high, 1)
            for t in range(T):
                act.wait_ge(c1_psum, t + 1)
                act.activation(c1t[:, t % 2, :], bank16[t % 2][:, 0:D], ACT.Copy).then_inc(c1t_ready, 1)
                if t >= 1:
                    act.wait_ge(rowb_ready, t)
                    act.activation(yb[:, (t - 1) % 2, :], bank[2 + t - 1][:], ACT.Identity,
                                   bias=stat[:, t - 1, 11:12], scale=scal[:, 6:7]).then_inc(u_ready, 1)
            act.wait_ge(rowb_ready, T)
            act.activation(yb[:, (T - 1) % 2, :], bank[2 + T - 1][:], ACT.Identity,
                           bias=stat[:, T - 1, 11:12], scale=scal[:, 6:7]).then_inc(u_ready, 1)

            for t in range(T):
                xt_high_parts(T + t)
                if t >= 1:
                    act.wait_ge(lg_max, t)
                    act.activation(prob[:, t - 1, :], bank[6 + (t - 1) % 2][:, 0:NCL], ACT.Exp, scale=INV_TEMP,
                                   bias=f2[:, t - 1, 0:1], accum_out=f2[:, t - 1, 1:2]).then_inc(lg_exp, 1)
            act.wait_ge(lg_max, T)
            act.activation(prob[:, T - 1, :], bank[6 + (T - 1) % 2][:, 0:NCL], ACT.Exp, scale=INV_TEMP,
                           bias=f2[:, T - 1, 0:1], accum_out=f2[:, T - 1, 1:2]).then_inc(lg_exp, 1)
            act.wait_ge(cl_psum, 2)
            act.activation(rsel[:], bank[6][:], ACT.Copy).then_inc(rsel_ready, 1)
            def value_parts(t):
                part = v3[:, t * H1 * 3 * D1:(t + 1) * H1 * 3 * D1].rearrange("p (h k d) -> p h k d", k=3, d=D1)
                act.wait_ge(qkv_out, 3 * t + 3)
                act.activation(part[:, :, 0, :], yb[:, 0, :].rearrange("p (h d) -> p h d", d=D1), ACT.Copy)\
                    .then_inc(v_high, 1)
                act.wait_ge(v_rest, t + 1)
                act.activation(part[:, :, 1, :], yb[:, 1, :].rearrange("p (h d) -> p h d", d=D1), ACT.Copy)\
                    .then_inc(v_mid, 1)

            xt_high_parts(2 * T)
            xt_high_parts(2 * T + 1)
            act.wait_ge(d_wk, 16)
            for t in range(T):
                act.activation(wkh[:, t, :], wkraw[:, t, :], ACT.Copy).then_inc(wk_high, 1)
            for t in range(T):
                if t + 2 < T:
                    xt_high_parts(2 * T + t + 2)
                value_parts(t)
            act.wait_ge(d_wv, 16)
            for c in range(C):
                act.activation(wvh[:, c, :], wvraw[:, c, :], ACT.Copy).then_inc(wv_high, 1)

            act.wait_ge(nw_ready, 1)
            def copy_stack(n, k, e):
                act.wait_ge(b0_full, n + 1)
                act.activation((qt, kt)[k][e][:], bank[0][:], ACT.Copy).then_inc(b0_free, 1)

            def context_high(i, n, first=False):
                act.wait_ge(d_ctl[n], i * 8 + (16 - 8 * n))
                if not first:
                    act.wait_ge(kv_done, i * 4 - 4)
                act.activation(cth[n], ctr[n], ACT.Copy).then_inc(ctx_high, 1)

            def act_body(i, odd, first=False, last=False):
                def exponentials(u):
                    e, hd, b = u // 4, u // 2 % 2, u % 2
                    for q in range(2):
                        cols = slice(0, P) if q == 0 else slice(P, KQ)
                        z = e * 8 + (2 * b + q) * 2 + hd
                        act.wait_ge(mx_done, i * 16 + 2 * u + q + 1)
                        if u % 4 == 0 and q == 0 and not first:
                            act.wait_ge(o_out, i * 2 - 1 + e)
                        r = rowp[:, u % 2, cols]
                        act.activation(r, r, ACT.Exp, scale=-1.0, bias=nrm[:, 2 * (u % 2) + q:2 * (u % 2) + q + 1],
                                       accum_out=zsum[:, z:z + 1]).then_inc(ex_done, 1)

                def key_square(h):
                    act.wait_ge(kv_done, i * 4 + h + 1)
                    if h or not first:
                        act.wait_ge(k_sum, i * 2 + h)
                    act.activation(yb[:, 1, :], bank[6 + h][:], ACT.Square).then_inc(k_square, 1)

                def keys_out(h):
                    act.wait_ge(b0_full, i * 6 + (5 if h == 0 else 6 if last else 8))
                    if last:
                        act.wait_ge(kv_done, 4 * CT)
                    act.activation(kf[:, 4 * h:4 * h + 4, bass.ds(i * P, P)],
                                   bank[0][:].rearrange("p (g k) -> p g k", g=4), ACT.Copy, scale=wqk)\
                        .then_inc(b0_free, 1)

                def values_out(h):
                    act.wait_ge(kv_done, i * 4 + 3 + h)
                    if last:
                        act.wait_ge(sc_done, 8 * CT)
                    act.activation(vf[:, bass.ds(i, 1), h * D:(h + 1) * D], bank[6 + h][:].unsqueeze(1), ACT.Copy)\
                        .then_inc(v_out, 1)

                for u in range(8):
                    exponentials(u)
                    if u == 0:
                        copy_stack(i * 6 + 2, 0, 1)
                    if u == 1:
                        copy_stack(i * 6 + 3, 1, 1)
                    if u in (1, 3):
                        key_square(u // 2)
                    if u == 3 and not last:
                        context_high(i + 1, 1 - odd, first)
                    if u == 4 and not last:
                        keys_out(0)
                    if u == 5 and not last:
                        copy_stack(i * 6 + 5, 0, 0)
                    if u == 5 and not last:
                        values_out(0)
                    if u == 6 and not last:
                        copy_stack(i * 6 + 6, 1, 0)
                if last:
                    keys_out(0)
                    values_out(0)
                keys_out(1)
                values_out(1)

            context_high(0, 0, first=True)
            copy_stack(0, 0, 0)
            copy_stack(1, 1, 0)
            act_body(0, 0, first=True)
            with act.Fori(0, CT // 2 - 1) as j:
                act_body(j * 2 + 1, 1)
                act_body(j * 2 + 2, 0)
            act_body(CT - 1, 1, last=True)

            act.wait_ge(d_wp, 16)
            act.activation(wph[:], wpraw[:], ACT.Copy).then_inc(wp_high, 1)
            for t in range(T):
                act.wait_ge(xt_psum, 3 * T + t + 1)
                act.activation(ath[:, :, t * P:(t + 1) * P],
                               bank[t % 2][:].rearrange("p (c q) -> p c q", c=C), ACT.Copy).then_inc(xt_high, 1)
            def wq_high_parts(g, n):
                act.wait_ge(d_stg, n * 16 + 16)
                act.wait_ge(q_done, g * T)
                for h in range(2):
                    act.activation(wqh[:, 2 * h:2 * h + 2, :], stg[:, 2 * h:2 * h + 2, :], ACT.Copy).then_inc(wq_high, 1)

            def wo_high_parts(g):
                act.wait_ge(d_stg, 32 * G if isinstance(g, int) and g == G - 1 else g * 32 + 48)
                act.wait_ge(o_done, g * T)
                for h in range(2):
                    act.activation(woh[:, 2 * h:2 * h + 2, :], stg[:, 2 * h:2 * h + 2, :], ACT.Copy).then_inc(wo_high, 1)

            def keys_high(g, b):
                if not (isinstance(g, int) and g == 0):
                    act.wait_ge(s_done, g * 16 - 8 + 8 * b)
                act.activation(kh[:, b:b + 1, :], kf[:, bass.ds(g, 1), b * S2:(b + 1) * S2], ACT.Copy)\
                    .then_inc(kx_high, 1)

            def values_high(g, b):
                if not (isinstance(g, int) and g == 0):
                    act.wait_ge(a_done, g * 8 - 4 + 4 * b)
                act.activation(vh[:, b], vf[:, b * C:(b + 1) * C, bass.ds(g * HD, HD)], ACT.Copy).then_inc(vx_high, 1)

            def query_square(n, slot):
                act.wait_ge(q_done, n + 1)
                if not (isinstance(n, int) and n < 2):
                    act.wait_ge(q_psum, n - 1)
                act.activation(yb[:, slot, :], bank[5][:], ACT.Copy).then_inc(q_raw, 1)
                act.wait_ge(q_raw, n + 1)
                if not (isinstance(n, int) and n == 0):
                    act.wait_ge(q_sum, n)
                act.activation(sqj[:], yb[:, slot, :], ACT.Square).then_inc(q_square, 1)

            def query_high(n, t):
                act.wait_ge(q_psum, n + 1)
                act.activation(qth[:, t // 2, :, t % 2 * P:(t % 2 + 1) * P],
                               bank[6][:].rearrange("p (j q) -> p j q", j=J), ACT.Copy).then_inc(q_high, 1)

            def scores_exp(g, u):
                for q in range(2):
                    k = 2 * (u % 2) + q
                    act.wait_ge(s_max, g * 16 + 2 * u + q + 1)
                    act.activation(px[k][:], px[k][:], ACT.Exp, scale=-1.0, bias=xmx[:, k:k + 1],
                                   accum_out=xz[:, k:k + 1]).then_inc(s_exp, 1)

            def probs_high(g, u):
                for q in range(2):
                    act.wait_ge(p_psum, g * 16 + 2 * u + q + 1)
                    act.activation(pth[:, :, q * P:(q + 1) * P], bank[2 + q][:].rearrange("p (k q) -> p k q", q=P),
                                   ACT.Copy).then_inc(p_high, 1)

            def output_high(g, u):
                act.wait_ge(a_done, g * 8 + u + 1)
                act.activation(oth[:, u // 4, u % 4, :], bank[4][:, 0:S], ACT.Copy).then_inc(a_high, 1)

            wq_high_parts(0, 0)
            for b in range(B):
                keys_high(0, b)
            for b in range(B):
                values_high(0, b)
            for t in range(T):
                xt_high_parts(4 * T + t)
            for t in range(T):
                query_square(t, t % 2)
                if t:
                    query_high(t - 1, t - 1)
            query_high(T - 1, T - 1)
            wq_high_parts(1, 1)
            scores_exp(0, 0)

            def act_group(g, more, most):
                first = isinstance(g, int) and g == 0
                for u in range(8):
                    if u:
                        output_high(g, u - 1)
                    elif not first:
                        output_high(g - 1, 7)
                        values_high(g, 1)
                    probs_high(g, u)
                    if u < 7:
                        scores_exp(g, u + 1)
                    elif more:
                        scores_exp(g + 1, 0)
                    if more and u in (1, 2, 4, 5):
                        t = (0, 1, 2, 3)[(1, 2, 4, 5).index(u)]
                        query_square(g * T + T + t, t % 2)
                    if u == 2:
                        wo_high_parts(g)
                    if more and u == 3:
                        keys_high(g + 1, 0)
                    if more and u == 4:
                        values_high(g + 1, 0)
                    if more and u in (3, 4, 6, 7):
                        t = (3, 4, 6, 7).index(u)
                        query_high(g * T + T + t, t)
                    if most and u == 6:
                        wq_high_parts(g + 2, g * 2 + 3)
                    if more and u == 7:
                        keys_high(g + 1, 1)

            act_group(0, True, True)
            with act.Fori(1, G - 2) as g:
                act_group(g, True, True)
            act_group(G - 2, True, False)
            act_group(G - 1, False, False)
            output_high(G - 1, 7)
            act.wait_ge(d_wb, 16)
            act.activation(wbh[:], wbraw[:], ACT.Copy).then_inc(f_high, 1)
            act.wait_ge(d_ra, 16)
            act.activation(rah[:], raraw[:], ACT.Copy).then_inc(f_high, 1)
            act.wait_ge(d_lb, 16)
            act.wait_ge(o_done, T * G)
            act.activation(lbh[:], lbraw[:], ACT.Copy).then_inc(f_high, 1)
            xt_high_parts(5 * T)
            xt_high_parts(5 * T + 1)
            for t in range(T):
                act.wait_ge(hw_psum, t + 1)
                act.activation(hth[:, t % 2, :], bank[t % 2][:, 0:P], ACT.Copy).then_inc(hw_high, 1)
                if t + 2 < T:
                    xt_high_parts(5 * T + t + 2)

        @block.vector
        def _(dve):
            chain = [0]

            def link(ins):
                chain[0] += 1
                ins.then_inc(vchain, 1)
                dve.wait_ge(vchain, chain[0])

            def xt_low_parts(n):
                t = n % T
                dve.wait_ge(xt_high, n + 1)
                dve.tensor_tensor(xtl[:, :, t * P:(t + 1) * P], bank[t % 2][:].rearrange("p (c q) -> p c q", c=C),
                                  xth[:, :, t * P:(t + 1) * P].bitcast(F32), ALU.subtract).then_inc(xt_ready, 1)

            def layer_norm(n, y, into):
                s = stat[:, n % T, :]
                link(dve.bn_stats(s[:, 0:6], y))
                link(dve.bn_aggr(s[:, 6:8], s[:, 0:6]))
                dve.tensor_scalar(s[:, 8:9], s[:, 7:8], LN_EPS, None, ALU.add).then_inc(moments, 1)
                dve.wait_ge(rstd, n + 1)
                dve.tensor_scalar(into, y, s[:, 6:7], s[:, 9:10], ALU.subtract, ALU.mult).then_inc(ln_done, 1)

            dve.wait_ge(d_m0, 16)
            dve.tensor_reduce(msum[:], m0[:].rearrange("p c (n k) -> p (c n) k", k=BLK), AX_X, ALU.add)\
                .then_inc(mask_summed, 1)
            dve.wait_ge(d_sc, 16)
            link(dve.reciprocal(scal[:, 4:6], scal[:, 0:4:2]))
            link(dve.tensor_tensor(scal[:, 6:7], scal[:, 0:1], scal[:, 2:3], ALU.mult))
            link(dve.tensor_scalar(scal[:, 7:9], scal[:, 1:4:2], -1.0, MID, ALU.mult, ALU.add))
            link(dve.tensor_scalar(scal[:, 9:11], scal[:, 7:9], scal[:, 6:7], None, ALU.mult))
            link(dve.tensor_scalar(scal[:, 11:12], scal[:, 9:10], scal[:, 8:9], float(D), ALU.mult, ALU.mult))
            dve.wait_ge(mask_counts, 1)
            link(dve.tensor_scalar(mkeep[:], bank[6][:, 0:C * D // BLK], 0.0, None, ALU.is_gt))
            dve.wait_ge(d_w0, 16)
            kp = mkeep[:].rearrange("p (c n) -> p c n", c=C)
            for c in range(C):
                w = w0raw[:, c, :].rearrange("p (n k) -> p n k", k=BLK)
                dve.tensor_tensor(w, w, kp[:, c, :].unsqueeze(2).broadcast_to([P, D // BLK, BLK]), ALU.mult)\
                    .then_inc(w0_masked, 1)
            for c in range(C):
                dve.wait_ge(w0_high, c + 1)
                dve.tensor_tensor(w0l[:, c, :], w0raw[:, c, :], w0h[:, c, :].bitcast(F32), ALU.subtract)\
                    .then_inc(w0_split, 1)
            for t in range(T):
                xt_low_parts(t)
            dve.wait_ge(d_ctx, 16)
            for b in range(B):
                v = ctxn[:, b * C:(b + 1) * C, :]
                link(dve.tensor_scalar(v, v, scal[:, 5:6], scal[:, 3:4], ALU.mult, ALU.add))
                link(dve.tensor_scalar(v, v, 0.0, QMAX, ALU.max, ALU.min))
                dve.tensor_scalar(c2[:, b * C:(b + 1) * C, :], v, ROUND, ROUND + MID, ALU.add, ALU.subtract)\
                    .then_inc(c2_ready, 1)

            def quantise(t):
                link(dve.tensor_scalar(c1f[:], xr[:, t, :], scal[:, 4:5], scal[:, 1:2], ALU.mult, ALU.add))
                link(dve.tensor_scalar(c1f[:], c1f[:], 0.0, QMAX, ALU.max, ALU.min))
                dve.tensor_scalar(c1[:, t, :], c1f[:], ROUND, ROUND + MID, ALU.add, ALU.subtract)\
                    .then_inc(c1_ready, 1)

            for t in range(T):
                dve.wait_ge(gemm_done, t + 1)
                link(dve.tensor_tensor(yb[:, t % 2, :], bank[2 + t][:], xr[:, t, :], ALU.add))
                layer_norm(t, yb[:, t % 2, :], xr[:, t, :])
                dve.wait_ge(ln_done, t + 1)
                quantise(t)
            for b in range(B):
                dve.wait_ge(r2_psum, b + 1)
                dve.tensor_scalar(bbn[:, b, :], bank[7 - b][:], scal[:, 9:10], None, ALU.mult).then_inc(bbn_ready, 1)
            for t in range(T):
                dve.wait_ge(xat_done, t + 1)
                dve.tensor_scalar(stat[:, t, 11:12], bank[7 - t % 2][:, 0:1], scal[:, 10:11], scal[:, 11:12],
                                  ALU.mult, ALU.add).then_inc(rowb_ready, 1)
                dve.wait_ge(u_ready, t + 1)
                dve.wait_ge(xb_ready, t + 1)
                ins = dve.tensor_tensor(yb[:, t % 2, :], yb[:, t % 2, :], xb[:, t % 2, :], ALU.add)
                ins.then_inc(xb_used, 1)
                dve.wait_ge(xb_used, t + 1)
                layer_norm(T + t, yb[:, t % 2, :], xr[:, t, :])

            dve.wait_ge(d_asg, 16)
            dve.wait_ge(d_fb, 16)
            dve.tensor_scalar(onehot[:], asgi[:], cst[0:NCL, K_IDX:K_IDX + 1], None, ALU.is_equal)\
                .then_inc(onehot_ready, 1)

            def cluster_hits(t):
                dve.wait_ge(lg_exp, t + 1)
                link(dve.reciprocal(f2[:, t, 2:3], f2[:, t, 1:2]))
                link(dve.tensor_scalar(hits[:, t, :], prob[:, t, :], f2[:, t, 2:3], HIT, ALU.mult, ALU.is_gt))
                dve.tensor_reduce(f2[:, t, 3:4], hits[:, t, :], AX_X, ALU.max).then_inc(hits_ready, 1)

            for t in range(T):
                xt_low_parts(T + t)
                if t >= 1:
                    dve.wait_ge(lg_psum, t)
                    link(dve.tensor_reduce(f2[:, t - 1, 0:1], bank[6 + (t - 1) % 2][:, 0:NCL], AX_X, ALU.max, negate=True))
                    dve.tensor_scalar(f2[:, t - 1, 0:1], f2[:, t - 1, 0:1], INV_TEMP, None, ALU.mult).then_inc(lg_max, 1)
                    dve.wait_ge(gemm_done, T + t)
                    dve.tensor_tensor(d1[:, t - 1, :], bank[2 + t - 1][:], fb[:], ALU.add).then_inc(vchain, 1)
                    chain[0] += 1
                    cluster_hits(t - 1)
            dve.wait_ge(lg_psum, T)
            link(dve.tensor_reduce(f2[:, T - 1, 0:1], bank[6 + (T - 1) % 2][:, 0:NCL], AX_X, ALU.max, negate=True))
            dve.tensor_scalar(f2[:, T - 1, 0:1], f2[:, T - 1, 0:1], INV_TEMP, None, ALU.mult).then_inc(lg_max, 1)
            dve.wait_ge(gemm_done, 2 * T)
            dve.tensor_tensor(d1[:, T - 1, :], bank[2 + T - 1][:], fb[:], ALU.add).then_inc(vchain, 1)
            chain[0] += 1
            cluster_hits(T - 1)
            dve.wait_ge(cl_psum, 1)
            dve.tensor_scalar(csel[:], bank[7][0:NCL, 0:P], 0.0, None, ALU.is_gt).then_inc(csel_ready, 1)
            dve.wait_ge(rsel_ready, 1)
            for t in range(T):
                y = yb[:, t % 2, :]
                link(dve.scalar_tensor_tensor(y, d1[:, t, :], f2[:, t, 3:4], rsel[:], ALU.mult, ALU.mult))
                link(dve.tensor_tensor(y, y, xr[:, t, :], ALU.add))
                layer_norm(2 * T + t, y, xr[:, t, :])
            dve.wait_ge(d_ba, 16)
            dve.wait_ge(v_low, 0)
            link(dve.tensor_scalar(bab[:, 0:D], bab[:, 0:D], 1.0 / D1, None, ALU.mult))
            dve.wait_ge(d_nw, 16)
            link(dve.tensor_tensor(wqk, nwt[:, 0:1], nwt[:, 1:2], ALU.mult))
            dve.tensor_scalar(wqk, wqk, HD ** -0.5, None, ALU.mult).then_inc(nw_ready, 1)
            xt_low_parts(2 * T)
            xt_low_parts(2 * T + 1)
            for t in range(T):
                at_bank = 2 + 3 * (t % 2)
                dve.wait_ge(qkv_done, 3 * t + 1)
                by_pair = "p (a k) -> p a k"
                dve.scalar_tensor_tensor(qr[:, :, t, :], bank[at_bank][:].rearrange(by_pair, a=PAIRS), 1.0 / D1,
                                         bab[:, 0:D].rearrange(by_pair, a=PAIRS), ALU.mult, ALU.add)\
                    .then_inc(qkv_out, 1)
                dve.wait_ge(qkv_done, 3 * t + 2)
                dve.tensor_tensor(kr[:, :, t, :], bank[at_bank + 1][:].rearrange(by_pair, a=PAIRS),
                                  bab[:, D:2 * D].rearrange(by_pair, a=PAIRS), ALU.add).then_inc(qkv_out, 1)
                dve.wait_ge(qkv_done, 3 * t + 3)
                if t:
                    dve.wait_ge(v_rest, t)
                dve.tensor_tensor(yb[:, 0, :], bank[at_bank + 2][:], bab[:, 2 * D:3 * D], ALU.add)\
                    .then_inc(qkv_out, 1)
                if t + 2 < T:
                    xt_low_parts(2 * T + t + 2)
                part = v3[:, t * H1 * 3 * D1:(t + 1) * H1 * 3 * D1].rearrange("p (h k d) -> p h k d", k=3, d=D1)
                dve.wait_ge(v_high, t + 1)
                if t:
                    dve.wait_ge(v_low, t)
                dve.tensor_tensor(yb[:, 1, :].rearrange("p (h d) -> p h d", d=D1),
                                  yb[:, 0, :].rearrange("p (h d) -> p h d", d=D1), part[:, :, 0, :], ALU.subtract)\
                    .then_inc(v_rest, 1)

            dve.wait_ge(v_low, T)
            dve.wait_ge(consts, 4)
            def two_parts(i, u):
                dve.wait_ge(ex_done, i * 16 + 2 * u + 2)
                if not (isinstance(i, int) and i * 8 + u < 2):
                    dve.wait_ge(pt_psum, i * 8 + (u - 1))
                r = rowp[:, u % 2, :]
                dve.tensor_scalar(phl[:, u % 2, 0, :], r, PSCALE, None, ALU.mult).then_inc(ph_high, 1)
                dve.wait_ge(ph_high, i * 8 + u + 1)
                dve.scalar_tensor_tensor(phl[:, u % 2, 1, :], r, PSCALE, phl[:, u % 2, 0, :], ALU.mult,
                                         ALU.subtract).then_inc(phl_ready, 1)

            def transposed_out(i, u):
                dve.wait_ge(pt_psum, i * 8 + u + 1)
                dve.tensor_copy(ptb[:, u % 2, :], bank16f[3 + u % 2][:, 0:2 * KQ]).then_inc(pt_ready, 1)

            def rows_out(i, e):
                dve.wait_ge(pv_done, i * 8 + 4 * e + 4)
                dve.tensor_reduce(orow[:].rearrange("p (a d) -> p a d", d=D1),
                                  bank[5][:, 0:2 * T * 3 * D1].rearrange("p (a k d) -> p a d k", k=3, d=D1),
                                  AX_X, ALU.add).then_inc(o_sum, 1)
                z = zsum[:, 8 * e:8 * e + 8]
                dve.tensor_scalar(zinv, z, PSCALE, None, ALU.mult).then_inc(o_sum, 1)
                dve.wait_ge(o_sum, i * 6 + 3 * e + 2)
                dve.reciprocal(zinv, zinv).then_inc(o_sum, 1)
                dve.wait_ge(o_sum, i * 6 + 3 * e + 3)
                dve.tensor_tensor(ao[:, :, bass.ds(i * 4 * D1 + 2 * e * D1, 2 * D1)].rearrange("p t (h d) -> p t h d", d=D1),
                                  orow[:].rearrange("p (t h d) -> p t h d", h=2, d=D1),
                                  zinv.rearrange("p (t h) -> p t h", h=2).unsqueeze(3).broadcast_to([P, T, 2, D1]),
                                  ALU.mult).then_inc(o_out, 1)

            def dve_body(i, first=False):
                def maxima(u):
                    dve.wait_ge(sc_done, i * 8 + u + 1)
                    if u % 2 == 0:
                        dve.wait_ge(bias_ready, i * 4 + u // 2 + 1)
                    dve.sem_inc(dve_passed, 1)
                    for q in range(2):
                        cols = slice(0, P) if q == 0 else slice(P, KQ)
                        dve.tensor_tensor_reduce(rowp[:, u % 2, cols], bank[1 + u % 2][:, cols],
                                                 bias[:, u // 2 % 2, cols], -1.0, 3e38, ALU.add, ALU.min,
                                                 nrm[:, 2 * (u % 2) + q:2 * (u % 2) + q + 1]).then_inc(mx_done, 1)

                def key_sum(h):
                    dve.wait_ge(k_square, i * 2 + h + 1)
                    s = kss[:, 4 * h:4 * h + 4]
                    dve.tensor_reduce(s, yb[:, 1, :].rearrange("p (g d) -> p g d", d=HD), AX_X, ALU.add)\
                        .then_inc(k_add, 1)
                    dve.wait_ge(k_add, i * 2 + h + 1)
                    dve.tensor_scalar(s, s, 1.0 / HD, LN_EPS, ALU.mult, ALU.add).then_inc(k_sum, 1)

                def key_rows(h):
                    dve.wait_ge(k_power, i * 2 + h + 1)
                    if h or not first:
                        dve.wait_ge(b0_full, i * 6 + (5 if h else 2))
                    dve.tensor_tensor(yb[:, 0, :].rearrange("p (g d) -> p g d", d=HD),
                                      bank[6 + h][:].rearrange("p (g d) -> p g d", d=HD),
                                      kpw[:, 4 * h:4 * h + 4].unsqueeze(2).broadcast_to([P, 4, HD]), ALU.mult)\
                        .then_inc(k_row, 1)

                for u in range(8):
                    if u % 2 == 0:
                        dve.tensor_scalar(bias[:, u // 2 % 2, :], cst[:, K_REL:K_REL + KQ],
                                          cst[:, bass.ds(i * 4 + (K_SLOPE + u // 2), 1)], None, ALU.mult)\
                            .then_inc(bias_ready, 1)
                    if u:
                        two_parts(i, u - 1)
                    elif not first:
                        two_parts(i - 1, 7)
                    if u >= 2:
                        transposed_out(i, u - 2)
                    elif not first:
                        transposed_out(i - 1, u + 6)
                    if u == 6:
                        rows_out(i, 0)
                    if u == 2 and not first:
                        rows_out(i - 1, 1)
                    maxima(u)
                    if u in (2, 4):
                        key_sum(u // 2 - 1)
                    if u in (3, 5):
                        key_rows(u // 2 - 1)

            dve_body(0, first=True)
            with dve.Fori(0, CT // 2 - 1) as j:
                dve_body(j * 2 + 1)
                dve_body(j * 2 + 2)
            dve_body(CT - 1)
            two_parts(CT - 1, 7)
            transposed_out(CT - 1, 6)
            transposed_out(CT - 1, 7)
            rows_out(CT - 1, 1)

            dve.wait_ge(d_bp, 16)
            for t in range(T):
                dve.wait_ge(xt_high, 3 * T + t + 1)
                dve.tensor_tensor(atl[:, :, t * P:(t + 1) * P], bank[t % 2][:].rearrange("p (c q) -> p c q", c=C),
                                  ath[:, :, t * P:(t + 1) * P].bitcast(F32), ALU.subtract).then_inc(xt_ready, 1)
            for t in range(T):
                y = yb[:, t % 2, :]
                dve.wait_ge(gemm_done, 2 * T + t + 1)
                link(dve.tensor_tensor(y, bank[2 + t][:], xr[:, t, :], ALU.add))
                link(dve.tensor_tensor(y, y, bpb[:], ALU.add))
                layer_norm(3 * T + t, y, xr[:, t, :])
            dve.wait_ge(d_mk, 16)

            def query_sum(n, slot):
                dve.wait_ge(q_square, n + 1)
                s = qss[:, 4 * slot:4 * slot + 4]
                dve.tensor_reduce(s, sqj[:].rearrange("p (j d) -> p j d", d=HD), AX_X, ALU.add).then_inc(q_add, 1)
                dve.wait_ge(q_add, n + 1)
                dve.tensor_scalar(s, s, 1.0 / HD, LN_EPS, ALU.mult, ALU.add).then_inc(q_sum, 1)

            def query_rows(n, slot):
                dve.wait_ge(q_power, n + 1)
                y = yb[:, slot, :].rearrange("p (j d) -> p j d", d=HD)
                dve.tensor_tensor(y, y, qpw[:, 4 * slot:4 * slot + 4].unsqueeze(2).broadcast_to([P, J, HD]), ALU.mult)\
                    .then_inc(q_norm, 1)

            def query_low(n, t):
                dve.wait_ge(q_high, n + 1)
                at_t = (slice(None), t // 2, slice(None), slice(t % 2 * P, (t % 2 + 1) * P))
                dve.tensor_tensor(qtl[at_t], bank[6][:].rearrange("p (j q) -> p j q", j=J), qth[at_t].bitcast(F32),
                                  ALU.subtract).then_inc(q_low, 1)

            def scores_max(g, u):
                for q in range(2):
                    k = 2 * (u % 2) + q
                    dve.wait_ge(s_done, g * 16 + 2 * u + q + 1)
                    dve.sem_inc(dve_passed, 1)
                    dve.tensor_tensor_reduce(px[k][:], bank[q][:], mk[:, q, :], -1.0, 3e38, ALU.add, ALU.min,
                                             xmx[:, k:k + 1]).then_inc(s_max, 1)

            def probs_norm(g, u):
                for q in range(2):
                    k = 2 * (u % 2) + q
                    dve.wait_ge(s_exp, g * 16 + 2 * u + q + 1)
                    dve.reciprocal(xzi[:, k:k + 1], xz[:, k:k + 1]).then_inc(z_inv, 1)
                    dve.wait_ge(z_inv, g * 16 + 2 * u + q + 1)
                    dve.tensor_scalar(px[k][:], px[k][:], xzi[:, k:k + 1], None, ALU.mult).then_inc(p_norm, 1)

            def probs_low(g, u):
                for q in range(2):
                    dve.wait_ge(p_high, g * 16 + 2 * u + q + 1)
                    cols = slice(q * P, (q + 1) * P)
                    dve.tensor_tensor(ptl[:, :, cols], bank[2 + q][:].rearrange("p (k q) -> p k q", q=P),
                                      pth[:, :, cols].bitcast(F32), ALU.subtract).then_inc(p_low, 1)

            def output_low(g, u):
                dve.wait_ge(a_high, g * 8 + u + 1)
                dve.tensor_tensor(otl[:, u // 4, u % 4, :], bank[4][:, 0:S], oth[:, u // 4, u % 4, :].bitcast(F32),
                                  ALU.subtract).then_inc(a_low, 1)

            def add_projection(n, t):
                dve.wait_ge(o_done, n + 1)
                dve.tensor_tensor(xr[:, t, :], xr[:, t, :], bank[7][:], ALU.add).then_inc(o_added, 1)

            dve.wait_ge(ln_done, 4 * T)
            for t in range(T):
                xt_low_parts(4 * T + t)
            for t in range(T):
                query_sum(t, t % 2)
                query_rows(t, t % 2)
                if t:
                    query_low(t - 1, t - 1)
            query_low(T - 1, T - 1)
            scores_max(0, 0)
            probs_norm(0, 0)

            def dve_group(g, more):
                first = isinstance(g, int) and g == 0
                for u in range(8):
                    if u:
                        output_low(g, u - 1)
                    elif not first:
                        output_low(g - 1, 7)
                    if u == 1 and not first:
                        add_projection(g * T - 2, 2)
                    if u == 2 and not first:
                        add_projection(g * T - 1, 3)
                    if u == 7:
                        add_projection(g * T, 0)
                    if u == 0 and not first:
                        add_projection(g * T - 3, 1)
                    if more and u in (3, 4, 6, 7):
                        t = (3, 4, 6, 7).index(u)
                        query_rows(g * T + T + t, t % 2)
                    probs_low(g, u)
                    if u < 7:
                        scores_max(g, u + 1)
                    elif more:
                        scores_max(g + 1, 0)
                    if more and u in (2, 3, 5, 6):
                        t = (2, 3, 5, 6).index(u)
                        query_sum(g * T + T + t, t % 2)
                    if u < 7:
                        probs_norm(g, u + 1)
                    elif more:
                        probs_norm(g + 1, 0)
                    if more and u in (3, 4, 6, 7):
                        t = (3, 4, 6, 7).index(u)
                        query_low(g * T + T + t, t)

            dve_group(0, True)
            with dve.Fori(1, G - 1) as g:
                dve_group(g, True)
            dve_group(G - 1, False)
            output_low(G - 1, 7)
            for t in range(T):
                if t:
                    add_projection(T * (G - 1) + t, t)
                    dve.wait_ge(o_added, T * (G - 1) + t + 1)
                layer_norm(4 * T + t, xr[:, t, :], xr[:, t, :])
            dve.wait_ge(d_bb, 16)
            dve.wait_ge(d_br, 16)
            dve.wait_ge(ln_done, 5 * T)

            def experts(t):
                z = [zt[:, t % 2, 8 * n:8 * n + 8] for n in range(8)]
                to = bank[6 + t % 2]
                counts = cst[:, K_CNT:K_CNT + NE]
                dve.wait_ge(ra_done, t + 1)
                if t >= 2:
                    dve.wait_ge(hw_psum, t - 1)
                link(dve.tensor_tensor(z[0], to[:, 0:NE], brb[:], ALU.add))
                link(dve.max(z[1], z[0]))
                link(dve.tensor_tensor_scan(z[2], oneb[:, 0:NE], z[1], 0.0, ALU.mult, ALU.add))
                link(dve.tensor_tensor(z[3], z[1], counts, ALU.mult))
                link(dve.tensor_scalar(z[3], z[3], 1.0, None, ALU.add))
                link(dve.tensor_tensor(z[3], z[3], z[2], ALU.is_gt))
                link(dve.tensor_reduce(z[4][:, 0:1], z[3], AX_X, ALU.add))
                link(dve.tensor_scalar(z[5], counts, z[4][:, 0:1], None, ALU.is_equal))
                link(dve.tensor_tensor(z[5], z[5], z[2], ALU.mult))
                link(dve.tensor_reduce(z[4][:, 1:2], z[5], AX_X, ALU.add))
                link(dve.reciprocal(z[4][:, 2:3], z[4][:, 0:1]))
                link(dve.tensor_scalar(z[4][:, 3:4], z[4][:, 1:2], -1.0, z[4][:, 2:3], ALU.add, ALU.mult))
                link(dve.tensor_scalar(z[6], z[0], z[4][:, 3:4], 0.0, ALU.subtract, ALU.max))
                dve.tensor_tensor(hw[:, t % 2, :].rearrange("p (e r) -> p e r", r=R),
                                  to[:, NE:RA].rearrange("p (e r) -> p e r", r=R),
                                  z[6].unsqueeze(2).broadcast_to([P, NE, R]), ALU.mult).then_inc(hw_ready, 1)

            def experts_low(t):
                dve.wait_ge(hw_high, t + 1)
                dve.tensor_tensor(htl[:, t % 2, :], bank[t % 2][:, 0:P], hth[:, t % 2, :].bitcast(F32), ALU.subtract)\
                    .then_inc(hw_split, 1)

            def last_norm(t):
                y = yb[:, t % 2, :]
                dve.wait_ge(ff_done, t + 1)
                link(dve.tensor_tensor(y, bank[2 + t][:], xr[:, t, :], ALU.add))
                link(dve.tensor_tensor(y, y, bbb[:], ALU.add))
                layer_norm(5 * T + t, y, xr[:, t, :])

            xt_low_parts(5 * T)
            xt_low_parts(5 * T + 1)
            for t in range(T):
                experts(t)
                experts_low(t)
                if t + 2 < T:
                    xt_low_parts(5 * T + t + 2)
                if t:
                    last_norm(t - 1)
            last_norm(T - 1)

        @block.tensor
        def _(pe):
            pe.wait_ge(d_cst, 16)
            pe.wait_ge(mask_summed, 1)
            pe.matmul(bank[6][:, 0:C * D // BLK], cst[:, K_BLK:K_BLK + P], msum[:], start=True, stop=True)\
                .then_inc(mask_counts, 1)
            pe.wait_ge(consts, 4)

            def product(into, lh, ll, rh, rl, first, last):
                pe.matmul(into, lh, rl, start=first, stop=False)
                pe.matmul(into, ll, rh, start=False, stop=False)
                return pe.matmul(into, lh, rh, start=False, stop=last)

            def transpose_rows(n, src):
                t = n % T
                if n >= 2:
                    pe.wait_ge(xt_ready, n - 1)
                for c in range(C):
                    ins = pe.transpose(bank[t % 2][:, c * P:(c + 1) * P], src[:, c * P:(c + 1) * P], ident)
                ins.then_inc(xt_psum, 1)

            def tile_gemm(into, t, wh, wl):
                for c in range(C):
                    s = slice(t * P, (t + 1) * P)
                    ins = product(into, xth[:, c, s], xtl[:, c, s], wh[:, c], wl[:, c], c == 0, c == C - 1)
                return ins

            pe.wait_ge(d_x, 16)
            transpose_rows(0, xr[:, 0])
            transpose_rows(1, xr[:, 1])
            for t in range(T):
                pe.wait_ge(w0_split, C)
                pe.wait_ge(xt_ready, t + 1)
                tile_gemm(bank[2 + t][:], t, w0h, w0l).then_inc(gemm_done, 1)
                if t + 2 < T:
                    transpose_rows(t + 2, xr[:, t + 2])

            for b in range(B):
                pe.wait_ge(c2_ready, b + 1)
                for c in range(C):
                    ins = pe.matmul(bank[7 - b][:], oneb[:], c2[:, b * C + c, :], start=c == 0, stop=c == C - 1)
                ins.then_inc(r2_psum, 1)

            def transpose_c1(t):
                pe.wait_ge(c1_ready, t + 1)
                if t >= 2:
                    pe.wait_ge(c1t_ready, t - 1)
                else:
                    pe.wait_ge(xt_ready, T)
                for c in range(C):
                    ins = pe.transpose(bank16[t % 2][:, c * P:(c + 1) * P], c1[:, t, c * P:(c + 1) * P], idb[:])
                ins.then_inc(c1_psum, 1)

            transpose_c1(0)
            transpose_c1(1)
            for t in range(T):
                pe.wait_ge(c1t_ready, t + 1)
                for c in range(C):
                    pe.matmul(bank[2 + t][:], c1t[:, t % 2, c * P:(c + 1) * P], c2[:, t // 2 * C + c, :],
                              start=c == 0, stop=c == C - 1)
                if t < 2:
                    pe.wait_ge(bbn_ready, t + 1)
                else:
                    pe.wait_ge(rowb_ready, t - 1)
                for c in range(C):
                    ins = pe.matmul(bank[7 - t % 2][:, 0:2], c1t[:, t % 2, c * P:(c + 1) * P], oneb[:, 0:2],
                                    start=c == 0, stop=c == C - 1)
                ins.then_inc(xat_done, 1)
                if t + 2 < T:
                    transpose_c1(t + 2)

            def transpose_ln(layer, t, ln):
                pe.wait_ge(ln_done, ln * T + t + 1)
                transpose_rows(layer * T + t, xr[:, t])

            pe.wait_ge(c1t_ready, T)
            transpose_ln(1, 0, 1)
            transpose_ln(1, 1, 1)
            for t in range(T):
                pe.wait_ge(wt_split, 2)
                pe.wait_ge(xt_ready, T + t + 1)
                if t >= 2:
                    pe.wait_ge(lg_exp, t - 1)
                tile_gemm(bank[6 + t % 2][:, 0:NCL], t, cenh, cenl).then_inc(lg_psum, 1)
                tile_gemm(bank[2 + t][:], t, wfh, wfl).then_inc(gemm_done, 1)
                if t + 2 < T:
                    transpose_ln(1, t + 2, 1)
            pe.wait_ge(hits_ready, T)
            for t in range(T):
                ins = pe.matmul(bank[7][0:NCL, 0:P], hits[:, t, :], oneb[:], start=t == 0, stop=t == T - 1)
            ins.then_inc(cl_psum, 1)
            pe.wait_ge(csel_ready, 1)
            pe.wait_ge(onehot_ready, 1)
            pe.matmul(bank[6][:], csel[:], onehot[:], start=True, stop=True).then_inc(cl_psum, 1)
            transpose_ln(2, 0, 2)
            transpose_ln(2, 1, 2)
            for t in range(T):
                pe.wait_ge(xt_ready, 2 * T + t + 1)
                pe.wait_ge(wa_split, 3 * C)
                if t == 1:
                    pe.wait_ge(rsel_ready, 1)
                for k in range(3):
                    if t >= 2:
                        pe.wait_ge(qkv_out, 3 * (t - 2) + k + 1)
                    cols = slice(k * D, (k + 1) * D)
                    tile_gemm(bank[2 + 3 * (t % 2) + k][:], t, wah[:, :, cols], wal[:, :, cols]).then_inc(qkv_done, 1)
                if t + 2 < T:
                    transpose_ln(2, t + 2, 2)

            pe.wait_ge(qkv_out, 3 * T)
            pe.wait_ge(xt_ready, 3 * T)
            pe.wait_ge(wk_split, C)
            pe.wait_ge(wv_split, C)
            pe.wait_ge(v_low, T)
            def transpose_stack(m, n, k):
                pe.wait_ge(stacked, m * 2 + k + 1)
                if not (isinstance(n, int) and n == 0):
                    pe.wait_ge(b0_free, n)
                src = (sq, sk)[k][:].bitcast(F32).rearrange("p t h k d -> p t (h k d)")
                for t in range(T):
                    ins = pe.transpose(bank[0][:, t * P:(t + 1) * P], src[:, t, :], ident)
                ins.then_inc(b0_full, 1)

            def transpose_probs(i, u):
                pe.wait_ge(phl_ready, i * 8 + u + 1)
                if not (isinstance(i, int) and i * 8 + u < 2):
                    pe.wait_ge(pt_ready, i * 8 + (u - 1))
                for part in range(2):
                    for k in range(3):
                        ins = pe.transpose(bank16f[3 + u % 2][:, (3 * part + k) * P:(3 * part + k + 1) * P],
                                           phl[:, u % 2, part, k * P:(k + 1) * P], idh[:])
                ins.then_inc(pt_psum, 1)

            def probs_values(i, u):
                e, hd, b = u // 4, u // 2 % 2, u % 2
                pe.wait_ge(pt_ready, i * 8 + u + 1)
                if u % 4 == 0 and not (isinstance(i, int) and i * 8 + u == 0):
                    pe.wait_ge(o_out, i * 2 + e)
                for q in range(2):
                    a = (2 * b + q) * 2 + hd
                    blocks = [(0, 0)] if q == 0 else [(1, 0), (2, 1)]
                    steps = [(part, k, kt_) for k, kt_ in blocks for part in range(2)]
                    for n, (part, k, kt_) in enumerate(steps):
                        at_v = (2 * b + kt_) * H1 * 3 * D1 + (2 * e + hd) * 3 * D1
                        ins = pe.matmul(bank[5][:, a * 3 * D1:(a + 1) * 3 * D1],
                                        ptb[:, u % 2, (3 * part + k) * P:(3 * part + k + 1) * P],
                                        v3[:, bass.ds(i * (4 * 3 * D1) + at_v, 3 * D1)],
                                        start=n == 0, stop=n == len(steps) - 1)
                ins.then_inc(pv_done, 1)

            def pe_body(i, odd, first=False, last=False):
                def scores(u):
                    e, hd, b = u // 4, u // 2 % 2, u % 2
                    d = slice(4 * D1 * hd, 4 * D1 * (hd + 1))
                    to = bank[1 + u % 2]
                    if u % 4 == 0:
                        pe.wait_ge(b0_free, i * 6 + 4 if e else 2 if first else i * 6 + 1)
                    if not (first and u < 2):
                        pe.wait_ge(mx_done, i * 16 + (2 * u - 2))
                    pe.matmul(to[:, 0:P], qt[e][d, b * S:b * S + P], kt[e][d, b * S:b * S + P], start=True, stop=True)
                    pe.matmul(to[:, P:KQ], qt[e][d, b * S + P:b * S + S], kt[e][d, b * S:b * S + S],
                              start=True, stop=True).then_inc(sc_done, 1)

                def context_half(n, cs):
                    h = n % 2
                    wh, wl = ((wkh, wkl), (wvh, wvl))[n // 2]
                    if cs[0] == 0:
                        if n == 0:
                            pe.wait_ge(ctx_split, i + 1)
                        if n >= 2:
                            pe.wait_ge(k_row, i * 2 + h + 1)
                        elif not first:
                            pe.wait_ge(v_out, i * 2 - 1 + h)
                    for c in cs:
                        cols = slice(h * D, (h + 1) * D)
                        ins = product(bank[6 + h][:], cth[odd][:, c, :], ctl[odd][:, c, :], wh[:, c, cols],
                                      wl[:, c, cols], c == 0, c == C - 1)
                    if cs[-1] == C - 1:
                        ins.then_inc(kv_done, 1)

                def transpose_keys(h):
                    pe.wait_ge(k_row, i * 2 + h + 1)
                    pe.wait_ge(b0_free, i * 6 + (4 if h == 0 else 5 if last else 7))
                    for g in range(4):
                        ins = pe.transpose(bank[0][:, g * P:(g + 1) * P], yb[:, 0, g * P:(g + 1) * P], ident)
                    ins.then_inc(b0_full, 1)

                for u in range(8):
                    if u >= 2:
                        transpose_probs(i, u - 2)
                    elif not first:
                        transpose_probs(i - 1, u + 6)
                    scores(u)
                    context_half(u // 2, (2, 3) if u % 2 else (0, 1))
                    if u >= 2:
                        probs_values(i, u - 2)
                    elif not first:
                        probs_values(i - 1, u + 6)
                    if u < 2:
                        transpose_stack(i * 2 + 1, i * 6 + 2 + u, u)
                    if u == 4:
                        transpose_keys(0)
                    if u in (5, 6) and not last:
                        transpose_stack(i * 2 + 2, i * 6 + u, u - 5)
                    if u == 7:
                        transpose_keys(1)

            transpose_stack(0, 0, 0)
            transpose_stack(0, 1, 1)
            pe_body(0, 0, first=True)
            with pe.Fori(0, CT // 2 - 1) as j:
                pe_body(j * 2 + 1, 1)
                pe_body(j * 2 + 2, 0)
            pe_body(CT - 1, 1, last=True)
            for u in (6, 7):
                transpose_probs(CT - 1, u)
            for u in (6, 7):
                probs_values(CT - 1, u)

            def transpose_ao(t):
                if t == 0:
                    pe.wait_ge(o_out, PAIRS)
                    pe.wait_ge(b0_free, 6 * CT)
                if t >= 2:
                    pe.wait_ge(xt_ready, 3 * T + t - 1)
                for c in range(C):
                    ins = pe.transpose(bank[t % 2][:, c * P:(c + 1) * P], ao[:, t, c * P:(c + 1) * P], ident)
                ins.then_inc(xt_psum, 1)

            transpose_ao(0)
            transpose_ao(1)
            pe.wait_ge(wp_split, 1)
            pe.wait_ge(v_out, 2 * CT)
            for t in range(T):
                pe.wait_ge(xt_ready, 3 * T + t + 1)
                for c in range(C):
                    s = slice(t * P, (t + 1) * P)
                    ins = product(bank[2 + t][:], ath[:, c, s], atl[:, c, s], wph[:, c], wpl[:, c], c == 0, c == C - 1)
                ins.then_inc(gemm_done, 1)
                if t + 2 < T:
                    transpose_ao(t + 2)
            def query_chunk(n, t, cs, g):
                if cs[0] == 0:
                    pe.wait_ge(wq_split, g * C + C)
                    if not (isinstance(n, int) and n == 0):
                        pe.wait_ge(q_raw, n)
                s = slice(t * P, (t + 1) * P)
                for c in cs:
                    ins = product(bank[5][:], xth[:, c, s], xtl[:, c, s], wqh[:, c], wql[:, c], c == 0, c == C - 1)
                if cs[-1] == C - 1:
                    ins.then_inc(q_done, 1)

            def transpose_queries(n, slot):
                pe.wait_ge(q_norm, n + 1)
                if not (isinstance(n, int) and n == 0):
                    pe.wait_ge(q_low, n)
                for j in range(J):
                    ins = pe.transpose(bank[6][:, j * P:(j + 1) * P], yb[:, slot, j * P:(j + 1) * P], ident)
                ins.then_inc(q_psum, 1)

            def unit_scores(g, u):
                b, j = u // 4, u % 4
                first = isinstance(g, int) and g == 0 and u == 0
                pe.wait_ge(kx_split, g * 2 + b + 1)
                pe.wait_ge(q_low, g * T + 2 * b + 2)
                for q in range(2):
                    if not first:
                        pe.wait_ge(s_max, g * 16 + 2 * u + q - 1)
                    cols = slice(q * P, (q + 1) * P)
                    product(bank[q][:], qth[:, b, j, cols], qtl[:, b, j, cols], kh[:, b, :], kl[:, b, :], True, True)\
                        .then_inc(s_done, 1)

            def transpose_unit(g, u):
                first = isinstance(g, int) and g == 0 and u == 0
                for q in range(2):
                    k = 2 * (u % 2) + q
                    pe.wait_ge(p_norm, g * 16 + 2 * u + q + 1)
                    if not first:
                        pe.wait_ge(p_low, g * 16 + 2 * u + q - 1)
                    for n in range(S2 // P):
                        ins = pe.transpose(bank[2 + q][:, n * P:(n + 1) * P], px[k][:, n * P:(n + 1) * P], ident)
                    ins.then_inc(p_psum, 1)

            def unit_output(g, u):
                b = u // 4
                pe.wait_ge(vx_split, g * 2 + b + 1)
                pe.wait_ge(p_low, g * 16 + 2 * u + 2)
                if not (isinstance(g, int) and g == 0 and u == 0):
                    pe.wait_ge(a_low, g * 8 + u)
                for n in range(S2 // P):
                    ins = product(bank[4][:, 0:S], vh[:, b, n, :], vl[:, b, n, :], pth[:, n, :], ptl[:, n, :],
                                  n == 0, n == S2 // P - 1)
                ins.then_inc(a_done, 1)

            def project(n, t, g):
                pe.wait_ge(wo_split, g * J + J)
                pe.wait_ge(a_low, g * 8 + 4 * (t // 2) + 4)
                if not (isinstance(n, int) and n == 0):
                    pe.wait_ge(o_added, n)
                cols = slice(t % 2 * P, (t % 2 + 1) * P)
                for j in range(J):
                    ins = product(bank[7][:], oth[:, t // 2, j, cols], otl[:, t // 2, j, cols], woh[:, j], wol[:, j],
                                  j == 0, j == J - 1)
                ins.then_inc(o_done, 1)

            pe.wait_ge(ln_done, 4 * T)
            for t in range(T):
                transpose_ln(4, t, 3)
            pe.wait_ge(xt_ready, 5 * T)
            for t in range(T):
                query_chunk(t, t, (0, 1, 2, 3), 0)
                if t:
                    transpose_queries(t - 1, (t - 1) % 2)
            transpose_queries(T - 1, (T - 1) % 2)
            unit_scores(0, 0)

            def pe_group(g, more):
                first = isinstance(g, int) and g == 0
                for u in range(8):
                    transpose_unit(g, u)
                    if u < 7:
                        unit_scores(g, u + 1)
                    elif more:
                        unit_scores(g + 1, 0)
                    if more and u < 6:
                        t, cs = ((0, (0, 1)), (0, (2, 3)), (1, (0, 1, 2, 3)),
                                 (2, (0, 1)), (2, (2, 3)), (3, (0, 1, 2, 3)))[u]
                        query_chunk(g * T + T + t, t, cs, g + 1)
                    if u < 2 and not first:
                        project(g * T - 2 + u, 2 + u, g - 1)
                    if u >= 6:
                        project(g * T + u - 6, u - 6, g)
                    if more and u in (3, 4, 6, 7):
                        t = (3, 4, 6, 7).index(u)
                        transpose_queries(g * T + T + t, t % 2)
                    unit_output(g, u)

            pe_group(0, True)
            with pe.Fori(1, G - 1) as g:
                pe_group(g, True)
            pe_group(G - 1, False)
            for t in (2, 3):
                project(T * (G - 1) + t, t, G - 1)
            pe.wait_ge(s_max, 16 * G)
            pe.wait_ge(p_low, 16 * G)
            pe.wait_ge(a_low, 8 * G)
            pe.wait_ge(o_added, T * G)

            def experts_in(t):
                pe.wait_ge(f_split, 2)
                pe.wait_ge(xt_ready, 5 * T + t + 1)
                if t >= 2:
                    pe.wait_ge(hw_ready, t - 1)
                tile_gemm(bank[6 + t % 2][:, 0:RA], t, rah, ral).then_inc(ra_done, 1)

            def base_product(t):
                for c in range(C):
                    s = slice(t * P, (t + 1) * P)
                    product(bank[2 + t][:], xth[:, c, s], xtl[:, c, s], wbh[:, c], wbl[:, c], c == 0, False)

            def experts_out(t):
                pe.wait_ge(hw_ready, t + 1)
                pe.wait_ge(xt_ready, 5 * T + min(t + 1 if t < 2 else t + 1, T))
                pe.transpose(bank[t % 2][:, 0:P], hw[:, t % 2, :], ident).then_inc(hw_psum, 1)
                pe.wait_ge(hw_split, t + 1)
                pe.wait_ge(f_split, 3)
                product(bank[2 + t][:], hth[:, t % 2, :], htl[:, t % 2, :], lbh[:], lbl[:], False, True)\
                    .then_inc(ff_done, 1)

            transpose_ln(5, 0, 4)
            transpose_ln(5, 1, 4)
            experts_in(0)
            base_product(0)
            for t in range(T):
                if t + 1 < T:
                    experts_in(t + 1)
                experts_out(t)
                if t + 1 < T:
                    base_product(t + 1)
                if t + 2 < T:
                    transpose_ln(5, t + 2, 4)


def _constants():
    import numpy as np
    c = np.zeros((P, K_ALL), np.float32)
    c[:, K_ID:K_ID + P] = np.eye(P)
    c[:, K_BLK:K_BLK + P] = np.kron(np.eye(P // BLK), np.ones((BLK, BLK)))
    q, k = np.arange(P)[:, None], np.arange(S)[None, :]
    for at, rows, keys in ((0, q, k[:, :P]), (P, q + P, k)):
        rel = (keys - rows).astype(np.float32)
        c[:, K_REL + at:K_REL + at + keys.shape[1]] = np.where(rel <= 0, rel, np.float32(-1e34))
    base = 2.0 ** (-2.0 ** (-(math.log2(H1) - 3)))
    c[:, K_SLOPE:K_SLOPE + H1] = (base ** np.arange(1, H1 + 1, dtype=np.float32)).astype(np.float32)
    c[:, K_IDX] = np.arange(P)
    c[:, K_CNT:K_CNT + NE] = np.arange(1, NE + 1)
    return c


def _layout(a):
    import numpy as np
    n = {k: np.asarray(v) for k, v in a.items()}
    rows = np.ascontiguousarray
    return {
        "x": n["x"].reshape(B * S, D),
        "ctx": n["ctx_4096"].reshape(B * S2, D),
        "ctxT": rows(n["ctx_4096"].reshape(B * S2, D).T),
        "amask": n["mask_1x1xSxS2_ff0"].reshape(S, S2),
        "w0T": rows(n["L0_attn_weight"].T),
        "m0T": rows(n["L0_attn_mask"].T),
        "qs": np.concatenate([n["L0_xattn_" + k] for k in ("x1_scale", "x1_zp", "x2_scale", "x2_zp")]),
        "wfT": rows(n["L0_ffn_weight"].T),
        "fbias": n["L0_ffn_bias"],
        "centT": rows(n["L0_ffn_centroids"].T),
        "asg": n["L0_ffn_assignments"],
        "waT": n["L1_attn_w_attn"],
        "ba": n["L1_attn_b_attn"],
        "wpT": n["L1_attn_w_proj"],
        "bp": n["L1_attn_b_proj"],
        "wqT": rows(n["L1_xattn_q_proj_w"].T),
        "wkT": rows(n["L1_xattn_k_proj_w"].T),
        "wvT": rows(n["L1_xattn_v_proj_w"].T),
        "woT": rows(n["L1_xattn_o_proj_w"].T),
        "nw": np.stack([n["L1_xattn_q_norm_w"], n["L1_xattn_k_norm_w"]], 1),
        "wbT": rows(n["L1_ffn_W_base"].T),
        "bb": n["L1_ffn_b_base"],
        "raT": rows(np.concatenate([n["L1_ffn_W_router"].T,
                                    n["L1_ffn_lora_A"].transpose(1, 0, 2).reshape(D, NE * R)], 1)),
        "br": n["L1_ffn_b_router"],
        "lb": n["L1_ffn_lora_B"].reshape(NE * R, D),
        "const": _constants(),
    }


def kernel(**inputs):
    import numpy as _np
    import concourse.bacc as _bacc
    from concourse import mybir as _mybir
    from concourse.bass_utils import run_bass_kernel_spmd as _run

    nc = _bacc.Bacc("TRN2", target_bir_lowering=False, num_devices=1)
    arrays, args = {}, []
    for name, a in _layout(inputs).items():
        a = _np.ascontiguousarray(a)
        arrays[f"in_{name}"] = a
        args.append(nc.dram_tensor(f"in_{name}", a.shape, _mybir.dt.from_np(a.dtype), kind="ExternalInput").ap())
    args.append(nc.dram_tensor("out", (B * S, D), F32, kind="ExternalOutput").ap())
    decoder_kernel(nc, *args)
    r = _run(nc, [arrays], core_ids=[0])
    return r.results[0]["out"].reshape(B, S, D)
```

```python
import math
from contextlib import ExitStack

import concourse.bass as bass
from concourse import mybir

F32 = mybir.dt.float32
F32R = mybir.dt.float32r
BF16 = mybir.dt.bfloat16
F16 = mybir.dt.float16
I32 = mybir.dt.int32
ALU = mybir.AluOpType
ACT = mybir.ActivationFunctionType
AX_X = mybir.AxisListType.X

P = 128
B, S, S2, D = 2, 256, 512, 512
T = B * S // P
C = D // P
CT = B * S2 // P
LN_EPS = 1e-5
QMAX = 255.0
MID = 128.0
ROUND = 12582912.0
BLK = 32
NCL = 64
HIT = 0.01
INV_TEMP = 10.0
H1, D1 = 32, 16
PAIRS = H1 // 2
KQ = 384
PSCALE = 32768.0
G, J, HD = 8, 4, 128
NE, R = 8, 16
RA = NE + NE * R

K_ID, K_BLK, K_REL, K_SLOPE, K_IDX, K_CNT = 0, 128, 256, 640, 672, 673
K_ALL = K_CNT + NE


def decoder_kernel(nc, x, ctx, ctxT, amask, w0T, m0T, qs, wfT, fbias, centT, asg,
                   waT, ba, wpT, bp, wqT, wkT, wvT, woT, nw, wbT, bb, raT, br, lb, const, out):
    with ExitStack() as st:
        cursor = [nc.sbuf_base + (-nc.sbuf_base) % 32]

        def at(name, shape, dt, offset):
            return nc.alloc_sbuf_tensor_at(name, shape, dt, offset=offset)

        def size(shape, dt):
            n = {F32: 4, F32R: 4, I32: 4, BF16: 2, F16: 2}[dt]
            for s in shape[1:]:
                n *= s
            return n + (-n) % 32

        class Region:

            def __init__(self, start, room):
                self.at, self.end = start, start + room

            def __call__(self, name, shape, dt):
                t = at(name, shape, dt, self.at)
                self.at += size(shape, dt)
                assert self.at <= self.end, (name, self.at, self.end)
                return t

        def sem(name):
            return st.enter_context(nc.semaphore(name))

        base, room = cursor[0], nc.sbuf_usable_end - cursor[0]
        KEEP, R1 = 28960, 65536
        keep = Region(base, KEEP)
        r1 = Region(base + KEEP, R1)
        R2AT = base + KEEP + R1
        R3AT = R2AT + 65536

        xr = keep("xr", [P, T, D], F32)
        xth = keep("xth", [P, C, T * P], F32R)
        XTL_AT = keep.at
        xtl = keep("xtl", [P, C, T * P], F32R)
        cst = keep("cst", [P, K_ALL], F32)
        idh = keep("idh", [P, P], F16)
        idb = keep("idb", [P, P], BF16)
        oneb = keep("oneb", [P, P], BF16)
        stat = keep("stat", [P, T, 16], F32)
        scal = keep("scal", [P, 16], F32)
        half = keep("half", [P, 8], F32)
        small = keep("small", [P, 64], F32)
        ident = cst[:, K_ID:K_ID + P]

        w0l = r1("w0l", [P, C, D], F32R)
        w0h = r1("w0h", [P, C, D], F32R)
        wal = r1("wal", [P, C, 3 * D], F32R)
        wah = r1("wah", [P, C, 3 * D], F32R)
        w0raw = at("w0raw", [P, C, D], F32, base + KEEP)
        waraw = at("waraw", [P, C, 3 * D], F32, base + KEEP + 2 * 8192)

        a2 = Region(R2AT, 65536)
        m0 = a2("m0", [P, C, D], I32)
        ctxn = a2("ctxn", [P, CT, D], F32)
        c2 = a2("c2", [P, CT, D], BF16)
        CENT_AT = a2.at
        cenl = a2("cenl", [P, C, NCL], F32R)
        cenh = a2("cenh", [P, C, NCL], F32R)
        cenraw = at("cenraw", [P, C, NCL], F32, CENT_AT)
        asgi = a2("asgi", [NCL, D], I32)
        onehot = a2("onehot", [NCL, D], BF16)
        fb = a2("fb", [P, D], F32)
        bbn = a2("bbn", [P, B, D], F32)
        xb2 = a2("xb2", [P, 2, D], F32)
        xb = [xb2[:, 0, :], xb2[:, 1, :]] + [at(f"xb{n}", [P, D], F32, R2AT + n * D * 4)[:] for n in (2, 3)]
        c1f = at("c1f", [P, 2, D], F32, R2AT)
        c1 = a2("c1", [P, T, D], BF16)
        c1t = a2("c1t", [P, 2, D], BF16)
        d1 = a2("d1", [P, T, D], F32)
        msum = a2("msum", [P, C * D // BLK], F32)
        mkeep = a2("mkeep", [P, C * D // BLK], F32)

        a3 = Region(R3AT, base + room - R3AT)
        yb = a3("yb", [P, 2, D], F32)
        WF_AT = a3.at
        wfl = a3("wfl", [P, C, D], F32R)
        wfh = a3("wfh", [P, C, D], F32R)
        wfraw = at("wfraw", [P, C, D], F32, WF_AT)
        rsel = a3("rsel", [P, D], F32)

        b2 = Region(R2AT, 65536)
        wkl = b2("wkl", [P, C, G * HD], F32R)
        wkh = b2("wkh", [P, C, G * HD], F32R)
        wvl = b2("wvl", [P, C, G * HD], F32R)
        wvh = b2("wvh", [P, C, G * HD], F32R)
        wkraw = at("wkraw", [P, C, G * HD], F32, R2AT)
        wvraw = at("wvraw", [P, C, G * HD], F32, R2AT + 32768)
        kf = at("kf", [P, G, B * S2], F32, base + KEEP)
        vf = at("vf", [P, CT, G * HD], F32, base + KEEP + 32768)
        b3 = Region(R3AT + size([P, 2, D], F32), base + room - R3AT - size([P, 2, D], F32))
        QR_AT = b3.at
        qr = b3("qr", [P, PAIRS, T, 2 * D1], F32)
        kr = b3("kr", [P, PAIRS, T, 2 * D1], F32)
        v3 = b3("v3", [P, T * H1 * 3 * D1], BF16)
        BA_AT = b3.at
        rowp = b3("rowp", [P, 2, KQ], F32)
        bias = b3("bias", [P, 2, KQ], F32)
        phl = b3("phl", [P, 2, 2, KQ], F16)
        ptb = b3("ptb", [P, 2, 2 * KQ], F16)
        CT_AT = b3.at
        ctl = [b3(f"ctl{n}", [P, C, P], F32R)[:] for n in range(2)]
        ctr = [at(f"ctr{n}", [P, C, P], F32, CT_AT + n * C * P * 4)[:] for n in range(2)]
        cth = [b3("cth0", [P, C, P], F32R)[:],
               at("cth1", [P, C, B * S2], F32R, base + KEEP + 16384)[:, :, (CT - 1) * P:]]
        nrm = b3("nrm", [P, 64], F32)
        bab = at("bab", [P, 3 * D], F32, BA_AT)
        ao = at("ao", [P, T, D], F32, XTL_AT)
        x1 = Region(XTL_AT - 8192, 8192)
        sq = x1("sq", [P, T, 2, 4, D1], F32R)
        sk = x1("sk", [P, T, 2, 4, D1], F32R)
        qt = [x1("qt0", [P, T * P], F32R), at("qt1", [P, T * P], F32R, base + KEEP + 65536 - 4096)]
        kt = [x1("kt0", [P, T * P], F32R), at("kt1", [P, T * P], F32R, base + KEEP + 65536 - 2048)]
        zsum, zinv = nrm[:, 8:24], nrm[:, 24:32]
        kss, kpw, wqk = nrm[:, 32:40], nrm[:, 40:48], nrm[:, 48:49]
        nwt = nrm[:, 50:52]
        orow = b3("orow", [P, T * 2 * D1], F32)
        wpl = at("wpl", [P, C, D], F32R, QR_AT)
        wph = at("wph", [P, C, D], F32R, QR_AT + 8192)
        wpraw = at("wpraw", [P, C, D], F32, QR_AT)
        ath = at("ath", [P, C, T * P], F32R, R2AT)
        atl = at("atl", [P, C, T * P], F32R, R2AT + 8192)
        x2 = Region(R2AT, 65536)
        woh = x2("woh", [P, J, D], F32R)
        wol = x2("wol", [P, J, D], F32R)
        STG_AT = x2.at
        stg = x2("stg", [P, C, D], F32)
        WQ_AT = x2.at
        wqh = x2("wqh", [P, C, D], F32R)
        wql = x2("wql", [P, C, D], F32R)
        kh = x2("kh", [P, B, S2], F32R)
        kl = x2("kl", [P, B, S2], F32R)
        vh = x2("vh", [P, B, S2 // P, HD], F32R)
        vl = x2("vl", [P, B, S2 // P, HD], F32R)
        mk = x2("mk", [P, S // P, S2], F32)
        sqj = x2("sqj", [P, D], F32)
        px3 = x2("px3", [P, S2], F32)
        x3 = Region(QR_AT, base + room - QR_AT)
        QT_AT = x3.at
        qth = x3("qth", [P, B, J, S], F32R)
        qtl = x3("qtl", [P, B, J, S], F32R)
        bpb = at("bpb", [P, D], F32, x3.at)
        oth = x3("oth", [P, B, J, S], F32R)
        otl = x3("otl", [P, B, J, S], F32R)
        pth = x3("pth", [P, S2 // P, S], F32R)
        ptl = x3("ptl", [P, S2 // P, S], F32R)
        px = [x3(f"px{n}", [P, S2], F32) for n in range(3)] + [px3]
        xmx, xz, xzi = small[:, 0:4], small[:, 4:8], small[:, 8:12]
        qss, qpw = small[:, 16:24], small[:, 24:32]
        wbh = at("wbh", [P, C, D], F32R, WQ_AT)
        wbl = at("wbl", [P, C, D], F32R, WQ_AT + 8192)
        wbraw = at("wbraw", [P, C, D], F32, WQ_AT + 8192)
        f4 = Region(STG_AT, 8192)
        rah = f4("rah", [P, C, RA], F32R)
        RA_AT = f4.at
        ral = f4("ral", [P, C, RA], F32R)
        raraw = at("raraw", [P, C, RA], F32, RA_AT)
        LB_AT = f4.at
        lbl = f4("lbl", [P, D], F32R)
        lbraw = at("lbraw", [P, D], F32, LB_AT)
        lbh = at("lbh", [P, D], F32R, STG_AT - 16384)
        f5 = Region(QT_AT, 16384)
        bbb = f5("bbb", [P, D], F32)
        brb = f5("brb", [P, NE], F32)
        hw = f5("hw", [P, T, NE * R], F32)
        hth = f5("hth", [P, T, NE * R], F32R)
        htl = f5("htl", [P, T, NE * R], F32R)
        zt = f5("zt", [P, 8, T, NE], F32)
        xs = at("xs", [P, T, D], F32, QT_AT + 16384)
        f2 = a3("f2", [P, T, 4], F32)
        csel = a3("csel", [NCL, P], BF16)
        hits = a3("hits", [P, T, NCL], BF16)
        prob = a3("prob", [P, T, NCL], F32)

        bank = [st.enter_context(nc.psum_tensor(f"bank{i}", [P, 512], F32)) for i in range(8)]
        bank16 = [b[:].bitcast(BF16) for b in bank]
        bank16f = [b[:].bitcast(F16) for b in bank]

        d_w0 = [sem(f"d_w0{n}") for n in range(2)]
        d_ctx = [sem(f"d_ctx{b}") for b in range(B)]
        d_x = [sem(f"d_x{n}") for n in range(2)]
        d_cst, d_m0, d_sc, d_wf, d_cen, d_asg, d_fb = (
            sem("d_" + n) for n in "cst m0 sc wf cen asg fb".split())
        d_out = sem("d_out")
        consts = sem("consts")
        mask_summed = sem("mask_summed")
        mask_counts = sem("mask_counts")
        w0_masked = sem("w0_masked")
        w0_high = sem("w0_high")
        w0_split = sem("w0_split")
        w0_split2 = sem("w0_split2")
        xt_psum = sem("xt_psum")
        xt_high = sem("xt_high")
        xt_ready = sem("xt_ready")
        gemm_done = sem("gemm_done")
        moments = sem("moments")
        rstd = sem("rstd")
        ln_done = sem("ln_done")
        vchain = sem("vchain")
        wt_high = sem("wt_high")
        wt_split = sem("wt_split")
        c2_ready = sem("c2_ready")
        c1_ready = sem("c1_ready")
        c1_psum = sem("c1_psum")
        c1t_ready = sem("c1t_ready")
        r2_psum = sem("r2_psum")
        bbn_ready = sem("bbn_ready")
        xb_ready = sem("xb_ready")
        xat_done = sem("xat_done")
        rowb_ready = sem("rowb_ready")
        u_ready = sem("u_ready")
        xb_used = sem("xb_used")
        lg_psum = sem("lg_psum")
        lg_max = sem("lg_max")
        lg_exp = sem("lg_exp")
        hits_ready = sem("hits_ready")
        cl_psum = sem("cl_psum")
        csel_ready = sem("csel_ready")
        onehot_ready = sem("onehot_ready")
        rsel_ready = sem("rsel_ready")
        wa_high, wa_split = sem("wa_high"), sem("wa_split")
        wk_high, wk_split = sem("wk_high"), sem("wk_split")
        wv_high, wv_split = sem("wv_high"), sem("wv_split")
        wp_high, wp_split = sem("wp_high"), sem("wp_split")
        d_wa, d_ba, d_wk, d_wv, d_nw, d_wp, d_bp = (
            sem("d_" + n) for n in "wa ba wk wv nw wp bp".split())
        d_ctl = [sem(f"d_ctl{n}") for n in range(2)]
        qkv_done = sem("qkv_done")
        qkv_out = sem("qkv_out")
        v_high = sem("v_high")
        v_rest = sem("v_rest")
        v_mid = sem("v_mid")
        v_low = sem("v_low")
        dve_passed, pool_passed = sem("dve_passed"), sem("pool_passed")
        pstack = sem("pstack")
        stacked = sem("stacked")
        b0_full = sem("b0_full")
        b0_free = sem("b0_free")
        sc_done = sem("sc_done")
        mx_done = sem("mx_done")
        ex_done = sem("ex_done")
        bias_ready = sem("bias_ready")
        ph_high = sem("ph_high")
        o_sum = sem("o_sum")
        k_add = sem("k_add")
        phl_ready = sem("phl_ready")
        pt_psum = sem("pt_psum")
        pt_even = sem("pt_even")
        pt_odd = sem("pt_odd")
        pv_done = sem("pv_done")
        pv_out = sem("pv_out")
        o_out = sem("o_out")
        kv_done = sem("kv_done")
        k_square = sem("k_square")
        k_sum = sem("k_sum")
        k_power = sem("k_power")
        k_row = sem("k_row")
        v_out = sem("v_out")
        ctx_high = sem("ctx_high")
        ctx_split = sem("ctx_split")
        d_mk, d_stg, d_wb, d_ra, d_lb, d_bb, d_br = (sem("d_" + n) for n in "mk stg wb ra lb bb br".split())
        wq_high, wq_split = sem("wq_high"), sem("wq_split")
        wo_high, wo_split = sem("wo_high"), sem("wo_split")
        kx_high, kx_split = sem("kx_high"), sem("kx_split")
        vx_high, vx_split = sem("vx_high"), sem("vx_split")
        q_done = sem("q_done")
        q_raw = sem("q_raw")
        q_square = sem("q_square")
        q_add = sem("q_add")
        q_sum = sem("q_sum")
        q_power = sem("q_power")
        q_norm = sem("q_norm")
        q_psum = sem("q_psum")
        q_high = sem("q_high")
        q_low = sem("q_low")
        s_done = sem("s_done")
        s_max = sem("s_max")
        s_exp = sem("s_exp")
        z_inv = sem("z_inv")
        p_norm = sem("p_norm")
        p_psum = sem("p_psum")
        p_high = sem("p_high")
        p_low = sem("p_low")
        a_done = sem("a_done")
        a_high = sem("a_high")
        a_low = sem("a_low")
        o_done = sem("o_done")
        o_added = sem("o_added")
        f_high, f_split = sem("f_high"), sem("f_split")
        ra_done = sem("ra_done")
        hw_ready = sem("hw_ready")
        hw_psum = sem("hw_psum")
        hw_high = sem("hw_high")
        hw_split = sem("hw_split")
        ff_done = sem("ff_done")
        xs_ready = sem("xs_ready")
        nw_ready = sem("nw_ready")

        PAIRS_OF_TILES = ((0, 1), (2, 3))
        SPARE = 5
        PROJ_BANK = (2, 3, 4, 7)
        WV_CHUNKS = ((0, 1), (2,), (3,), ())

        block = st.enter_context(nc.Block())

        @block.sync
        def _(sp):
            sp.dma_start(m0[:], m0T.rearrange("(c p) n -> p c n", p=P)).then_inc(d_m0, 16)
            sp.dma_start(cst[:], const).then_inc(d_cst, 16)
            for n in range(2):
                sp.dma_start(w0raw[:, 2 * n:2 * n + 2, :], w0T.rearrange("(c p) n -> p c n", p=P)[:, 2 * n:2 * n + 2, :])\
                    .then_inc(d_w0[n], 16)
            for n in range(2):
                sp.dma_start(xr[:, 2 * n:2 * n + 2, :], x.rearrange("(t p) n -> p t n", p=P)[:, 2 * n:2 * n + 2, :])\
                    .then_inc(d_x[n], 16)
            sp.dma_start(scal[:, 0:4], qs.partition_broadcast(P)).then_inc(d_sc, 16)
            for b in range(B):
                sp.dma_start(ctxn[:, b * C:(b + 1) * C, :], ctx.rearrange("(t p) n -> p t n", p=P)[:, b * C:(b + 1) * C, :])\
                    .then_inc(d_ctx[b], 16)
            sp.dma_start(wfraw[:], wfT.rearrange("(c p) n -> p c n", p=P)).then_inc(d_wf, 16)
            sp.dma_start(cenraw[:], centT.rearrange("(c p) n -> p c n", p=P)).then_inc(d_cen, 16)
            sp.dma_start(asgi[:], asg.partition_broadcast(NCL)).then_inc(d_asg, 16)
            sp.dma_start(fb[:], fbias.partition_broadcast(P)).then_inc(d_fb, 16)
            sp.dma_start(waraw[:], waT.rearrange("(c p) n -> p c n", p=P)).then_inc(d_wa, 16)
            sp.dma_start(bab[:], ba.partition_broadcast(P)).then_inc(d_ba, 16)
            sp.dma_start(nwt, nw).then_inc(d_nw, 16)
            ctile = ctxT.rearrange("(c p) n -> p c n", p=P)
            sp.dma_start(ctr[0], ctile[:, :, 0:P]).then_inc(d_ctl[0], 16)
            sp.wait_ge(xat_done, T)
            sp.wait_ge(xb_used, T)
            sp.dma_start(wkraw[:], wkT.rearrange("(c p) n -> p c n", p=P)).then_inc(d_wk, 16)
            sp.wait_ge(ln_done, 3 * T)
            sp.wait_ge(xt_ready, 2 * T)
            sp.dma_start(wvraw[:], wvT.rearrange("(c p) n -> p c n", p=P)).then_inc(d_wv, 16)
            sp.dma_start(ctr[1], ctile[:, :, P:2 * P]).then_inc(d_ctl[1], 16)
            with sp.Fori(1, CT // 2) as j:
                for n in range(2):
                    sp.wait_ge(kv_done, j * 8 - 4 + 4 * n)
                    sp.dma_start(ctr[n], ctile[:, :, bass.ds(j * 2 * P + n * P, P)]).then_inc(d_ctl[n], 16)
            sp.wait_ge(stacked, 2 * PAIRS)
            sp.dma_start(wpraw[:], wpT.rearrange("(c p) n -> p c n", p=P)).then_inc(d_wp, 16)
            sp.wait_ge(kv_done, 4 * CT)
            wq_g = wqT.rearrange("(c p) n -> p c n", p=P)
            wo_g = woT.rearrange("(h p) n -> p h n", p=P)
            sp.dma_start(stg[:], wq_g[:, :, 0:D]).then_inc(d_stg, 16)
            sp.dma_start(bpb[:], bp.partition_broadcast(P)).then_inc(d_bp, 16)
            sp.dma_start(mk[:], amask.rearrange("(q p) n -> p q n", p=P)).then_inc(d_mk, 16)
            sp.wait_ge(wq_split, C)
            sp.dma_start(stg[:], wq_g[:, :, D:2 * D]).then_inc(d_stg, 16)

            def sp_body(g, more):
                sp.wait_ge(wq_split, g * C + 2 * C if more or isinstance(g, int) and g + 2 <= G else G * C)
                sp.dma_start(stg[:], wo_g[:, bass.ds(g * J, J), :]).then_inc(d_stg, 16)
                if more:
                    sp.wait_ge(wo_split, g * J + J)
                    sp.dma_start(stg[:], wq_g[:, :, bass.ds(g * D + 2 * D, D)]).then_inc(d_stg, 16)

            with sp.Fori(0, G - 2) as g:
                sp_body(g, True)
            sp_body(G - 2, False)
            sp.wait_ge(q_done, T * G)
            sp.dma_start(wbraw[:], wbT.rearrange("(c p) n -> p c n", p=P)).then_inc(d_wb, 16)
            sp.wait_ge(wo_split, (G - 1) * J)
            sp_body(G - 1, False)
            sp.wait_ge(wo_split, G * J)
            sp.dma_start(raraw[:], raT.rearrange("(c p) n -> p c n", p=P)).then_inc(d_ra, 16)
            sp.dma_start(lbraw[:], lb).then_inc(d_lb, 16)
            sp.wait_ge(s_done, 2 * 8 * G)
            sp.dma_start(bbb[:], bb.partition_broadcast(P)).then_inc(d_bb, 16)
            sp.dma_start(brb[:], br.partition_broadcast(P)).then_inc(d_br, 16)
            rows = out.rearrange("(t p) n -> p t n", p=P)
            for t in range(T):
                sp.wait_ge(ln_done, 5 * T + t + 1)
                sp.dma_start(rows[:, t, :], xr[:, t, :]).then_inc(d_out, 16)
            sp.wait_ge(d_out, 16 * T)

        @block.gpsimd
        def _(pool):
            pool.memset(half[:], -0.5).then_inc(consts, 1)
            pool.memset(oneb[:], 1.0).then_inc(consts, 1)
            pool.wait_ge(d_cst, 16)
            pool.tensor_copy(idh[:], ident).then_inc(consts, 1)
            pool.tensor_copy(idb[:], ident).then_inc(consts, 1)
            pool.wait_ge(consts, 4)

            def low(job, lo, raw, hi):
                pool.wait_ge(wt_high, job)
                pool.tensor_tensor(lo, raw, hi.bitcast(F32), ALU.subtract).then_inc(wt_split, 1)

            def ln_power(n):
                pool.wait_ge(moments, n + 1)
                s = stat[:, n % T, :]
                pool.tensor_tensor(s[:, 9:10], s[:, 8:9], half[:, 0:1], ALU.pow).then_inc(rstd, 1)

            for c in range(2, C):
                pool.wait_ge(w0_high, c + 1)
                pool.tensor_tensor(w0l[:, c, :], w0raw[:, c, :], w0h[:, c, :].bitcast(F32), ALU.subtract)\
                    .then_inc(w0_split2, 1)
            low(1, wfl[:, 0, :], wfraw[:, 0, :], wfh[:, 0, :])
            low(1, wfl[:, 1, :], wfraw[:, 1, :], wfh[:, 1, :])
            low(2, cenl[:], cenraw[:], cenh[:])

            def wa_low(n):
                c, q = n // 3, n % 3 * D
                pool.wait_ge(wa_high, c + 1)
                pool.tensor_tensor(wal[:, c, q:q + D], waraw[:, c, q:q + D], wah[:, c, q:q + D].bitcast(F32),
                                   ALU.subtract).then_inc(wa_split, 1)

            def context_low(i, n):
                pool.wait_ge(ctx_high, i + 1)
                pool.tensor_tensor(ctl[n], ctr[n], cth[n].bitcast(F32), ALU.subtract).then_inc(ctx_split, 1)

            for pair in PAIRS_OF_TILES:
                for t in pair:
                    ln_power(t)
                for t in pair:
                    pool.wait_ge(ln_done, t + 1)
                    pool.wait_ge(bbn_ready, t // 2 + 1)
                    if t >= 2:
                        pool.wait_ge(c1_ready, 2)
                    pool.tensor_tensor(xb[t], xr[:, t, :], bbn[:, t // 2, :], ALU.add).then_inc(xb_ready, 1)
                if pair[0] == 0:
                    low(1, wfl[:, 2, :], wfraw[:, 2, :], wfh[:, 2, :])
                    low(1, wfl[:, 3, :], wfraw[:, 3, :], wfh[:, 3, :])
            wa_low(0)
            wa_low(1)
            for pair in PAIRS_OF_TILES:
                for t in pair:
                    ln_power(T + t)
                wa_low(pair[0] + 2)
                wa_low(pair[1] + 2)
            for n in range(6, 3 * C):
                wa_low(n)
            context_low(0, 0)
            for c in range(C):
                pool.wait_ge(wk_high, c + 1)
                pool.tensor_tensor(wkl[:, c, :], wkraw[:, c, :], wkh[:, c, :].bitcast(F32), ALU.subtract)\
                    .then_inc(wk_split, 1)
            for t in range(T):
                ln_power(2 * T + t)

            def values_weights_low(c):
                pool.wait_ge(wv_high, c + 1)
                pool.tensor_tensor(wvl[:, c, :], wvraw[:, c, :], wvh[:, c, :].bitcast(F32), ALU.subtract)\
                    .then_inc(wv_split, 1)

            for t in range(T):
                part = v3[:, t * H1 * 3 * D1:(t + 1) * H1 * 3 * D1].rearrange("p (h k d) -> p h k d", k=3, d=D1)
                pool.wait_ge(v_mid, t + 1)
                pool.tensor_tensor(part[:, :, 2, :], yb[:, 1, :].rearrange("p (h d) -> p h d", d=D1),
                                   part[:, :, 1, :], ALU.subtract).then_inc(v_low, 1)
                for c in WV_CHUNKS[t]:
                    values_weights_low(c)

            pair_shape = [P, 2 * T, 2, D1]

            def stack_queries(n):
                src_q = qr[:].rearrange("p a t k -> p (a t k)")[:, bass.ds(n * P, P)]\
                    .rearrange("p (a d) -> p a d", d=D1).unsqueeze(2).broadcast_to(pair_shape)
                q4 = sq[:].rearrange("p t h k d -> p (t h) k d")
                pool.tensor_copy(q4[:, :, 0:2, :], src_q).then_inc(pstack, 1)
                pool.wait_ge(pstack, n * 2 + 1)
                pool.sem_inc(pool_passed, 1)
                pool.tensor_tensor(q4[:, :, 2:4, :], src_q, q4[:, :, 0:2, :].bitcast(F32), ALU.subtract)\
                    .then_inc(stacked, 1)

            def stack_keys(n):
                src_k = kr[:].rearrange("p a t k -> p (a t k)")[:, bass.ds(n * P, P)]\
                    .rearrange("p (a d) -> p a d", d=D1).unsqueeze(2).broadcast_to(pair_shape)
                k4 = sk[:].rearrange("p t h k d -> p (t h) k d")
                pool.tensor_copy(k4[:, :, 0:4:2, :], src_k).then_inc(pstack, 1)
                pool.wait_ge(pstack, n * 2 + 2)
                pool.sem_inc(pool_passed, 1)
                pool.tensor_tensor(k4[:, :, 1:4:2, :], src_k, k4[:, :, 0:4:2, :].bitcast(F32), ALU.subtract)\
                    .then_inc(stacked, 1)

            def stack(n):
                stack_queries(n)
                stack_keys(n)

            def key_power(i, h):
                pool.wait_ge(k_sum, i * 2 + h + 1)
                pool.tensor_tensor(kpw[:, 4 * h:4 * h + 4], kss[:, 4 * h:4 * h + 4], half[:, 0:4], ALU.pow)\
                    .then_inc(k_power, 1)

            def head_bias(m, slot):
                if not (isinstance(m, int) and m < 2):
                    pool.wait_ge(mx_done, m * 4 - 4)
                pool.tensor_tensor(bias[:, slot, :], cst[:, K_REL:K_REL + KQ],
                                   cst[:, bass.ds(m + K_SLOPE, 1)].broadcast_to([P, KQ]), ALU.mult)\
                    .then_inc(bias_ready, 1)

            def pool_body(i, odd, last=False):
                head_bias(i * 4 + 2, 0)
                if not last:
                    pool.wait_ge(b0_full, i * 6 + 4)
                    stack_queries(i * 2 + 2)
                key_power(i, 0)
                if not last:
                    stack_keys(i * 2 + 2)
                head_bias(i * 4 + 3, 1)
                if not last:
                    context_low(i + 1, 1 - odd)
                key_power(i, 1)
                if not last:
                    head_bias(i * 4 + 4, 0)
                    pool.wait_ge(b0_full, i * 6 + 7)
                    stack(i * 2 + 3)
                    head_bias(i * 4 + 5, 1)

            pool.wait_ge(qkv_out, 3 * T)
            stack(0)
            head_bias(0, 0)
            head_bias(1, 1)
            pool.wait_ge(b0_full, 2)
            stack(1)
            pool_body(0, 0)
            with pool.Fori(0, CT // 2 - 1) as j:
                pool_body(j * 2 + 1, 1)
                pool_body(j * 2 + 2, 0)
            pool_body(CT - 1, 1, last=True)
            for c in range(C):
                pool.wait_ge(wp_high, c + 1)
                pool.tensor_tensor(wpl[:, c, :], wpraw[:, c, :], wph[:, c, :].bitcast(F32), ALU.subtract)\
                    .then_inc(wp_split, 1)

            def wq_low(g, chunks=range(C)):
                for c in chunks:
                    pool.wait_ge(wq_high, g * 2 + c // 2 + 1)
                    pool.tensor_tensor(wql[:, c, :], stg[:, c, :], wqh[:, c, :].bitcast(F32), ALU.subtract)\
                        .then_inc(wq_split, 1)

            for pair in PAIRS_OF_TILES:
                wq_low(0, pair)
                for t in pair:
                    ln_power(3 * T + t)

            def wo_low(g):
                for j in range(J):
                    pool.wait_ge(wo_high, g * 2 + j // 2 + 1)
                    pool.tensor_tensor(wol[:, j, :], stg[:, j, :], woh[:, j, :].bitcast(F32), ALU.subtract)\
                        .then_inc(wo_split, 1)

            def keys_low(g, b):
                pool.wait_ge(kx_high, g * 2 + b + 1)
                pool.tensor_tensor(kl[:, b:b + 1, :], kf[:, bass.ds(g, 1), b * S2:(b + 1) * S2],
                                   kh[:, b:b + 1, :].bitcast(F32), ALU.subtract).then_inc(kx_split, 1)

            def values_low(g, b):
                pool.wait_ge(vx_high, g * 2 + b + 1)
                pool.tensor_tensor(vl[:, b], vf[:, b * C:(b + 1) * C, bass.ds(g * HD, HD)],
                                   vh[:, b].bitcast(F32), ALU.subtract).then_inc(vx_split, 1)

            def query_power(n, slot):
                pool.wait_ge(q_sum, n + 1)
                pool.tensor_tensor(qpw[:, 4 * slot:4 * slot + 4], qss[:, 4 * slot:4 * slot + 4], half[:, 0:4], ALU.pow)\
                    .then_inc(q_power, 1)

            keys_low(0, 0)
            keys_low(0, 1)
            values_low(0, 0)
            query_power(0, 0)
            values_low(0, 1)
            for t in range(1, T):
                query_power(t, t % 2)
            wq_low(1)

            def pool_group(g, more, most):
                if not (isinstance(g, int) and g == 0):
                    values_low(g, 1)
                wo_low(g)
                if more:
                    query_power(g * T + T, 0)
                    keys_low(g + 1, 0)
                    query_power(g * T + T + 1, 1)
                    values_low(g + 1, 0)
                    query_power(g * T + T + 2, 0)
                    query_power(g * T + T + 3, 1)
                if most:
                    wq_low(g + 2)
                if more:
                    keys_low(g + 1, 1)

            pool_group(0, True, True)
            with pool.Fori(1, G - 2) as g:
                pool_group(g, True, True)
            pool_group(G - 2, True, False)
            pool_group(G - 1, False, False)
            for c in range(C):
                pool.wait_ge(f_high, c + 1)
                pool.tensor_tensor(wbl[:, c, :], wbraw[:, c, :], wbh[:, c, :].bitcast(F32), ALU.subtract)\
                    .then_inc(f_split, 1)
            pool.wait_ge(f_high, C + 1)
            pool.tensor_tensor(ral[:], raraw[:], rah[:].bitcast(F32), ALU.subtract).then_inc(f_split, 1)
            for t in range(T):
                ln_power(4 * T + t)
            pool.wait_ge(f_high, C + 2)
            pool.tensor_tensor(lbl[:], lbraw[:], lbh[:].bitcast(F32), ALU.subtract).then_inc(f_split, 1)
            pool.wait_ge(d_bb, 16)
            for t in range(T):
                pool.wait_ge(ln_done, 4 * T + t + 1)
                pool.tensor_tensor(xs[:, t, :], xr[:, t, :], bbb[:], ALU.add).then_inc(xs_ready, 1)
            for t in range(T):
                ln_power(5 * T + t)

        @block.scalar
        def _(act):
            act.wait_ge(consts, 1)
            act.activation(small[:, 56:57], half[:, 0:1], ACT.Exp)
            for c in range(C):
                act.wait_ge(w0_masked, c + 1)
                act.activation(w0h[:, c, :], w0raw[:, c, :], ACT.Copy).then_inc(w0_high, 1)

            def xt_high_parts(n):
                t = n % T
                act.wait_ge(xt_psum, n + 1)
                act.activation(xth[:, :, t * P:(t + 1) * P],
                               bank[t % 2][:].rearrange("p (c q) -> p c q", c=C), ACT.Copy).then_inc(xt_high, 1)

            def high(dma, hi, raw):
                act.wait_ge(dma, 16)
                act.activation(hi, raw, ACT.Copy).then_inc(wt_high, 1)

            for t in range(T):
                xt_high_parts(t)
            high(d_wf, wfh[:], wfraw[:])
            high(d_cen, cenh[:], cenraw[:])
            def wa_high_part(c):
                act.activation(wah[:, c, :], waraw[:, c, :], ACT.Copy).then_inc(wa_high, 1)

            act.wait_ge(d_wa, 16)
            wa_high_part(0)
            for t in range(T):
                act.wait_ge(c1_psum, t + 1)
                act.activation(c1t[:, t % 2, :], bank16[t % 2][:, 0:D], ACT.Copy).then_inc(c1t_ready, 1)
                if t in (1, 2):
                    wa_high_part(t)
                if t >= 1:
                    act.wait_ge(rowb_ready, t)
                    if t >= 3:
                        act.wait_ge(ln_done, T + t - 2)
                    act.activation(yb[:, (t - 1) % 2, :], bank[2 + t - 1][:], ACT.Identity,
                                   bias=stat[:, t - 1, 11:12], scale=scal[:, 6:7]).then_inc(u_ready, 1)
            wa_high_part(3)
            act.wait_ge(rowb_ready, T)
            act.wait_ge(ln_done, T + 2)
            act.activation(yb[:, (T - 1) % 2, :], bank[2 + T - 1][:], ACT.Identity,
                           bias=stat[:, T - 1, 11:12], scale=scal[:, 6:7]).then_inc(u_ready, 1)

            def keys_weights_high(c):
                act.wait_ge(d_wk, 16)
                act.activation(wkh[:, c, :], wkraw[:, c, :], ACT.Copy).then_inc(wk_high, 1)

            def context_high(i, n, first=False):
                act.wait_ge(d_ctl[n], i * 8 + (16 - 8 * n))
                if not first:
                    act.wait_ge(kv_done, i * 4 - 4)
                act.activation(cth[n], ctr[n], ACT.Copy).then_inc(ctx_high, 1)

            context_high(0, 0, first=True)
            for t in range(T):
                xt_high_parts(T + t)
                if t >= 1:
                    act.wait_ge(lg_max, t)
                    act.activation(prob[:, t - 1, :], bank[6 + (t - 1) % 2][:, 0:NCL], ACT.Exp, scale=INV_TEMP,
                                   bias=f2[:, t - 1, 0:1], accum_out=f2[:, t - 1, 1:2]).then_inc(lg_exp, 1)
                    keys_weights_high(t - 1)
            act.wait_ge(lg_max, T)
            act.activation(prob[:, T - 1, :], bank[6 + (T - 1) % 2][:, 0:NCL], ACT.Exp, scale=INV_TEMP,
                           bias=f2[:, T - 1, 0:1], accum_out=f2[:, T - 1, 1:2]).then_inc(lg_exp, 1)
            keys_weights_high(T - 1)
            act.wait_ge(cl_psum, 2)
            act.activation(rsel[:], bank[6][:], ACT.Copy).then_inc(rsel_ready, 1)
            def value_parts(t):
                part = v3[:, t * H1 * 3 * D1:(t + 1) * H1 * 3 * D1].rearrange("p (h k d) -> p h k d", k=3, d=D1)
                act.wait_ge(qkv_out, 3 * t + 1)
                act.activation(part[:, :, 0, :], yb[:, 0, :].rearrange("p (h d) -> p h d", d=D1), ACT.Copy)\
                    .then_inc(v_high, 1)
                act.wait_ge(v_rest, t + 1)
                act.activation(part[:, :, 1, :], yb[:, 1, :].rearrange("p (h d) -> p h d", d=D1), ACT.Copy)\
                    .then_inc(v_mid, 1)

            xt_high_parts(2 * T)
            xt_high_parts(2 * T + 1)
            for t in range(T):
                if t + 2 < T:
                    xt_high_parts(2 * T + t + 2)
                value_parts(t)
                if t == 0:
                    act.wait_ge(d_wv, 16)
                for c in WV_CHUNKS[t]:
                    act.activation(wvh[:, c, :], wvraw[:, c, :], ACT.Copy).then_inc(wv_high, 1)

            act.wait_ge(nw_ready, 1)
            def copy_stack(n, k, e):
                act.wait_ge(b0_full, n + 1)
                act.activation((qt, kt)[k][e][:], bank[0][:], ACT.Copy).then_inc(b0_free, 1)

            def transposed_out(i, u):
                act.wait_ge(pt_psum, i * 8 + u + 1)
                act.activation(ptb[:, 1, :], bank16f[4][:, 0:2 * KQ], ACT.Copy).then_inc(pt_odd, 1)

            def act_body(i, odd, first=False, last=False):
                def exponentials(u):
                    e, hd, b = u // 4, u // 2 % 2, u % 2
                    for q in range(2):
                        cols = slice(0, P) if q == 0 else slice(P, KQ)
                        z = e * 8 + (2 * b + q) * 2 + hd
                        act.wait_ge(mx_done, i * 16 + 2 * u + q + 1)
                        if u % 4 == 0 and q == 0 and not first:
                            act.wait_ge(o_out, i * 2 - 1 + e)
                        r = rowp[:, u % 2, cols]
                        act.activation(r, r, ACT.Exp, scale=-1.0, bias=nrm[:, 2 * (u % 2) + q:2 * (u % 2) + q + 1],
                                       accum_out=zsum[:, z:z + 1]).then_inc(ex_done, 1)

                def key_square(h):
                    act.wait_ge(kv_done, i * 4 + h + 1)
                    if h or not first:
                        act.wait_ge(k_sum, i * 2 + h)
                    act.activation(yb[:, 1, :], bank[6 + h][:], ACT.Square).then_inc(k_square, 1)

                def keys_out(h):
                    act.wait_ge(b0_full, i * 6 + (5 if h == 0 else 6 if last else 8))
                    if last:
                        act.wait_ge(kv_done, 4 * CT)
                    act.activation(kf[:, 4 * h:4 * h + 4, bass.ds(i * P, P)],
                                   bank[0][:].rearrange("p (g k) -> p g k", g=4), ACT.Copy, scale=wqk)\
                        .then_inc(b0_free, 1)

                def values_out(h):
                    act.wait_ge(kv_done, i * 4 + 3 + h)
                    if last:
                        act.wait_ge(sc_done, 8 * CT)
                    act.activation(vf[:, bass.ds(i, 1), h * D:(h + 1) * D], bank[6 + h][:].unsqueeze(1), ACT.Copy)\
                        .then_inc(v_out, 1)

                for u in range(8):
                    if u % 2 and u > 1:
                        transposed_out(i, u - 2)
                    elif u == 1 and not first:
                        transposed_out(i - 1, 7)
                    exponentials(u)
                    if u == 0:
                        copy_stack(i * 6 + 2, 0, 1)
                    if u == 1:
                        copy_stack(i * 6 + 3, 1, 1)
                    if u in (1, 3):
                        key_square(u // 2)
                    if u == 3 and not last:
                        context_high(i + 1, 1 - odd, first)
                    if u == 4 and not last:
                        keys_out(0)
                    if u == 5 and not last:
                        copy_stack(i * 6 + 5, 0, 0)
                    if u == 5 and not last:
                        values_out(0)
                    if u == 6 and not last:
                        copy_stack(i * 6 + 6, 1, 0)
                    if u >= 4 and last:
                        act.wait_ge(d_wp, 16)
                        act.activation(wph[:, u - 4, :], wpraw[:, u - 4, :], ACT.Copy).then_inc(wp_high, 1)
                if last:
                    keys_out(0)
                    values_out(0)
                keys_out(1)
                values_out(1)

            copy_stack(0, 0, 0)
            copy_stack(1, 1, 0)
            act_body(0, 0, first=True)
            with act.Fori(0, CT // 2 - 1) as j:
                act_body(j * 2 + 1, 1)
                act_body(j * 2 + 2, 0)
            act_body(CT - 1, 1, last=True)
            transposed_out(CT - 1, 7)

            for t in range(T):
                act.wait_ge(xt_psum, 3 * T + t + 1)
                act.activation(ath[:, :, t * P:(t + 1) * P],
                               bank[t % 2][:].rearrange("p (c q) -> p c q", c=C), ACT.Copy).then_inc(xt_high, 1)
            def wq_high_parts(g, n):
                act.wait_ge(d_stg, n * 16 + 16)
                act.wait_ge(q_done, g * T)
                for h in range(2):
                    act.activation(wqh[:, 2 * h:2 * h + 2, :], stg[:, 2 * h:2 * h + 2, :], ACT.Copy).then_inc(wq_high, 1)

            def wo_high_parts(g, halves=(0, 1)):
                act.wait_ge(d_stg, 32 * G if isinstance(g, int) and g == G - 1 else g * 32 + 48)
                act.wait_ge(o_done, g * T)
                for h in halves:
                    act.activation(woh[:, 2 * h:2 * h + 2, :], stg[:, 2 * h:2 * h + 2, :], ACT.Copy).then_inc(wo_high, 1)

            def keys_high(g, b):
                if not (isinstance(g, int) and g == 0):
                    act.wait_ge(s_done, g * 16 - 8 + 8 * b)
                act.activation(kh[:, b:b + 1, :], kf[:, bass.ds(g, 1), b * S2:(b + 1) * S2], ACT.Copy)\
                    .then_inc(kx_high, 1)

            def values_high(g, b):
                if not (isinstance(g, int) and g == 0):
                    act.wait_ge(a_done, g * 8 - 4 + 4 * b)
                act.activation(vh[:, b], vf[:, b * C:(b + 1) * C, bass.ds(g * HD, HD)], ACT.Copy).then_inc(vx_high, 1)

            def query_square(n, slot):
                act.wait_ge(q_done, n + 1)
                if not (isinstance(n, int) and n < 2):
                    act.wait_ge(q_psum, n - 1)
                act.activation(yb[:, slot, :], bank[5][:], ACT.Copy).then_inc(q_raw, 1)
                act.wait_ge(q_raw, n + 1)
                if not (isinstance(n, int) and n == 0):
                    act.wait_ge(q_sum, n)
                act.activation(sqj[:], yb[:, slot, :], ACT.Square).then_inc(q_square, 1)

            def query_high(n, t):
                act.wait_ge(q_psum, n + 1)
                act.activation(qth[:, t // 2, :, t % 2 * P:(t % 2 + 1) * P],
                               bank[6][:].rearrange("p (j q) -> p j q", j=J), ACT.Copy).then_inc(q_high, 1)

            def scores_exp(g, u):
                for q in range(2):
                    k = 2 * (u % 2) + q
                    act.wait_ge(s_max, g * 16 + 2 * u + q + 1)
                    act.activation(px[k][:], px[k][:], ACT.Exp, scale=-1.0, bias=xmx[:, k:k + 1],
                                   accum_out=xz[:, k:k + 1]).then_inc(s_exp, 1)

            def probs_high(g, u):
                for q in range(2):
                    act.wait_ge(p_psum, g * 16 + 2 * u + q + 1)
                    act.activation(pth[:, :, q * P:(q + 1) * P], bank[2 + q][:].rearrange("p (k q) -> p k q", q=P),
                                   ACT.Copy).then_inc(p_high, 1)

            def output_high(g, u):
                act.wait_ge(a_done, g * 8 + u + 1)
                act.activation(oth[:, u // 4, u % 4, :], bank[4][:, 0:S], ACT.Copy).then_inc(a_high, 1)

            wq_high_parts(0, 0)
            for b in range(B):
                keys_high(0, b)
            for b in range(B):
                values_high(0, b)
            xt_high_parts(4 * T)
            xt_high_parts(4 * T + 1)
            act.wait_ge(ln_done, 4 * T)
            query_square(0, 0)
            xt_high_parts(4 * T + 2)
            query_square(1, 1)
            xt_high_parts(4 * T + 3)
            query_high(0, 0)
            query_square(2, 0)
            query_high(1, 1)
            query_square(3, 1)
            scores_exp(0, 0)
            query_high(2, 2)
            query_high(3, 3)
            wq_high_parts(1, 1)

            def act_group(g, more, most):
                first = isinstance(g, int) and g == 0
                for u in range(8):
                    if u:
                        output_high(g, u - 1)
                    elif not first:
                        output_high(g - 1, 7)
                        values_high(g, 1)
                    if not more and u == 0:
                        scores_exp(g, 1)
                    probs_high(g, u)
                    if more and u < 7:
                        scores_exp(g, u + 1)
                    elif more:
                        scores_exp(g + 1, 0)
                    elif u < 6:
                        scores_exp(g, u + 2)
                    if more and u == 2:
                        wo_high_parts(g)
                    if not more and u in (1, 2):
                        wo_high_parts(g, (u - 1,))
                    if more and 2 <= u < 6:
                        query_square(g * T + T + u - 2, u % 2)
                    if more and u == 3:
                        keys_high(g + 1, 0)
                    if more and u == 4:
                        values_high(g + 1, 0)
                    if more and u >= 4:
                        query_high(g * T + T + u - 4, u - 4)
                    if most and u == 6:
                        wq_high_parts(g + 2, g * 2 + 3)
                    if more and u == 7:
                        keys_high(g + 1, 1)
                    if not more and 3 <= u < 7:
                        act.wait_ge(d_wb, 16)
                        act.activation(wbh[:, u - 3, :], wbraw[:, u - 3, :], ACT.Copy).then_inc(f_high, 1)
                    if not more and u == 7:
                        act.wait_ge(d_ra, 16)
                        act.activation(rah[:], raraw[:], ACT.Copy).then_inc(f_high, 1)

            act_group(0, True, True)
            with act.Fori(1, G - 2) as g:
                act_group(g, True, True)
            act_group(G - 2, True, False)
            act_group(G - 1, False, False)
            output_high(G - 1, 7)
            xt_high_parts(5 * T)
            xt_high_parts(5 * T + 1)
            act.wait_ge(d_lb, 16)
            act.wait_ge(o_done, T * G)
            act.activation(lbh[:], lbraw[:], ACT.Copy).then_inc(f_high, 1)
            xt_high_parts(5 * T + 2)
            xt_high_parts(5 * T + 3)
            for n in range(2):
                act.wait_ge(hw_psum, n + 1)
                act.activation(hth[:, 2 * n:2 * n + 2, :], bank[n][:, 0:2 * P].rearrange("p (t q) -> p t q", q=P), ACT.Copy)\
                    .then_inc(hw_high, 1)

        @block.vector
        def _(dve):
            chain = [0]

            def link(ins):
                chain[0] += 1
                ins.then_inc(vchain, 1)
                dve.wait_ge(vchain, chain[0])

            def xt_low_parts(n):
                t = n % T
                dve.wait_ge(xt_high, n + 1)
                dve.tensor_tensor(xtl[:, :, t * P:(t + 1) * P], bank[t % 2][:].rearrange("p (c q) -> p c q", c=C),
                                  xth[:, :, t * P:(t + 1) * P].bitcast(F32), ALU.subtract).then_inc(xt_ready, 1)

            last = {}

            def mark(t, ins):
                chain[0] += 1
                ins.then_inc(vchain, 1)
                last[t] = chain[0]

            def until(t):
                dve.wait_ge(vchain, last[t])

            def moments_of(ts, n, y):
                for t in ts:
                    until(t)
                    mark(t, dve.bn_stats(stat[:, t, 0:6], y(t)))
                for t in ts:
                    until(t)
                    mark(t, dve.bn_aggr(stat[:, t, 6:8], stat[:, t, 0:6]))
                for t in ts:
                    until(t)
                    dve.tensor_scalar(stat[:, t, 8:9], stat[:, t, 7:8], LN_EPS, None, ALU.add).then_inc(moments, 1)

            def normalise(ts, n, y):
                for t in ts:
                    dve.wait_ge(rstd, n * T + t + 1)
                    dve.tensor_scalar(xr[:, t, :], y(t), stat[:, t, 6:7], stat[:, t, 9:10], ALU.subtract, ALU.mult)\
                        .then_inc(ln_done, 1)

            def yrow(t):
                return yb[:, t % 2, :]

            def row_free(t, n):
                if t >= 2:
                    dve.wait_ge(ln_done, n * T + t - 1)

            dve.wait_ge(d_m0, 16)
            dve.tensor_reduce(msum[:], m0[:].rearrange("p c (n k) -> p (c n) k", k=BLK), AX_X, ALU.add)\
                .then_inc(mask_summed, 1)
            dve.wait_ge(mask_counts, 1)
            link(dve.tensor_scalar(mkeep[:], bank[6][:, 0:C * D // BLK], 0.0, None, ALU.is_gt))
            kp = mkeep[:].rearrange("p (c n) -> p c n", c=C)
            for c in range(C):
                dve.wait_ge(d_w0[c // 2], 16)
                w = w0raw[:, c, :].rearrange("p (n k) -> p n k", k=BLK)
                dve.tensor_tensor(w, w, kp[:, c, :].unsqueeze(2).broadcast_to([P, D // BLK, BLK]), ALU.mult)\
                    .then_inc(w0_masked, 1)
            for c in range(2):
                dve.wait_ge(w0_high, c + 1)
                dve.tensor_tensor(w0l[:, c, :], w0raw[:, c, :], w0h[:, c, :].bitcast(F32), ALU.subtract)\
                    .then_inc(w0_split, 1)
            xt_low_parts(0)
            xt_low_parts(1)
            dve.wait_ge(d_sc, 16)
            link(dve.reciprocal(scal[:, 4:6], scal[:, 0:4:2]))
            link(dve.tensor_tensor(scal[:, 6:7], scal[:, 0:1], scal[:, 2:3], ALU.mult))
            link(dve.tensor_scalar(scal[:, 7:9], scal[:, 1:4:2], -1.0, MID, ALU.mult, ALU.add))
            link(dve.tensor_scalar(scal[:, 9:11], scal[:, 7:9], scal[:, 6:7], None, ALU.mult))
            link(dve.tensor_scalar(scal[:, 11:12], scal[:, 9:10], scal[:, 8:9], float(D), ALU.mult, ALU.mult))
            def quantise_context(b):
                dve.wait_ge(d_ctx[b], 16)
                v = ctxn[:, b * C:(b + 1) * C, :]
                link(dve.tensor_scalar(v, v, scal[:, 5:6], scal[:, 3:4], ALU.mult, ALU.add))
                link(dve.tensor_scalar(v, v, 0.0, QMAX, ALU.max, ALU.min))
                dve.tensor_scalar(c2[:, b * C:(b + 1) * C, :], v, ROUND, ROUND + MID, ALU.add, ALU.subtract)\
                    .then_inc(c2_ready, 1)

            for b in range(B):
                quantise_context(b)
                xt_low_parts(2 + b)

            def quantise(ts):
                for t in ts:
                    dve.wait_ge(ln_done, t + 1)
                    mark(t, dve.tensor_scalar(c1f[:, t % 2, :], xr[:, t, :], scal[:, 4:5], scal[:, 1:2], ALU.mult, ALU.add))
                for t in ts:
                    until(t)
                    mark(t, dve.tensor_scalar(c1f[:, t % 2, :], c1f[:, t % 2, :], 0.0, QMAX, ALU.max, ALU.min))
                for t in ts:
                    until(t)
                    dve.tensor_scalar(c1[:, t, :], c1f[:, t % 2, :], ROUND, ROUND + MID, ALU.add, ALU.subtract)\
                        .then_inc(c1_ready, 1)

            def column_term(b):
                dve.wait_ge(r2_psum, b + 1)
                dve.tensor_scalar(bbn[:, b, :], bank[7 - b][:], scal[:, 9:10], None, ALU.mult).then_inc(bbn_ready, 1)

            for pair in PAIRS_OF_TILES:
                for t in pair:
                    dve.wait_ge(gemm_done, t + 1)
                    mark(t, dve.tensor_tensor(yrow(t), bank[2 + t][:], xr[:, t, :], ALU.add))
                moments_of(pair, 0, yrow)
                normalise(pair, 0, yrow)
                if pair[0]:
                    column_term(1)
                else:
                    column_term(0)
                quantise(pair)

            def row_term(t):
                dve.wait_ge(xat_done, t + 1)
                dve.tensor_scalar(stat[:, t, 11:12], bank[7 - t % 2][:, 0:1], scal[:, 10:11], scal[:, 11:12],
                                  ALU.mult, ALU.add).then_inc(rowb_ready, 1)

            row_term(0)
            row_term(1)
            for pair in PAIRS_OF_TILES:
                for t in pair:
                    dve.wait_ge(u_ready, t + 1)
                    dve.wait_ge(xb_ready, t + 1)
                    dve.tensor_tensor(yrow(t), yrow(t), xb[t], ALU.add).then_inc(xb_used, 1)
                for t in pair:
                    dve.wait_ge(xb_used, t + 1)
                    mark(t, dve.bn_stats(stat[:, t, 0:6], yrow(t)))
                for t in pair:
                    until(t)
                    mark(t, dve.bn_aggr(stat[:, t, 6:8], stat[:, t, 0:6]))
                for t in pair:
                    until(t)
                    dve.tensor_scalar(stat[:, t, 8:9], stat[:, t, 7:8], LN_EPS, None, ALU.add).then_inc(moments, 1)
                if pair[0] == 0:
                    row_term(2)
                    row_term(3)
                else:
                    xt_low_parts(T)
                    xt_low_parts(T + 1)
                normalise(pair, 1, yrow)

            dve.wait_ge(d_asg, 16)
            dve.wait_ge(d_fb, 16)
            dve.tensor_scalar(onehot[:], asgi[:], cst[0:NCL, K_IDX:K_IDX + 1], None, ALU.is_equal)\
                .then_inc(onehot_ready, 1)

            def cluster_hits(t):
                dve.wait_ge(lg_exp, t + 1)
                link(dve.reciprocal(f2[:, t, 2:3], f2[:, t, 1:2]))
                link(dve.tensor_scalar(hits[:, t, :], prob[:, t, :], f2[:, t, 2:3], HIT, ALU.mult, ALU.is_gt))
                dve.tensor_reduce(f2[:, t, 3:4], hits[:, t, :], AX_X, ALU.max).then_inc(hits_ready, 1)

            for t in range(T):
                if t >= 2:
                    xt_low_parts(T + t)
                if t >= 1:
                    dve.wait_ge(lg_psum, t)
                    link(dve.tensor_reduce(f2[:, t - 1, 0:1], bank[6 + (t - 1) % 2][:, 0:NCL], AX_X, ALU.max, negate=True))
                    dve.tensor_scalar(f2[:, t - 1, 0:1], f2[:, t - 1, 0:1], INV_TEMP, None, ALU.mult).then_inc(lg_max, 1)
                    dve.wait_ge(gemm_done, T + t)
                    dve.tensor_tensor(d1[:, t - 1, :], bank[2 + t - 1][:], fb[:], ALU.add).then_inc(vchain, 1)
                    chain[0] += 1
                    cluster_hits(t - 1)
            dve.wait_ge(lg_psum, T)
            link(dve.tensor_reduce(f2[:, T - 1, 0:1], bank[6 + (T - 1) % 2][:, 0:NCL], AX_X, ALU.max, negate=True))
            dve.tensor_scalar(f2[:, T - 1, 0:1], f2[:, T - 1, 0:1], INV_TEMP, None, ALU.mult).then_inc(lg_max, 1)
            dve.wait_ge(gemm_done, 2 * T)
            dve.tensor_tensor(d1[:, T - 1, :], bank[2 + T - 1][:], fb[:], ALU.add).then_inc(vchain, 1)
            chain[0] += 1
            cluster_hits(T - 1)
            dve.wait_ge(cl_psum, 1)
            dve.tensor_scalar(csel[:], bank[7][0:NCL, 0:P], 0.0, None, ALU.is_gt).then_inc(csel_ready, 1)
            dve.wait_ge(rsel_ready, 1)
            for pair in PAIRS_OF_TILES:
                for t in pair:
                    row_free(t, 2)
                    mark(t, dve.scalar_tensor_tensor(yrow(t), d1[:, t, :], f2[:, t, 3:4], rsel[:], ALU.mult, ALU.mult))
                for t in pair:
                    until(t)
                    mark(t, dve.tensor_tensor(yrow(t), yrow(t), xr[:, t, :], ALU.add))
                if pair[0]:
                    xt_low_parts(2 * T)
                    xt_low_parts(2 * T + 1)
                moments_of(pair, 2, yrow)
                normalise(pair, 2, yrow)
            dve.wait_ge(d_ba, 16)
            link(dve.tensor_scalar(bab[:, 0:D], bab[:, 0:D], 1.0 / D1, None, ALU.mult))
            dve.wait_ge(d_nw, 16)
            link(dve.tensor_tensor(wqk, nwt[:, 0:1], nwt[:, 1:2], ALU.mult))
            dve.tensor_scalar(wqk, wqk, HD ** -0.5, None, ALU.mult).then_inc(nw_ready, 1)
            for t in range(T):
                at_bank = 2 + 3 * (t % 2)
                dve.wait_ge(qkv_done, 3 * t + 1)
                if t:
                    dve.wait_ge(v_rest, t)
                dve.tensor_tensor(yb[:, 0, :], bank[at_bank + 2][:], bab[:, 2 * D:3 * D], ALU.add)\
                    .then_inc(qkv_out, 1)
                by_pair = "p (a k) -> p a k"
                dve.wait_ge(qkv_done, 3 * t + 2)
                dve.scalar_tensor_tensor(qr[:, :, t, :], bank[at_bank][:].rearrange(by_pair, a=PAIRS), 1.0 / D1,
                                         bab[:, 0:D].rearrange(by_pair, a=PAIRS), ALU.mult, ALU.add)\
                    .then_inc(qkv_out, 1)
                part = v3[:, t * H1 * 3 * D1:(t + 1) * H1 * 3 * D1].rearrange("p (h k d) -> p h k d", k=3, d=D1)
                dve.wait_ge(v_high, t + 1)
                if t:
                    dve.wait_ge(v_low, t)
                dve.tensor_tensor(yb[:, 1, :].rearrange("p (h d) -> p h d", d=D1),
                                  yb[:, 0, :].rearrange("p (h d) -> p h d", d=D1), part[:, :, 0, :], ALU.subtract)\
                    .then_inc(v_rest, 1)
                dve.wait_ge(qkv_done, 3 * t + 3)
                dve.tensor_tensor(kr[:, :, t, :], bank[at_bank + 1][:].rearrange(by_pair, a=PAIRS),
                                  bab[:, D:2 * D].rearrange(by_pair, a=PAIRS), ALU.add).then_inc(qkv_out, 1)
                if t + 2 < T:
                    xt_low_parts(2 * T + t + 2)

            dve.wait_ge(v_low, T)
            dve.wait_ge(consts, 4)
            def two_parts(i, u):
                dve.wait_ge(ex_done, i * 16 + 2 * u + 2)
                if not (isinstance(i, int) and i * 8 + u < 2):
                    dve.wait_ge(pt_psum, i * 8 + (u - 1))
                r = rowp[:, u % 2, :]
                dve.tensor_scalar(phl[:, u % 2, 0, :], r, PSCALE, None, ALU.mult).then_inc(ph_high, 1)
                dve.wait_ge(ph_high, i * 8 + u + 1)
                dve.scalar_tensor_tensor(phl[:, u % 2, 1, :], r, PSCALE, phl[:, u % 2, 0, :], ALU.mult,
                                         ALU.subtract).then_inc(phl_ready, 1)

            def transposed_out(i, u):
                dve.wait_ge(pt_psum, i * 8 + u + 1)
                dve.tensor_copy(ptb[:, 0, :], bank16f[3][:, 0:2 * KQ]).then_inc(pt_even, 1)

            def rows_sum(i, e):
                dve.wait_ge(pv_done, i * 8 + 4 * e + 4)
                dve.tensor_reduce(orow[:].rearrange("p (a d) -> p a d", d=D1),
                                  bank[5][:, 0:2 * T * 3 * D1].rearrange("p (a k d) -> p a d k", k=3, d=D1),
                                  AX_X, ALU.add).then_inc(pv_out, 1)

            def rows_out(i, e):
                z = zsum[:, 8 * e:8 * e + 8]
                dve.tensor_scalar(zinv, z, PSCALE, None, ALU.mult).then_inc(o_sum, 1)
                dve.wait_ge(o_sum, i * 4 + 2 * e + 1)
                dve.reciprocal(zinv, zinv).then_inc(o_sum, 1)
                dve.wait_ge(pv_out, i * 2 + e + 1)
                dve.wait_ge(o_sum, i * 4 + 2 * e + 2)
                dve.tensor_tensor(ao[:, :, bass.ds(i * 4 * D1 + 2 * e * D1, 2 * D1)].rearrange("p t (h d) -> p t h d", d=D1),
                                  orow[:].rearrange("p (t h d) -> p t h d", h=2, d=D1),
                                  zinv.rearrange("p (t h) -> p t h", h=2).unsqueeze(3).broadcast_to([P, T, 2, D1]),
                                  ALU.mult).then_inc(o_out, 1)

            def dve_body(i, first=False):
                def maxima(u):
                    dve.wait_ge(sc_done, i * 8 + u + 1)
                    if u % 2 == 0:
                        dve.wait_ge(bias_ready, i * 4 + u // 2 + 1)
                    dve.sem_inc(dve_passed, 1)
                    for q in range(2):
                        cols = slice(0, P) if q == 0 else slice(P, KQ)
                        dve.tensor_tensor_reduce(rowp[:, u % 2, cols], bank[1 + u % 2][:, cols],
                                                 bias[:, u // 2 % 2, cols], -1.0, 3e38, ALU.add, ALU.min,
                                                 nrm[:, 2 * (u % 2) + q:2 * (u % 2) + q + 1]).then_inc(mx_done, 1)

                def key_sum(h):
                    dve.wait_ge(k_square, i * 2 + h + 1)
                    s = kss[:, 4 * h:4 * h + 4]
                    dve.tensor_reduce(s, yb[:, 1, :].rearrange("p (g d) -> p g d", d=HD), AX_X, ALU.add)\
                        .then_inc(k_add, 1)
                    dve.wait_ge(k_add, i * 2 + h + 1)
                    dve.tensor_scalar(s, s, 1.0 / HD, LN_EPS, ALU.mult, ALU.add).then_inc(k_sum, 1)

                def key_rows(h):
                    dve.wait_ge(k_power, i * 2 + h + 1)
                    if h or not first:
                        dve.wait_ge(b0_full, i * 6 + (5 if h else 2))
                    dve.tensor_tensor(yb[:, 0, :].rearrange("p (g d) -> p g d", d=HD),
                                      bank[6 + h][:].rearrange("p (g d) -> p g d", d=HD),
                                      kpw[:, 4 * h:4 * h + 4].unsqueeze(2).broadcast_to([P, 4, HD]), ALU.mult)\
                        .then_inc(k_row, 1)

                for u in range(8):
                    if u == 6:
                        rows_sum(i, 0)
                    if u == 2 and not first:
                        rows_sum(i - 1, 1)
                    if u:
                        two_parts(i, u - 1)
                    elif not first:
                        two_parts(i - 1, 7)
                    if u % 2 == 0 and u:
                        transposed_out(i, u - 2)
                    elif u == 0 and not first:
                        transposed_out(i - 1, 6)
                    maxima(u)
                    if u in (2, 4):
                        key_sum(u // 2 - 1)
                    if u == 6:
                        rows_out(i, 0)
                    if u == 2 and not first:
                        rows_out(i - 1, 1)
                    if u in (3, 5):
                        key_rows(u // 2 - 1)

            dve_body(0, first=True)
            with dve.Fori(0, CT // 2 - 1) as j:
                dve_body(j * 2 + 1)
                dve_body(j * 2 + 2)
            dve_body(CT - 1)
            two_parts(CT - 1, 7)
            transposed_out(CT - 1, 6)
            rows_sum(CT - 1, 1)
            rows_out(CT - 1, 1)

            dve.wait_ge(d_bp, 16)
            for t in range(T):
                dve.wait_ge(xt_high, 3 * T + t + 1)
                dve.tensor_tensor(atl[:, :, t * P:(t + 1) * P], bank[t % 2][:].rearrange("p (c q) -> p c q", c=C),
                                  ath[:, :, t * P:(t + 1) * P].bitcast(F32), ALU.subtract).then_inc(xt_ready, 1)
            for pair in PAIRS_OF_TILES:
                for t in pair:
                    dve.wait_ge(gemm_done, 2 * T + t + 1)
                    row_free(t, 3)
                    mark(t, dve.tensor_tensor(yrow(t), bank[PROJ_BANK[t]][:], xr[:, t, :], ALU.add))
                if pair[0]:
                    xt_low_parts(4 * T)
                    xt_low_parts(4 * T + 1)
                for t in pair:
                    until(t)
                    mark(t, dve.tensor_tensor(yrow(t), yrow(t), bpb[:], ALU.add))
                moments_of(pair, 3, yrow)
                normalise(pair, 3, yrow)
            dve.wait_ge(d_mk, 16)

            def query_sum(n, slot):
                dve.wait_ge(q_square, n + 1)
                s = qss[:, 4 * slot:4 * slot + 4]
                dve.tensor_reduce(s, sqj[:].rearrange("p (j d) -> p j d", d=HD), AX_X, ALU.add).then_inc(q_add, 1)
                dve.wait_ge(q_add, n + 1)
                dve.tensor_scalar(s, s, 1.0 / HD, LN_EPS, ALU.mult, ALU.add).then_inc(q_sum, 1)

            def query_rows(n, slot):
                dve.wait_ge(q_power, n + 1)
                y = yb[:, slot, :].rearrange("p (j d) -> p j d", d=HD)
                dve.tensor_tensor(y, y, qpw[:, 4 * slot:4 * slot + 4].unsqueeze(2).broadcast_to([P, J, HD]), ALU.mult)\
                    .then_inc(q_norm, 1)

            def query_low(n, t):
                dve.wait_ge(q_high, n + 1)
                at_t = (slice(None), t // 2, slice(None), slice(t % 2 * P, (t % 2 + 1) * P))
                dve.tensor_tensor(qtl[at_t], bank[6][:].rearrange("p (j q) -> p j q", j=J), qth[at_t].bitcast(F32),
                                  ALU.subtract).then_inc(q_low, 1)

            def scores_max(g, u, at_bank=0):
                for q in range(2):
                    k = 2 * (u % 2) + q
                    dve.wait_ge(s_done, g * 16 + 2 * u + q + 1)
                    dve.sem_inc(dve_passed, 1)
                    dve.tensor_tensor_reduce(px[k][:], bank[at_bank + q][:], mk[:, q, :], -1.0, 3e38, ALU.add, ALU.min,
                                             xmx[:, k:k + 1]).then_inc(s_max, 1)

            def probs_norm(g, u):
                for q in range(2):
                    k = 2 * (u % 2) + q
                    dve.wait_ge(s_exp, g * 16 + 2 * u + q + 1)
                    dve.reciprocal(xzi[:, k:k + 1], xz[:, k:k + 1]).then_inc(z_inv, 1)
                    dve.wait_ge(z_inv, g * 16 + 2 * u + q + 1)
                    dve.tensor_scalar(px[k][:], px[k][:], xzi[:, k:k + 1], None, ALU.mult).then_inc(p_norm, 1)

            def probs_low(g, u):
                for q in range(2):
                    dve.wait_ge(p_high, g * 16 + 2 * u + q + 1)
                    cols = slice(q * P, (q + 1) * P)
                    dve.tensor_tensor(ptl[:, :, cols], bank[2 + q][:].rearrange("p (k q) -> p k q", q=P),
                                      pth[:, :, cols].bitcast(F32), ALU.subtract).then_inc(p_low, 1)

            def output_low(g, u):
                dve.wait_ge(a_high, g * 8 + u + 1)
                dve.tensor_tensor(otl[:, u // 4, u % 4, :], bank[4][:, 0:S], oth[:, u // 4, u % 4, :].bitcast(F32),
                                  ALU.subtract).then_inc(a_low, 1)

            def add_projection(n, t, at_bank=7):
                dve.wait_ge(o_done, n + 1)
                dve.tensor_tensor(xr[:, t, :], xr[:, t, :], bank[at_bank][:], ALU.add).then_inc(o_added, 1)

            query_sum(0, 0)
            xt_low_parts(4 * T + 2)
            query_rows(0, 0)
            query_sum(1, 1)
            xt_low_parts(4 * T + 3)
            query_low(0, 0)
            query_rows(1, 1)
            query_sum(2, 0)
            query_low(1, 1)
            query_rows(2, 0)
            scores_max(0, 0)
            query_sum(3, 1)
            probs_norm(0, 0)
            query_low(2, 2)
            query_rows(3, 1)
            query_low(3, 3)

            def dve_group(g, more):
                first = isinstance(g, int) and g == 0
                for u in range(8):
                    if not more and 0 < u < 7:
                        probs_norm(g, u + 1)
                    if u == 1 and not first:
                        add_projection(g * T - 2, 2)
                    if u == 2 and not first:
                        add_projection(g * T - 1, 3)
                    if u == 7:
                        add_projection(g * T, 0)
                    if u == 0 and not first:
                        add_projection(g * T - 3, 1)
                    if u:
                        output_low(g, u - 1)
                    elif not first:
                        output_low(g - 1, 7)
                    if not more and u == 0:
                        scores_max(g, 1, SPARE)
                    if more and u >= 4:
                        query_rows(g * T + T + u - 4, u % 2)
                    probs_low(g, u)
                    if more and u < 7:
                        scores_max(g, u + 1)
                    elif more:
                        scores_max(g + 1, 0)
                    if more and 3 <= u < 7:
                        query_sum(g * T + T + u - 3, (u - 3) % 2)
                    if more and u < 7 or u == 0:
                        probs_norm(g, u + 1)
                    elif more:
                        probs_norm(g + 1, 0)
                    if not more and u < 6:
                        scores_max(g, u + 2, SPARE * (u % 2))
                    if more and u >= 4:
                        query_low(g * T + T + u - 4, u - 4)

            dve_group(0, True)
            with dve.Fori(1, G - 1) as g:
                dve_group(g, True)
            dve_group(G - 1, False)
            output_low(G - 1, 7)
            for pair in PAIRS_OF_TILES:
                for t in pair:
                    if t == T - 1:
                        xt_low_parts(5 * T)
                        xt_low_parts(5 * T + 1)
                    if t:
                        add_projection(T * (G - 1) + t, t, SPARE if t == T - 1 else 7)
                for t in pair:
                    dve.wait_ge(o_added, T * (G - 1) + t + 1)
                    mark(t, dve.bn_stats(stat[:, t, 0:6], xr[:, t, :]))
                for t in pair:
                    until(t)
                    mark(t, dve.bn_aggr(stat[:, t, 6:8], stat[:, t, 0:6]))
                for t in pair:
                    until(t)
                    dve.tensor_scalar(stat[:, t, 8:9], stat[:, t, 7:8], LN_EPS, None, ALU.add).then_inc(moments, 1)
                normalise(pair, 4, lambda t: xr[:, t, :])
            dve.wait_ge(d_br, 16)

            def experts(n):
                pair = PAIRS_OF_TILES[n]
                z = [zt[:, k, pair[0]:pair[0] + 2, :] for k in range(8)]
                to = bank[6 + n][:, 0:2 * RA].rearrange("p (t m) -> p t m", m=RA)
                both = [P, 2, NE]
                counts = cst[:, K_CNT:K_CNT + NE].unsqueeze(1).broadcast_to(both)
                dve.wait_ge(ra_done, 2 * n + 2)
                link(dve.tensor_tensor(z[0], to[:, :, 0:NE], brb[:].unsqueeze(1).broadcast_to(both), ALU.add))
                for k in range(2):
                    dve.max(z[1][:, k, :], z[0][:, k, :]).then_inc(vchain, 1)
                chain[0] += 2
                dve.wait_ge(vchain, chain[0])
                for k in range(2):
                    dve.tensor_tensor_scan(z[2][:, k, :], oneb[:, 0:NE], z[1][:, k, :], 0.0, ALU.mult, ALU.add)\
                        .then_inc(vchain, 1)
                chain[0] += 2
                link(dve.tensor_tensor(z[3], z[1], counts, ALU.mult))
                link(dve.tensor_scalar(z[3], z[3], 1.0, None, ALU.add))
                link(dve.tensor_tensor(z[3], z[3], z[2], ALU.is_gt))
                link(dve.tensor_reduce(z[4][:, :, 0:1], z[3], AX_X, ALU.add))
                link(dve.tensor_tensor(z[5], counts, z[4][:, :, 0:1].broadcast_to(both), ALU.is_equal))
                link(dve.tensor_tensor(z[5], z[5], z[2], ALU.mult))
                dve.reciprocal(z[4][:, :, 2:3], z[4][:, :, 0:1]).then_inc(vchain, 1)
                chain[0] += 1
                link(dve.tensor_reduce(z[4][:, :, 1:2], z[5], AX_X, ALU.add))
                link(dve.tensor_scalar(z[4][:, :, 1:2], z[4][:, :, 1:2], -1.0, None, ALU.add))
                link(dve.tensor_tensor(z[4][:, :, 3:4], z[4][:, :, 1:2], z[4][:, :, 2:3], ALU.mult))
                link(dve.tensor_tensor(z[6], z[0], z[4][:, :, 3:4].broadcast_to(both), ALU.subtract))
                link(dve.tensor_scalar(z[6], z[6], 0.0, None, ALU.max))
                for k, t in enumerate(pair):
                    dve.tensor_tensor(hw[:, t, :].rearrange("p (e r) -> p e r", r=R),
                                      to[:, k, NE:RA].rearrange("p (e r) -> p e r", r=R),
                                      z[6][:, k, :].unsqueeze(2).broadcast_to([P, NE, R]), ALU.mult).then_inc(hw_ready, 1)

            def experts_low(n):
                dve.wait_ge(hw_high, n + 1)
                dve.tensor_tensor(htl[:, 2 * n:2 * n + 2, :], bank[n][:, 0:2 * P].rearrange("p (t q) -> p t q", q=P),
                                  hth[:, 2 * n:2 * n + 2, :].bitcast(F32), ALU.subtract).then_inc(hw_split, 1)

            def last_norm(pair):
                for t in pair:
                    dve.wait_ge(ff_done, t + 1)
                    dve.wait_ge(xs_ready, t + 1)
                    row_free(t, 5)
                    mark(t, dve.tensor_tensor(yrow(t), bank[2 + t][:], xs[:, t, :], ALU.add))
                moments_of(pair, 5, yrow)
                normalise(pair, 5, yrow)

            experts(0)
            xt_low_parts(5 * T + 2)
            xt_low_parts(5 * T + 3)
            experts_low(0)
            experts(1)
            last_norm(PAIRS_OF_TILES[0])
            experts_low(1)
            last_norm(PAIRS_OF_TILES[1])

        @block.tensor
        def _(pe):
            pe.wait_ge(d_cst, 16)
            pe.wait_ge(mask_summed, 1)
            pe.matmul(bank[6][:, 0:C * D // BLK], cst[:, K_BLK:K_BLK + P], msum[:], start=True, stop=True)\
                .then_inc(mask_counts, 1)
            pe.wait_ge(consts, 4)

            def product(into, lh, ll, rh, rl, first, last):
                pe.matmul(into, lh, rl, start=first, stop=False)
                pe.matmul(into, ll, rh, start=False, stop=False)
                return pe.matmul(into, lh, rh, start=False, stop=last)

            def transpose_rows(n, src):
                t = n % T
                if n >= 2:
                    pe.wait_ge(xt_ready, n - 1)
                for c in range(C):
                    ins = pe.transpose(bank[t % 2][:, c * P:(c + 1) * P], src[:, c * P:(c + 1) * P], ident)
                ins.then_inc(xt_psum, 1)

            def w0_chunk(c):
                if c < 2:
                    pe.wait_ge(w0_split, c + 1)
                else:
                    pe.wait_ge(w0_split2, c - 1)

            def tile_gemm(into, t, wh, wl, wait_chunk=None):
                for c in range(C):
                    if wait_chunk:
                        wait_chunk(c)
                    s = slice(t * P, (t + 1) * P)
                    ins = product(into, xth[:, c, s], xtl[:, c, s], wh[:, c], wl[:, c], c == 0, c == C - 1)
                return ins

            pe.wait_ge(d_x[0], 16)
            transpose_rows(0, xr[:, 0])
            transpose_rows(1, xr[:, 1])
            for t in range(T):
                pe.wait_ge(xt_ready, t + 1)
                tile_gemm(bank[2 + t][:], t, w0h, w0l, w0_chunk if t == 0 else None).then_inc(gemm_done, 1)
                if t + 2 < T:
                    pe.wait_ge(d_x[1], 16)
                    transpose_rows(t + 2, xr[:, t + 2])

            for b in range(B):
                pe.wait_ge(c2_ready, b + 1)
                for c in range(C):
                    ins = pe.matmul(bank[7 - b][:], oneb[:], c2[:, b * C + c, :], start=c == 0, stop=c == C - 1)
                ins.then_inc(r2_psum, 1)

            def transpose_c1(t):
                pe.wait_ge(c1_ready, t + 1)
                if t >= 2:
                    pe.wait_ge(c1t_ready, t - 1)
                else:
                    pe.wait_ge(xt_ready, T)
                for c in range(C):
                    ins = pe.transpose(bank16[t % 2][:, c * P:(c + 1) * P], c1[:, t, c * P:(c + 1) * P], idb[:])
                ins.then_inc(c1_psum, 1)

            transpose_c1(0)
            transpose_c1(1)
            for t in range(T):
                pe.wait_ge(c1t_ready, t + 1)
                for c in range(C):
                    pe.matmul(bank[2 + t][:], c1t[:, t % 2, c * P:(c + 1) * P], c2[:, t // 2 * C + c, :],
                              start=c == 0, stop=c == C - 1)
                if t < 2:
                    pe.wait_ge(bbn_ready, t + 1)
                else:
                    pe.wait_ge(rowb_ready, t - 1)
                for c in range(C):
                    ins = pe.matmul(bank[7 - t % 2][:, 0:2], c1t[:, t % 2, c * P:(c + 1) * P], oneb[:, 0:2],
                                    start=c == 0, stop=c == C - 1)
                ins.then_inc(xat_done, 1)
                if t + 2 < T:
                    transpose_c1(t + 2)

            def transpose_ln(layer, t, ln):
                pe.wait_ge(ln_done, ln * T + t + 1)
                transpose_rows(layer * T + t, xr[:, t])

            pe.wait_ge(c1t_ready, T)
            transpose_ln(1, 0, 1)
            transpose_ln(1, 1, 1)
            for t in range(T):
                pe.wait_ge(wt_split, C + 1)
                pe.wait_ge(xt_ready, T + t + 1)
                if t >= 2:
                    pe.wait_ge(lg_exp, t - 1)
                tile_gemm(bank[6 + t % 2][:, 0:NCL], t, cenh, cenl).then_inc(lg_psum, 1)
                tile_gemm(bank[2 + t][:], t, wfh, wfl).then_inc(gemm_done, 1)
                if t + 2 < T:
                    transpose_ln(1, t + 2, 1)
            pe.wait_ge(hits_ready, T)
            for t in range(T):
                ins = pe.matmul(bank[7][0:NCL, 0:P], hits[:, t, :], oneb[:], start=t == 0, stop=t == T - 1)
            ins.then_inc(cl_psum, 1)
            pe.wait_ge(csel_ready, 1)
            pe.wait_ge(onehot_ready, 1)
            pe.matmul(bank[6][:], csel[:], onehot[:], start=True, stop=True).then_inc(cl_psum, 1)
            transpose_ln(2, 0, 2)
            transpose_ln(2, 1, 2)
            for t in range(T):
                pe.wait_ge(xt_ready, 2 * T + t + 1)
                pe.wait_ge(wa_split, 3 * C)
                if t == 1:
                    pe.wait_ge(rsel_ready, 1)
                for k in range(3):
                    if t >= 2:
                        pe.wait_ge(qkv_out, 3 * (t - 2) + k + 1)
                    m = (2, 0, 1)[k]
                    cols = slice(m * D, (m + 1) * D)
                    tile_gemm(bank[2 + 3 * (t % 2) + m][:], t, wah[:, :, cols], wal[:, :, cols]).then_inc(qkv_done, 1)
                if t + 2 < T:
                    transpose_ln(2, t + 2, 2)

            pe.wait_ge(qkv_out, 3 * T)
            pe.wait_ge(xt_ready, 3 * T)
            pe.wait_ge(wk_split, C)
            pe.wait_ge(wv_split, C)
            pe.wait_ge(v_low, T)
            def transpose_stack(m, n, k):
                pe.wait_ge(stacked, m * 2 + k + 1)
                if not (isinstance(n, int) and n == 0):
                    pe.wait_ge(b0_free, n)
                src = (sq, sk)[k][:].bitcast(F32).rearrange("p t h k d -> p t (h k d)")
                for t in range(T):
                    ins = pe.transpose(bank[0][:, t * P:(t + 1) * P], src[:, t, :], ident)
                ins.then_inc(b0_full, 1)

            def transpose_probs(i, u):
                pe.wait_ge(phl_ready, i * 8 + u + 1)
                if not (isinstance(i, int) and i * 8 + u < 2):
                    pe.wait_ge(pt_odd if u % 2 else pt_even, i * 4 + u // 2)
                for part in range(2):
                    for k in range(3):
                        ins = pe.transpose(bank16f[3 + u % 2][:, (3 * part + k) * P:(3 * part + k + 1) * P],
                                           phl[:, u % 2, part, k * P:(k + 1) * P], idh[:])
                ins.then_inc(pt_psum, 1)

            def probs_values(i, u):
                e, hd, b = u // 4, u // 2 % 2, u % 2
                pe.wait_ge(pt_odd if u % 2 else pt_even, i * 4 + (u // 2 + 1))
                if u % 4 == 0 and not (isinstance(i, int) and i * 8 + u == 0):
                    pe.wait_ge(pv_out, i * 2 + e)
                for q in range(2):
                    a = (2 * b + q) * 2 + hd
                    blocks = [(0, 0)] if q == 0 else [(1, 0), (2, 1)]
                    steps = [(part, k, kt_) for k, kt_ in blocks for part in range(2)]
                    for n, (part, k, kt_) in enumerate(steps):
                        at_v = (2 * b + kt_) * H1 * 3 * D1 + (2 * e + hd) * 3 * D1
                        ins = pe.matmul(bank[5][:, a * 3 * D1:(a + 1) * 3 * D1],
                                        ptb[:, u % 2, (3 * part + k) * P:(3 * part + k + 1) * P],
                                        v3[:, bass.ds(i * (4 * 3 * D1) + at_v, 3 * D1)],
                                        start=n == 0, stop=n == len(steps) - 1)
                ins.then_inc(pv_done, 1)

            def pe_body(i, odd, first=False, last=False):
                def scores(u):
                    e, hd, b = u // 4, u // 2 % 2, u % 2
                    d = slice(4 * D1 * hd, 4 * D1 * (hd + 1))
                    to = bank[1 + u % 2]
                    if u % 4 == 0:
                        pe.wait_ge(b0_free, i * 6 + 4 if e else 2 if first else i * 6 + 1)
                    if not (first and u < 2):
                        pe.wait_ge(mx_done, i * 16 + (2 * u - 2))
                    pe.matmul(to[:, 0:P], qt[e][d, b * S:b * S + P], kt[e][d, b * S:b * S + P], start=True, stop=True)
                    pe.matmul(to[:, P:KQ], qt[e][d, b * S + P:b * S + S], kt[e][d, b * S:b * S + S],
                              start=True, stop=True).then_inc(sc_done, 1)

                def context_half(n, cs):
                    h = n % 2
                    wh, wl = ((wkh, wkl), (wvh, wvl))[n // 2]
                    if cs[0] == 0:
                        if n == 0:
                            pe.wait_ge(ctx_split, i + 1)
                        if n >= 2:
                            pe.wait_ge(k_row, i * 2 + h + 1)
                        elif not first:
                            pe.wait_ge(v_out, i * 2 - 1 + h)
                    for c in cs:
                        cols = slice(h * D, (h + 1) * D)
                        ins = product(bank[6 + h][:], cth[odd][:, c, :], ctl[odd][:, c, :], wh[:, c, cols],
                                      wl[:, c, cols], c == 0, c == C - 1)
                    if cs[-1] == C - 1:
                        ins.then_inc(kv_done, 1)

                def transpose_keys(h):
                    pe.wait_ge(k_row, i * 2 + h + 1)
                    pe.wait_ge(b0_free, i * 6 + (4 if h == 0 else 5 if last else 7))
                    for g in range(4):
                        ins = pe.transpose(bank[0][:, g * P:(g + 1) * P], yb[:, 0, g * P:(g + 1) * P], ident)
                    ins.then_inc(b0_full, 1)

                for u in range(8):
                    if u >= 2:
                        transpose_probs(i, u - 2)
                    elif not first:
                        transpose_probs(i - 1, u + 6)
                    scores(u)
                    context_half(u // 2, (2, 3) if u % 2 else (0, 1))
                    if u >= 2:
                        probs_values(i, u - 2)
                    elif not first:
                        probs_values(i - 1, u + 6)
                    if u < 2:
                        transpose_stack(i * 2 + 1, i * 6 + 2 + u, u)
                    if u == 4:
                        transpose_keys(0)
                    if u in (5, 6) and not last:
                        transpose_stack(i * 2 + 2, i * 6 + u, u - 5)
                    if u == 7:
                        transpose_keys(1)

            transpose_stack(0, 0, 0)
            transpose_stack(0, 1, 1)
            pe_body(0, 0, first=True)
            with pe.Fori(0, CT // 2 - 1) as j:
                pe_body(j * 2 + 1, 1)
                pe_body(j * 2 + 2, 0)
            pe_body(CT - 1, 1, last=True)
            for u in (6, 7):
                transpose_probs(CT - 1, u)
            for u in (6, 7):
                probs_values(CT - 1, u)

            def transpose_ao(t):
                if t == 0:
                    pe.wait_ge(o_out, PAIRS)
                    pe.wait_ge(b0_free, 6 * CT)
                if t >= 2:
                    pe.wait_ge(xt_ready, 3 * T + t - 1)
                for c in range(C):
                    ins = pe.transpose(bank[t % 2][:, c * P:(c + 1) * P], ao[:, t, c * P:(c + 1) * P], ident)
                ins.then_inc(xt_psum, 1)

            transpose_ao(0)
            transpose_ao(1)
            pe.wait_ge(wp_split, C)
            pe.wait_ge(v_out, 2 * CT)
            for t in range(T):
                pe.wait_ge(xt_ready, 3 * T + t + 1)
                for c in range(C):
                    s = slice(t * P, (t + 1) * P)
                    ins = product(bank[PROJ_BANK[t]][:], ath[:, c, s], atl[:, c, s], wph[:, c], wpl[:, c],
                                  c == 0, c == C - 1)
                ins.then_inc(gemm_done, 1)
                if t + 2 < T:
                    transpose_ao(t + 2)
            def query_chunk(n, t, cs, g):
                if cs[0] == 0:
                    pe.wait_ge(wq_split, g * C + C)
                    if not (isinstance(n, int) and n == 0):
                        pe.wait_ge(q_raw, n)
                s = slice(t * P, (t + 1) * P)
                for c in cs:
                    ins = product(bank[5][:], xth[:, c, s], xtl[:, c, s], wqh[:, c], wql[:, c], c == 0, c == C - 1)
                if cs[-1] == C - 1:
                    ins.then_inc(q_done, 1)

            def transpose_queries(n, slot):
                pe.wait_ge(q_norm, n + 1)
                if not (isinstance(n, int) and n == 0):
                    pe.wait_ge(q_low, n)
                for j in range(J):
                    ins = pe.transpose(bank[6][:, j * P:(j + 1) * P], yb[:, slot, j * P:(j + 1) * P], ident)
                ins.then_inc(q_psum, 1)

            def unit_scores(g, u, ahead=False):
                b, j = u // 4, u % 4
                first = isinstance(g, int) and g == 0 and u == 0
                pe.wait_ge(kx_split, g * 2 + b + 1)
                pe.wait_ge(q_low, g * T + (T if ahead and u == 1 else 2 * b + 2))
                for q in range(2):
                    if ahead and u > 1:
                        pe.wait_ge(s_max, g * 16 + 2 * u + q - 3)
                    elif ahead:
                        pe.wait_ge(q_raw, G * T)
                    elif not first:
                        pe.wait_ge(s_max, g * 16 + 2 * u + q - 1)
                    cols = slice(q * P, (q + 1) * P)
                    to = bank[(SPARE if ahead and u % 2 else 0) + q]
                    product(to[:], qth[:, b, j, cols], qtl[:, b, j, cols], kh[:, b, :], kl[:, b, :], True, True)\
                        .then_inc(s_done, 1)

            def transpose_unit(g, u):
                first = isinstance(g, int) and g == 0 and u == 0
                for q in range(2):
                    k = 2 * (u % 2) + q
                    pe.wait_ge(p_norm, g * 16 + 2 * u + q + 1)
                    if not first:
                        pe.wait_ge(p_low, g * 16 + 2 * u + q - 1)
                    for n in range(S2 // P):
                        ins = pe.transpose(bank[2 + q][:, n * P:(n + 1) * P], px[k][:, n * P:(n + 1) * P], ident)
                    ins.then_inc(p_psum, 1)

            def unit_output(g, u):
                b = u // 4
                pe.wait_ge(vx_split, g * 2 + b + 1)
                pe.wait_ge(p_low, g * 16 + 2 * u + 2)
                if not (isinstance(g, int) and g == 0 and u == 0):
                    pe.wait_ge(a_low, g * 8 + u)
                for n in range(S2 // P):
                    ins = product(bank[4][:, 0:S], vh[:, b, n, :], vl[:, b, n, :], pth[:, n, :], ptl[:, n, :],
                                  n == 0, n == S2 // P - 1)
                ins.then_inc(a_done, 1)

            def project(n, t, g, to=7):
                pe.wait_ge(wo_split, g * J + J)
                pe.wait_ge(a_low, g * 8 + 4 * (t // 2) + 4)
                if to != 7:
                    pe.wait_ge(s_max, 16 * G)
                elif not (isinstance(n, int) and n == 0):
                    pe.wait_ge(o_added, n)
                cols = slice(t % 2 * P, (t % 2 + 1) * P)
                for j in range(J):
                    ins = product(bank[to][:], oth[:, t // 2, j, cols], otl[:, t // 2, j, cols], woh[:, j], wol[:, j],
                                  j == 0, j == J - 1)
                ins.then_inc(o_done, 1)

            transpose_ln(4, 0, 3)
            transpose_ln(4, 1, 3)
            for t in range(T):
                pe.wait_ge(xt_ready, 4 * T + t + 1)
                query_chunk(t, t, range(C), 0)
                if t < 2:
                    transpose_ln(4, t + 2, 3)
                if t in (1, 2):
                    transpose_queries(t - 1, t - 1)
            unit_scores(0, 0)
            transpose_queries(2, 0)
            transpose_queries(3, 1)

            def pe_group(g, more):
                first = isinstance(g, int) and g == 0
                for u in range(8):
                    if not more and u == 0:
                        unit_scores(g, 1, ahead=True)
                    transpose_unit(g, u)
                    if not more and u < 6:
                        unit_scores(g, u + 2, ahead=True)
                    elif more and u < 7:
                        unit_scores(g, u + 1)
                    elif more:
                        unit_scores(g + 1, 0)
                    if more and 2 <= u < 6:
                        query_chunk(g * T + T + u - 2, u - 2, range(C), g + 1)
                    if u < 2 and not first:
                        project(g * T - 2 + u, 2 + u, g - 1)
                    if u >= 6:
                        project(g * T + u - 6, u - 6, g)
                    if more and u >= 4:
                        transpose_queries(g * T + T + u - 4, u % 2)
                    unit_output(g, u)

            pe_group(0, True)
            with pe.Fori(1, G - 1) as g:
                pe_group(g, True)
            pe_group(G - 1, False)
            project(T * (G - 1) + 2, 2, G - 1)
            pe.wait_ge(s_max, 16 * G)
            pe.wait_ge(p_low, 16 * G)
            pe.wait_ge(a_low, 8 * G)
            transpose_ln(5, 0, 4)
            transpose_ln(5, 1, 4)
            project(T * (G - 1) + 3, 3, G - 1, SPARE)

            def experts_in(t):
                pe.wait_ge(f_split, C + 1)
                pe.wait_ge(xt_ready, 5 * T + t + 1)
                tile_gemm(bank[6 + t // 2][:, t % 2 * RA:(t % 2 + 1) * RA], t, rah, ral).then_inc(ra_done, 1)

            def base_product(t):
                for c in range(C):
                    s = slice(t * P, (t + 1) * P)
                    product(bank[2 + t][:], xth[:, c, s], xtl[:, c, s], wbh[:, c], wbl[:, c], c == 0, False)

            def transpose_weighted(n):
                pe.wait_ge(hw_ready, 2 * n + 2)
                pe.wait_ge(xt_ready, 6 * T)
                for k in range(2):
                    ins = pe.transpose(bank[n][:, k * P:(k + 1) * P], hw[:, 2 * n + k, :], ident)
                ins.then_inc(hw_psum, 1)

            def experts_out(n):
                pe.wait_ge(hw_split, n + 1)
                pe.wait_ge(f_split, C + 2)
                for t in PAIRS_OF_TILES[n]:
                    product(bank[2 + t][:], hth[:, t, :], htl[:, t, :], lbh[:], lbl[:], False, True).then_inc(ff_done, 1)

            experts_in(0)
            experts_in(1)
            transpose_ln(5, 2, 4)
            transpose_ln(5, 3, 4)
            base_product(0)
            pe.wait_ge(o_added, T * G)
            experts_in(2)
            experts_in(3)
            transpose_weighted(0)
            base_product(1)
            experts_out(0)
            base_product(2)
            transpose_weighted(1)
            base_product(3)
            experts_out(1)


def _constants():
    import numpy as np
    c = np.zeros((P, K_ALL), np.float32)
    c[:, K_ID:K_ID + P] = np.eye(P)
    c[:, K_BLK:K_BLK + P] = np.kron(np.eye(P // BLK), np.ones((BLK, BLK)))
    q, k = np.arange(P)[:, None], np.arange(S)[None, :]
    for at, rows, keys in ((0, q, k[:, :P]), (P, q + P, k)):
        rel = (keys - rows).astype(np.float32)
        c[:, K_REL + at:K_REL + at + keys.shape[1]] = np.where(rel <= 0, rel, np.float32(-1e34))
    base = 2.0 ** (-2.0 ** (-(math.log2(H1) - 3)))
    c[:, K_SLOPE:K_SLOPE + H1] = (base ** np.arange(1, H1 + 1, dtype=np.float32)).astype(np.float32)
    c[:, K_IDX] = np.arange(P)
    c[:, K_CNT:K_CNT + NE] = np.arange(1, NE + 1)
    return c


def _layout(a):
    import numpy as np
    n = {k: np.asarray(v) for k, v in a.items()}
    rows = np.ascontiguousarray
    return {
        "x": n["x"].reshape(B * S, D),
        "ctx": n["ctx_4096"].reshape(B * S2, D),
        "ctxT": rows(n["ctx_4096"].reshape(B * S2, D).T),
        "amask": n["mask_1x1xSxS2_ff0"].reshape(S, S2),
        "w0T": rows(n["L0_attn_weight"].T),
        "m0T": rows(n["L0_attn_mask"].T),
        "qs": np.concatenate([n["L0_xattn_" + k] for k in ("x1_scale", "x1_zp", "x2_scale", "x2_zp")]),
        "wfT": rows(n["L0_ffn_weight"].T),
        "fbias": n["L0_ffn_bias"],
        "centT": rows(n["L0_ffn_centroids"].T),
        "asg": n["L0_ffn_assignments"],
        "waT": n["L1_attn_w_attn"],
        "ba": n["L1_attn_b_attn"],
        "wpT": n["L1_attn_w_proj"],
        "bp": n["L1_attn_b_proj"],
        "wqT": rows(n["L1_xattn_q_proj_w"].T),
        "wkT": rows(n["L1_xattn_k_proj_w"].T),
        "wvT": rows(n["L1_xattn_v_proj_w"].T),
        "woT": rows(n["L1_xattn_o_proj_w"].T),
        "nw": np.stack([n["L1_xattn_q_norm_w"], n["L1_xattn_k_norm_w"]], 1),
        "wbT": rows(n["L1_ffn_W_base"].T),
        "bb": n["L1_ffn_b_base"],
        "raT": rows(np.concatenate([n["L1_ffn_W_router"].T,
                                    n["L1_ffn_lora_A"].transpose(1, 0, 2).reshape(D, NE * R)], 1)),
        "br": n["L1_ffn_b_router"],
        "lb": n["L1_ffn_lora_B"].reshape(NE * R, D),
        "const": _constants(),
    }


def kernel(**inputs):
    import numpy as _np
    import concourse.bacc as _bacc
    from concourse import mybir as _mybir
    from concourse.bass_utils import run_bass_kernel_spmd as _run

    nc = _bacc.Bacc("TRN2", target_bir_lowering=False, num_devices=1)
    arrays, args = {}, []
    for name, a in _layout(inputs).items():
        a = _np.ascontiguousarray(a)
        arrays[f"in_{name}"] = a
        args.append(nc.dram_tensor(f"in_{name}", a.shape, _mybir.dt.from_np(a.dtype), kind="ExternalInput").ap())
    args.append(nc.dram_tensor("out", (B * S, D), F32, kind="ExternalOutput").ap())
    decoder_kernel(nc, *args)
    r = _run(nc, [arrays], core_ids=[0])
    return r.results[0]["out"].reshape(B, S, D)
```
